# Optimizing a Trainium2 kernel written in Bass

```python
import numpy as np
import jax
import jax.numpy as jnp

def _softmax(x, axis=-1):
    return jax.nn.softmax(x, axis=axis)

def _gelu(x):
    return jax.nn.gelu(x, approximate=True)

def _silu(x):
    return jax.nn.silu(x)

def _sigmoid(x):
    return jax.nn.sigmoid(x)

def _layernorm(x, axis=-1, eps=1e-05):
    m = jnp.mean(x, axis=axis, keepdims=True)
    v = jnp.var(x, axis=axis, keepdims=True)
    return (x - m) / jnp.sqrt(v + eps)

def _scatter_add(tgt, idx, src, axis=0):
    return tgt.at[idx].add(src)

def _segment_sum(src, seg, n):
    return jax.ops.segment_sum(src, seg, n)
kernel_name = 'mk_adj_resnorm_d4_adj_r2_f2ff0d'

def setup_inputs(seed: int=0):
    np.random.seed(seed)
    _w = jnp.asarray

    def _rec_inputs():
        import jax
        import jax.numpy as jnp
        _gk = jax.random.key(seed)
        x = -0.000125 + 0.9999 * jax.random.normal(jax.random.fold_in(_gk, 1), (8, 1024, 128), jnp.float32)
        _a = jax.random.bernoulli(jax.random.fold_in(_gk, 2), 0.0078125, (1024, 1024))
        _a = jnp.logical_or(_a, jnp.swapaxes(_a, -1, -2))
        _a = jnp.logical_or(_a, jnp.eye(1024, dtype=bool))
        _af = _a.astype(jnp.float32)
        _af = _af * jax.random.uniform(jax.random.fold_in(_gk, 3), (1024, 1024), jnp.float32, 0.05, 0.000488281)
        adj = _af
        return (x, adj)
    x, adj = _rec_inputs()

    def _L0_gnn_setup():
        import jax, jax.numpy as jnp
        import numpy as np
        B, T, D, H = (64, 1024, 128, 128)
        MAX_SKIP = 4

        def _lstm_last(Wih, Whh, bih, bhh, xs):
            N, _, Hd = xs.shape
            bias = bih + bhh

            def step(carry, x_t):
                h, c = carry
                g = x_t @ Wih.T + h @ Whh.T + bias
                i, f, gg, o = jnp.split(g, 4, axis=-1)
                c = jax.nn.sigmoid(f) * c + jax.nn.sigmoid(i) * jnp.tanh(gg)
                h = jax.nn.sigmoid(o) * jnp.tanh(c)
                return ((h, c), None)
            init = (jnp.zeros((N, Hd), xs.dtype), jnp.zeros((N, Hd), xs.dtype))
            (h_last, _), _ = jax.lax.scan(step, init, jnp.swapaxes(xs, 0, 1))
            return h_last
        key = jax.random.key(seed)
        ks = jax.random.split(key, 8)
        s = 0.05
        x = jax.random.normal(ks[0], (B, T, D), jnp.float32)
        adj = jax.random.uniform(ks[1], (T, T), jnp.float32) / T
        Wg0 = jax.random.normal(ks[2], (D, H), jnp.float32) * s
        bg0 = jnp.zeros((H,), jnp.float32)
        Wg1 = jax.random.normal(ks[3], (H, H), jnp.float32) * s
        bg1 = jnp.zeros((H,), jnp.float32)
        Wih = jax.random.normal(ks[4], (MAX_SKIP, 4 * H, H), jnp.float32) * s
        Whh = jax.random.normal(ks[5], (MAX_SKIP, 4 * H, H), jnp.float32) * s
        bih = jax.random.normal(ks[6], (MAX_SKIP, 4 * H), jnp.float32) * s
        bhh = jax.random.normal(ks[7], (MAX_SKIP, 4 * H), jnp.float32) * s
        return dict(x=x, adj=adj, Wg0=Wg0, bg0=bg0, Wg1=Wg1, bg1=bg1, Wih=Wih, Whh=Whh, bih=bih, bhh=bhh)
    _L0_gnn_all = _L0_gnn_setup()
    _L0_gnn_in = {k: v for k, v in _L0_gnn_all.items() if k in ('Wg0', 'bg0', 'Wg1', 'bg1', 'Wih', 'Whh', 'bih', 'bhh')}
    del _L0_gnn_all

    def _L1_gnn_setup():
        import jax, jax.numpy as jnp
        import numpy as np
        N = 3445
        B = 32
        IN_DIM = 128
        HID_DIM = 128

        def _make_adj(key):
            a = jax.random.uniform(key, (N, N), dtype=jnp.float32)
            a = (a < 0.001).astype(jnp.float32)
            a = jnp.maximum(a, a.T)
            deg = jnp.sum(a, axis=1, keepdims=True)
            return a / jnp.maximum(deg, 1.0)

        def _graph_conv(x, adj, w_loop, w_neigh, b):
            loop = jnp.einsum('bnd,dh->bnh', x, w_loop)
            neigh = jnp.einsum('nm,bmh->bnh', adj, jnp.einsum('bnd,dh->bnh', x, w_neigh))
            return loop + neigh + b
        key = jax.random.key(seed)
        k = jax.random.split(key, 8)
        s1 = 1.0 / np.sqrt(IN_DIM)
        s2 = 1.0 / np.sqrt(HID_DIM)
        return {'x': jax.random.normal(k[0], (B, N, IN_DIM), dtype=jnp.float32), 'adj': _make_adj(k[1]), 'w1_loop': jax.random.normal(k[2], (IN_DIM, HID_DIM), dtype=jnp.float32) * s1, 'w1_neigh': jax.random.normal(k[3], (IN_DIM, HID_DIM), dtype=jnp.float32) * s1, 'b1': jnp.zeros((HID_DIM,), dtype=jnp.float32), 'w2_loop': jax.random.normal(k[4], (HID_DIM, IN_DIM), dtype=jnp.float32) * s2, 'w2_neigh': jax.random.normal(k[5], (HID_DIM, IN_DIM), dtype=jnp.float32) * s2, 'b2': jnp.zeros((IN_DIM,), dtype=jnp.float32)}
    _L1_gnn_all = _L1_gnn_setup()
    _L1_gnn_in = {k: v for k, v in _L1_gnn_all.items() if k in ('w1_loop', 'w1_neigh', 'b1', 'w2_loop', 'w2_neigh', 'b2')}
    del _L1_gnn_all

    def _L2_gnn_setup():
        import jax, jax.numpy as jnp
        import numpy as np
        EPS = 1e-05

        def _batchnorm(x, gamma, beta):
            mu = jnp.mean(x, axis=0)
            var = jnp.var(x, axis=0)
            return (x - mu) * jax.lax.rsqrt(var + EPS) * gamma + beta
        key = jax.random.key(seed)
        ks = jax.random.split(key, 4)
        b, n, d, h, o = (32, 1024, 128, 256, 128)
        features = jax.random.normal(ks[0], (b, n, d), dtype=jnp.float32)
        A = jax.random.uniform(ks[1], (n, n), dtype=jnp.float32)
        lim1 = float(np.sqrt(6.0 / (d + h)))
        W1 = jax.random.uniform(ks[2], (h, d), minval=-lim1, maxval=lim1, dtype=jnp.float32)
        b1 = jnp.zeros((h,), jnp.float32)
        lim2 = float(np.sqrt(6.0 / (h + o)))
        W2 = jax.random.uniform(ks[3], (o, h), minval=-lim2, maxval=lim2, dtype=jnp.float32)
        b2 = jnp.zeros((o,), jnp.float32)
        g1 = jnp.ones((h,), jnp.float32)
        be1 = jnp.zeros((h,), jnp.float32)
        g2 = jnp.ones((o,), jnp.float32)
        be2 = jnp.zeros((o,), jnp.float32)
        return {'features': features, 'A': A, 'W1': W1, 'b1': b1, 'g1': g1, 'be1': be1, 'W2': W2, 'b2': b2, 'g2': g2, 'be2': be2}
    _L2_gnn_all = _L2_gnn_setup()
    _L2_gnn_in = {k: v for k, v in _L2_gnn_all.items() if k in ('W1', 'b1', 'g1', 'be1', 'W2', 'b2', 'g2', 'be2')}
    del _L2_gnn_all

    def _L3_gnn_setup():
        import jax, jax.numpy as jnp
        import numpy as np
        ALPHA = 0.2
        key = jax.random.key(seed)
        k1, k2, k3, k4 = jax.random.split(key, 4)
        B, N, Fin, Fout = (8, 1024, 128, 128)
        h = jax.random.normal(k1, (B, N, Fin), dtype=jnp.float32)
        adj = jax.random.randint(k2, (N, N), 0, 2).astype(jnp.float32)
        adj = jnp.maximum(adj, jnp.eye(N, dtype=jnp.float32))

        def xavier(k, shape, gain=1.414):
            fan_in, fan_out = (shape[0], shape[1])
            a = gain * np.sqrt(6.0 / (fan_in + fan_out))
            return jax.random.uniform(k, shape, dtype=jnp.float32, minval=-a, maxval=a)
        W = xavier(k3, (Fin, Fout))
        a = xavier(k4, (2 * Fout, 1))
        return {'h': h, 'adj_matrix': adj, 'W': W, 'a': a}
    _L3_gnn_all = _L3_gnn_setup()
    _L3_gnn_in = {k: v for k, v in _L3_gnn_all.items() if k in ('W', 'a')}
    del _L3_gnn_all
    return {'x': x, 'adj': adj, 'L0_gnn_Wg0': _L0_gnn_in['Wg0'], 'L0_gnn_bg0': _L0_gnn_in['bg0'], 'L0_gnn_Wg1': _L0_gnn_in['Wg1'], 'L0_gnn_bg1': _L0_gnn_in['bg1'], 'L0_gnn_Wih': _L0_gnn_in['Wih'], 'L0_gnn_Whh': _L0_gnn_in['Whh'], 'L0_gnn_bih': _L0_gnn_in['bih'], 'L0_gnn_bhh': _L0_gnn_in['bhh'], 'L1_gnn_w1_loop': _L1_gnn_in['w1_loop'], 'L1_gnn_w1_neigh': _L1_gnn_in['w1_neigh'], 'L1_gnn_b1': _L1_gnn_in['b1'], 'L1_gnn_w2_loop': _L1_gnn_in['w2_loop'], 'L1_gnn_w2_neigh': _L1_gnn_in['w2_neigh'], 'L1_gnn_b2': _L1_gnn_in['b2'], 'L2_gnn_W1': _L2_gnn_in['W1'], 'L2_gnn_b1': _L2_gnn_in['b1'], 'L2_gnn_g1': _L2_gnn_in['g1'], 'L2_gnn_be1': _L2_gnn_in['be1'], 'L2_gnn_W2': _L2_gnn_in['W2'], 'L2_gnn_b2': _L2_gnn_in['b2'], 'L2_gnn_g2': _L2_gnn_in['g2'], 'L2_gnn_be2': _L2_gnn_in['be2'], 'L3_gnn_W': _L3_gnn_in['W'], 'L3_gnn_a': _L3_gnn_in['a']}

def reference(x, adj, L0_gnn_Wg0, L0_gnn_bg0, L0_gnn_Wg1, L0_gnn_bg1, L0_gnn_Wih, L0_gnn_Whh, L0_gnn_bih, L0_gnn_bhh, L1_gnn_w1_loop, L1_gnn_w1_neigh, L1_gnn_b1, L1_gnn_w2_loop, L1_gnn_w2_neigh, L1_gnn_b2, L2_gnn_W1, L2_gnn_b1, L2_gnn_g1, L2_gnn_be1, L2_gnn_W2, L2_gnn_b2, L2_gnn_g2, L2_gnn_be2, L3_gnn_W, L3_gnn_a):
    import jax
    import jax.numpy as jnp

    def _L0_gnn_ref(x, adj, Wg0, bg0, Wg1, bg1, Wih, Whh, bih, bhh):
        import jax, jax.numpy as jnp
        import numpy as np
        B, T, D, H = (64, 1024, 128, 128)
        MAX_SKIP = 4

        def _lstm_last(Wih, Whh, bih, bhh, xs):
            N, _, Hd = xs.shape
            bias = bih + bhh

            def step(carry, x_t):
                h, c = carry
                g = x_t @ Wih.T + h @ Whh.T + bias
                i, f, gg, o = jnp.split(g, 4, axis=-1)
                c = jax.nn.sigmoid(f) * c + jax.nn.sigmoid(i) * jnp.tanh(gg)
                h = jax.nn.sigmoid(o) * jnp.tanh(c)
                return ((h, c), None)
            init = (jnp.zeros((N, Hd), xs.dtype), jnp.zeros((N, Hd), xs.dtype))
            (h_last, _), _ = jax.lax.scan(step, init, jnp.swapaxes(xs, 0, 1))
            return h_last
        h = jax.nn.relu(jnp.einsum('ts,bsh->bth', adj, x @ Wg0 + bg0))
        h = jax.nn.relu(jnp.einsum('ts,bsh->bth', adj, h @ Wg1 + bg1))
        Bv, Tv, Hd = h.shape
        for p in range(1, MAX_SKIP + 1):
            nw = Tv // p
            wins = h[:, :nw * p, :].reshape(Bv * nw, p, Hd)
            last = _lstm_last(Wih[p - 1], Whh[p - 1], bih[p - 1], bhh[p - 1], wins)
            idx = jnp.arange(nw) * p + (p - 1)
            h = h.at[:, idx, :].set(last.reshape(Bv, nw, Hd))
        return h

    def _L1_gnn_ref(x, adj, w1_loop, w1_neigh, b1, w2_loop, w2_neigh, b2):
        import jax, jax.numpy as jnp
        import numpy as np
        N = 3445
        B = 32
        IN_DIM = 128
        HID_DIM = 128

        def _make_adj(key):
            a = jax.random.uniform(key, (N, N), dtype=jnp.float32)
            a = (a < 0.001).astype(jnp.float32)
            a = jnp.maximum(a, a.T)
            deg = jnp.sum(a, axis=1, keepdims=True)
            return a / jnp.maximum(deg, 1.0)

        def _graph_conv(x, adj, w_loop, w_neigh, b):
            loop = jnp.einsum('bnd,dh->bnh', x, w_loop)
            neigh = jnp.einsum('nm,bmh->bnh', adj, jnp.einsum('bnd,dh->bnh', x, w_neigh))
            return loop + neigh + b
        h = jax.nn.relu(_graph_conv(x, adj, w1_loop, w1_neigh, b1))
        h = jax.nn.relu(_graph_conv(h, adj, w2_loop, w2_neigh, b2))
        return (x + h) * 0.5

    def _L2_gnn_ref(features, A, W1, b1, g1, be1, W2, b2, g2, be2):
        import jax, jax.numpy as jnp
        import numpy as np
        EPS = 1e-05

        def _batchnorm(x, gamma, beta):
            mu = jnp.mean(x, axis=0)
            var = jnp.var(x, axis=0)
            return (x - mu) * jax.lax.rsqrt(var + EPS) * gamma + beta
        b, n, d = features.shape
        A_norm = A + jnp.eye(n, dtype=A.dtype)
        deg = jnp.sum(A_norm, axis=0) + jnp.sum(A_norm, axis=1) - jnp.diagonal(A_norm)
        dinv = jax.lax.rsqrt(deg)
        A_hat = A_norm * dinv[:, None] * dinv[None, :]
        agg = jnp.einsum('nm,bmd->bnd', A_hat, features)
        x = agg.reshape(-1, d)
        h = jax.nn.relu(_batchnorm(x @ W1.T + b1, g1, be1))
        out = h @ W2.T + b2
        out = _batchnorm(out, g2, be2)
        return out.reshape(b, n, -1)

    def _L3_gnn_ref(h, adj_matrix, W, a):
        import jax, jax.numpy as jnp
        import numpy as np
        ALPHA = 0.2
        Fout = W.shape[1]
        Wh = jnp.einsum('bnf,fo->bno', h, W)
        a1, a2 = (a[:Fout, 0], a[Fout:, 0])
        s1 = Wh @ a1
        s2 = Wh @ a2
        e = s1[:, :, None] + s2[:, None, :]
        e = jnp.where(e >= 0, e, ALPHA * e)
        e = jnp.where(adj_matrix[None] == 0, -jnp.inf, e)
        attention = jax.nn.softmax(e, axis=-1)
        h_prime = jnp.einsum('bij,bjo->bio', attention, Wh)
        return h_prime
    x = _layernorm(x + _L0_gnn_ref(x, adj, L0_gnn_Wg0, L0_gnn_bg0, L0_gnn_Wg1, L0_gnn_bg1, L0_gnn_Wih, L0_gnn_Whh, L0_gnn_bih, L0_gnn_bhh), axis=-1)
    x = _layernorm(x + _L1_gnn_ref(x, adj, L1_gnn_w1_loop, L1_gnn_w1_neigh, L1_gnn_b1, L1_gnn_w2_loop, L1_gnn_w2_neigh, L1_gnn_b2), axis=-1)
    x = _layernorm(x + _L2_gnn_ref(x, adj, L2_gnn_W1, L2_gnn_b1, L2_gnn_g1, L2_gnn_be1, L2_gnn_W2, L2_gnn_b2, L2_gnn_g2, L2_gnn_be2), axis=-1)
    x = _layernorm(x + _L3_gnn_ref(x, adj, L3_gnn_W, L3_gnn_a), axis=-1)
    return x

_drawn_inputs = setup_inputs


def setup_inputs(seed=0):
    import zlib

    import numpy as np

    out = dict(_drawn_inputs(seed))
    spreads = {'L0_gnn_bg0': (0.0, 0.8),
     'L0_gnn_bg1': (0.0, 0.8),
     'L1_gnn_b1': (0.0, 0.364),
     'L1_gnn_b2': (0.0, 0.284),
     'L2_gnn_b1': (0.0, 0.8),
     'L2_gnn_g1': (1.0, 0.2),
     'L2_gnn_be1': (0.0, 0.1),
     'L2_gnn_b2': (0.0, 0.8),
     'L2_gnn_g2': (1.0, 0.2),
     'L2_gnn_be2': (0.0, 0.1)}
    factors = {'L0_gnn_Wg0': 8.0, 'L0_gnn_Wg1': 8.0, 'L0_gnn_Wih': 5.997, 'L0_gnn_Whh': 8.0}
    for name, (base, spread) in spreads.items():
        noise = np.random.default_rng([zlib.crc32(name.encode()), seed]).standard_normal(out[name].shape)
        drawn = base * np.exp(spread * noise) if base else spread * noise
        out[name] = jnp.asarray(drawn.astype(out[name].dtype))
    for name, factor in factors.items():
        out[name] = (out[name] * factor).astype(out[name].dtype)
    return out
```

```python
from contextlib import ExitStack

import concourse.bass as bass
from concourse import mybir

P = 128
B, T, D = 8, 1024, 128
NT = T // P
HALF = 512
SLOTS = 2
PAIRS = B // SLOTS
SKIPS = 4
GATE_I, GATE_F, GATE_G, GATE_O = range(4)
HID = 256
NHC = HID // P
LN_EPS = 1e-5
BN_EPS = 1e-5
ALPHA = 0.2
BLOCKED = -1e30
TPAD = T + 2

F32 = mybir.dt.float32
F32R = mybir.dt.float32r
BF16 = mybir.dt.bfloat16
ALU = mybir.AluOpType
ACT = mybir.ActivationFunctionType
AX_X = mybir.AxisListType.X


def program(nc, x, adj, Wg0, bg0, Wg1, bg1, Wih, Whh, bih, bhh,
            w1_loop, w1_neigh, b1, w2_loop, w2_neigh, b2,
            W1, c1, g1, be1, W2, c2, g2, be2, W3, a3, out):
    root = ExitStack()

    def sb(ctx, name, shape, dt=F32):
        return ctx.enter_context(nc.sbuf_tensor(name, shape, dt))

    def sem(name):
        return root.enter_context(nc.semaphore(name))

    def sems(name):
        return [sem(f"{name}{s}") for s in range(SLOTS)]

    with root:
        PS = root.enter_context(nc.psum_tensor("PS", [P, 8, HALF], F32))
        X = sb(root, "X", [P, B, NT, D])
        HT = sb(root, "HT", [P, B, TPAD])
        ident = sb(root, "ident", [P, P])
        identr = sb(root, "identr", [P, P], F32R)
        neg_half = sb(root, "neg_half", [P, NT])
        MATS = 6
        Mh = sb(root, "Mh", [P, MATS, D], F32R)
        Ml = sb(root, "Ml", [P, MATS, D], F32R)
        W1Th = sb(root, "W1Th", [P, NHC, P], F32R)
        W1Tl = sb(root, "W1Tl", [P, NHC, P], F32R)
        W2Th = sb(root, "W2Th", [P, NHC, P], F32R)
        W2Tl = sb(root, "W2Tl", [P, NHC, P], F32R)
        W3h = sb(root, "W3h", [P, D + 2], F32R)
        W3l = sb(root, "W3l", [P, D + 2], F32R)
        A2h = sb(root, "A2h", [P, 2, P], F32R)
        A2l = sb(root, "A2l", [P, 2, P], F32R)
        cols = sb(root, "cols", [P, 32])
        dinv = sb(root, "dinv", [P, NT])
        MV = sb(root, "MV", [P, SLOTS, NT, 2])
        ST = sb(root, "ST", [P, SLOTS, NT, 6])
        RSTD = sb(root, "RSTD", [P, SLOTS, NT])
        VE = sb(root, "VE", [P, SLOTS, NT])
        S1 = sb(root, "S1", [P, NHC, 2 * B, 6])
        S2 = sb(root, "S2", [P, 2 * B, 6])
        bnp = sb(root, "bnp", [P, 3, 6])
        C_B1, C_B2, C_C1, C_G1, C_BE1, C_C2, C_G2, C_BE2 = 0, 1, 2, 4, 6, 8, 9, 10
        C_LSTM = 11
        NROWS = 11

        def col(n):
            return cols[:, n:n + 1]

        def bank2(n):
            return PS[:, n:n + 2, :].rearrange("p a b -> p (a b)")

        passed = sem("passed")

        def settle(eng):
            eng.sem_inc(passed, 1)

        def passes(out_ap, lh, ll, rh, rl, start, stop):
            nc.tensor.matmul(out_ap, lh, rh, start=start, stop=False, skip_group_check=True)
            nc.tensor.matmul(out_ap, lh, rl, start=False, stop=False, skip_group_check=True)
            return nc.tensor.matmul(out_ap, ll, rh, start=False, stop=stop, skip_group_check=True)

        def times_adj(bank, lh, ll, last_terms=None):
            for h in range(2):
                cs = slice(h * HALF, (h + 1) * HALF)
                for st in range(NT):
                    mm = passes(PS[:, bank + h, :], lh[:, st, :], ll[:, st, :], ATh[:, st, cs], ATl[:, st, cs],
                                st == 0, st == NT - 1 and last_terms is None)
                if last_terms is not None:
                    mm = last_terms(bank, h, cs)
            return mm

        def node_major(bank, lh, ll, wh, wl, first=True):
            for st in range(NT):
                o = PS[:, bank + st // 4, (st % 4) * P:(st % 4 + 1) * P]
                mm = passes(o, lh[:, st * P:(st + 1) * P], ll[:, st * P:(st + 1) * P], wh, wl, first, True)
            return mm

        def transposes(bank, blocks):
            for n, block_ap in enumerate(blocks):
                mm = nc.tensor.transpose(PS[:, bank + n // 4, (n % 4) * P:(n % 4 + 1) * P], block_ap, ident[:, :])
            return mm

        dinv_row = sb(root, "dinv_row", [P, T])
        graph = ExitStack()
        ATh = sb(graph, "ATh", [P, NT, T], F32R)
        ATl = sb(graph, "ATl", [P, NT, T], F32R)
        s0 = ExitStack()
        B0 = sb(s0, "B0", [P, T])
        bg1r = sb(s0, "bg1r", [P, HALF], F32R)
        onesr = sb(s0, "onesr", [P, P], F32R)
        s1 = ExitStack()
        NAT = sb(s1, "NAT", [P, NT, T])
        ones = sb(s1, "ones", [P, P])
        STG = sb(s1, "STG", [P, 7, D])
        W1s = sb(s1, "W1s", [P, NHC, P])
        W2s = sb(s1, "W2s", [P, HID])
        a_rows = sb(s1, "a_rows", [P, 2, P])
        wa = sb(s1, "wa", [P, 2])
        bg0_rows = sb(s1, "bg0_rows", [P, D])
        bg0h = sb(s1, "bg0h", [P, D], F32R)
        bg0l = sb(s1, "bg0l", [P, D], F32R)
        bg1s = sb(s1, "bg1s", [1, D])
        bg1hs = sb(s1, "bg1hs", [1, D], F32R)
        bg1lo = sb(s1, "bg1lo", [1, HALF], F32R)
        bg1t = sb(s1, "bg1t", [1, D])
        vecs = sb(s1, "vecs", [16, P])
        lb = sb(s1, "lb", [16, P])
        lb2 = sb(s1, "lb2", [16, P])
        junk = sb(s1, "junk", [P, P])
        rsum = sb(s1, "rsum", [P, NT])
        csum = sb(s1, "csum", [P, NT, 2])
        dsum = sb(s1, "dsum", [P, NT])
        deg = sb(s1, "deg", [P, NT])
        diag = sb(s1, "diag", [P, NT, P])

        adj_in = [sem(f"adj_in{n}") for n in range(NT)]
        mats_in, vec_in, x_in, konst, dve0, act0, pe0, pool0, moved, diagonals = (
            sem(n) for n in ("mats_in", "vec_in", "x_in", "konst", "dve0", "act0", "pe0", "pool0", "moved", "diagonals"))

        def row(v):
            return v.rearrange("(a n) -> a n", a=1)

        with nc.Block() as block:
            @block.sync
            def _(sp):
                for n in range(NT):
                    sp.dma_start(NAT[:, n, :], adj[n * P:(n + 1) * P, :]).then_inc(adj_in[n], 16)
                for b in range(B):
                    sp.dma_start(X[:, b], x[b].rearrange("(t p) d -> p t d", p=P)).then_inc(x_in, 16)
                sp.wait_ge(dve0, 3)
                sp.wait_ge(konst, 7)
                sp.dma_start(bg1r[1:2, :].bitcast(F32), bg1lo[:, :].bitcast(F32)).then_inc(moved, 16)
                sp.wait_ge(moved, 16)
                sp.wait_ge(x_in, 16 * B)

            @block.scalar
            def _(act):
                for n, w in enumerate((Wg0, Wg1, w1_loop, w1_neigh, w2_loop, w2_neigh, W3)):
                    act.dma_start(STG[:, n, :], w).then_inc(mats_in, 16)
                act.dma_start(W1s[:, :, :], W1.rearrange("(c p) d -> p c d", p=P)).then_inc(mats_in, 16)
                act.dma_start(W2s[:, :], W2).then_inc(mats_in, 16)
                act.dma_start(bg0_rows[:, :], row(bg0).broadcast_to([P, D])).then_inc(mats_in, 16)
                for n in range(2):
                    act.dma_start(a_rows[:, n, :], a3[n * P:(n + 1) * P, :].rearrange("o u -> u o").broadcast_to([P, P])).then_inc(mats_in, 16)
                act.dma_start(bg1s[:, :], row(bg1)).then_inc(mats_in, 16)
                n = 0
                for v in (b1, b2, c1, g1, be1, c2, g2, be2):
                    k = v.shape[0] // P
                    act.dma_start(vecs[n:n + k, :], v.rearrange("(k p) -> k p", p=P)).then_inc(vec_in, 16)
                    n += k
                act.dma_start(lb[:, :], bih.rearrange("s (g p) -> (s g) p", p=P)).then_inc(vec_in, 16)
                act.dma_start(lb2[:, :], bhh.rearrange("s (g p) -> (s g) p", p=P)).then_inc(vec_in, 16)
                for n in range(2 * NT):
                    act.wait_ge(pe0, n + 1)
                    st, h = n // 2, n % 2
                    nc.scalar.activation(ATh[:, st, h * HALF:(h + 1) * HALF], PS[:, n % 8, :], ACT.Copy).then_inc(act0, 1)

            @block.gpsimd
            def _(pool):
                nc.gpsimd.memset(ident[:, :], 0.0).then_inc(konst, 1)
                nc.gpsimd.memset(ones[:, :], 1.0).then_inc(konst, 1)
                nc.gpsimd.memset(neg_half[:, :], -0.5).then_inc(konst, 1)
                nc.gpsimd.memset(bg1r[:, :].bitcast(F32), 0.0).then_inc(konst, 1)
                pool.wait_ge(konst, 4)
                nc.gpsimd.affine_select(out=ident[:, :], in_=ident[:, :], compare_op=ALU.not_equal, fill=1.0,
                                        base=0, pattern=[[-1, P]], channel_multiplier=1).then_inc(konst, 1)
                pool.wait_ge(konst, 5)
                nc.gpsimd.tensor_copy(identr[:, :], ident[:, :]).then_inc(konst, 1)
                nc.gpsimd.tensor_copy(onesr[:, :], ones[:, :]).then_inc(konst, 1)
                pool.wait_ge(pool0, 1)
                nc.gpsimd.tensor_tensor(dinv[:, :], deg[:, :], neg_half[:, :], ALU.pow).then_inc(pool0, 1)

            @block.vector
            def _(dve):
                count = [0]

                def done(ins):
                    count[0] += 1
                    ins.then_inc(dve0, 1)
                    dve.wait_ge(dve0, count[0])

                dve.wait_ge(mats_in, 16 * 13)
                dve.wait_ge(vec_in, 16 * 10)
                dve.wait_ge(konst, 7)
                V4 = bg1r[0:1, :].rearrange("p (r d) -> p r d", r=4)
                bg1w = bg1s[:, :].rearrange("p (r d) -> p r d", r=1).broadcast_to([1, 4, D])
                done(nc.vector.tensor_copy(bg1hs[:, :], bg1s[:, :]))
                done(nc.vector.tensor_copy(V4, bg1w))
                done(nc.vector.tensor_tensor(bg1lo[:, :].rearrange("p (r d) -> p r d", r=4), bg1w,
                                             V4.bitcast(F32), ALU.subtract))
                done(nc.vector.tensor_tensor(lb[:, :], lb[:, :], lb2[:, :], ALU.add))
                done(nc.vector.tensor_copy(Mh[:, :, :], STG[:, 0:MATS, :]))
                done(nc.vector.tensor_tensor(Ml[:, :, :], STG[:, 0:MATS, :], Mh[:, :, :].bitcast(F32), ALU.subtract))
                done(nc.vector.tensor_copy(bg0h[:, :], bg0_rows[:, :]))
                done(nc.vector.tensor_tensor(bg0l[:, :], bg0_rows[:, :], bg0h[:, :].bitcast(F32), ALU.subtract))
                for n in range(2):
                    done(nc.vector.tensor_tensor_reduce(junk[:, :], STG[:, 6, :], a_rows[:, n, :], 1.0, 0.0,
                                                        ALU.mult, ALU.add, wa[:, n:n + 1]))
                done(nc.vector.tensor_copy(W3h[:, 0:D], STG[:, 6, :]))
                done(nc.vector.tensor_copy(W3h[:, D:D + 2], wa[:, :]))
                done(nc.vector.tensor_tensor(W3l[:, 0:D], STG[:, 6, :], W3h[:, 0:D].bitcast(F32), ALU.subtract))
                done(nc.vector.tensor_tensor(W3l[:, D:D + 2], wa[:, :], W3h[:, D:D + 2].bitcast(F32), ALU.subtract))
                for n in range(2):
                    done(nc.vector.tensor_scalar(A2h[:, n, :], ones[:, :], W3h[:, D + n:D + n + 1].bitcast(F32), None, ALU.mult))
                    done(nc.vector.tensor_scalar(A2l[:, n, :], ones[:, :], W3l[:, D + n:D + n + 1].bitcast(F32), None, ALU.mult))
                for n in range(2 * NT):
                    dve.wait_ge(act0, n + 1)
                    st, h = n // 2, n % 2
                    hs = slice(h * HALF, (h + 1) * HALF)
                    nc.vector.tensor_tensor(ATl[:, st, hs], PS[:, n % 8, :], ATh[:, st, hs].bitcast(F32), ALU.subtract).then_inc(dve0, 1)
                    nc.vector.tensor_reduce(csum[:, st, h:h + 1], PS[:, n % 8, :], AX_X, ALU.add).then_inc(dve0, 1)
                count[0] += 4 * NT
                for n in range(NT):
                    nc.vector.tensor_reduce(rsum[:, n:n + 1], NAT[:, n, :], AX_X, ALU.add).then_inc(dve0, 1)
                    count[0] += 1
                    done(nc.vector.tensor_tensor_reduce(junk[:, :], NAT[:, n, n * P:(n + 1) * P], ident[:, :], 1.0, 0.0,
                                                        ALU.mult, ALU.add, dsum[:, n:n + 1]))
                dve.wait_ge(dve0, count[0])
                done(nc.vector.tensor_tensor(deg[:, :], rsum[:, :], csum[:, :, 0], ALU.add))
                done(nc.vector.tensor_tensor(deg[:, :], deg[:, :], csum[:, :, 1], ALU.add))
                done(nc.vector.scalar_tensor_tensor(out=deg[:, :], in0=deg[:, :], scalar=1.0, in1=dsum[:, :],
                                                    op0=ALU.add, op1=ALU.subtract))
                nc.vector.tensor_copy(junk[:, 0:NT], deg[:, :]).then_inc(pool0, 1)
                dve.wait_ge(pe0, 2 * NT + 1)
                sq = PS[:, 0, :].rearrange("p (c d) -> p c d", c=4)
                done(nc.vector.tensor_copy(W1Th[:, :, :], sq[:, 0:2, :]))
                done(nc.vector.tensor_tensor(W1Tl[:, :, :], sq[:, 0:2, :], W1Th[:, :, :].bitcast(F32), ALU.subtract))
                done(nc.vector.tensor_copy(W2Th[:, :, :], sq[:, 2:4, :]))
                done(nc.vector.tensor_tensor(W2Tl[:, :, :], sq[:, 2:4, :], W2Th[:, :, :].bitcast(F32), ALU.subtract))
                done(nc.vector.tensor_copy(cols[:, 0:NROWS], PS[:, 1, 0:NROWS]))
                done(nc.vector.tensor_copy(cols[:, C_LSTM:C_LSTM + 16], PS[:, 1, 16:32]))
                done(nc.vector.tensor_scalar(col(C_B2), col(C_B2), 0.5, None, ALU.mult))
                dve.wait_ge(pe0, 2 * NT + 2)
                done(nc.vector.tensor_copy(B0[:, :], bank2(2)))
                dve.wait_ge(pool0, 2)
                for n in range(NT):
                    nc.vector.tensor_scalar(diag[:, n, :], ident[:, :], dinv[:, n:n + 1], None, ALU.mult).then_inc(diagonals, 1)
                dve.wait_ge(pe0, 2 * NT + 3)
                nc.vector.tensor_copy(dinv_row[:, :], bank2(4)).then_inc(dve0, 1)

            @block.tensor
            def _(pe):
                pe.wait_ge(konst, 7)
                for n in range(NT):
                    pe.wait_ge(adj_in[n], 16)
                for n in range(2 * NT):
                    st, h = n // 2, n % 2
                    if n >= 8:
                        pe.wait_ge(dve0, 18 + 2 * (n - 8) + 2)
                    for k in range(4):
                        mm = nc.tensor.transpose(PS[:, n % 8, k * P:(k + 1) * P],
                                                 NAT[:, 4 * h + k, st * P:(st + 1) * P], ident[:, :])
                    mm.then_inc(pe0, 1)
                pe.wait_ge(dve0, 18 + 4 * NT)
                for c in range(NHC):
                    nc.tensor.transpose(PS[:, 0, c * P:(c + 1) * P], W1s[:, c, :], ident[:, :])
                    nc.tensor.transpose(PS[:, 0, (2 + c) * P:(3 + c) * P], W2s[:, c * P:(c + 1) * P], ident[:, :])
                nc.tensor.transpose(PS[:, 1, 0:NROWS], vecs[0:NROWS, :], ident[0:NROWS, 0:NROWS])
                nc.tensor.transpose(PS[:, 1, 16:32], lb[:, :], ident[0:16, 0:16]).then_inc(pe0, 1)
                for h in range(2):
                    hs = slice(h * HALF, (h + 1) * HALF)
                    for st in range(NT):
                        mm = passes(PS[:, 2 + h, :], bg0h[:, :], bg0l[:, :], ATh[:, st, hs], ATl[:, st, hs], st == 0, st == NT - 1)
                mm.then_inc(pe0, 1)
                pe.wait_ge(diagonals, NT)
                for h in range(2):
                    mm = nc.tensor.matmul(PS[:, 4 + h, :], ones[:, :], diag[:, 4 * h:4 * h + 4, :], start=True, stop=True)
                mm.then_inc(pe0, 1)
        s1.close()

        st_ = ExitStack()
        Nh = [sb(st_, f"g0n_h{s}", [P, NT, D], F32R) for s in range(SLOTS)]
        Nl = [sb(st_, f"g0n_l{s}", [P, NT, D], F32R) for s in range(SLOTS)]
        Fh = [sb(st_, f"g0f_h{s}", [P, T], F32R) for s in range(SLOTS)]
        Fl = [sb(st_, f"g0f_l{s}", [P, T], F32R) for s in range(SLOTS)]
        Z = [sb(st_, f"g0z{s}", [P, T]) for s in range(SLOTS)]
        hi0, lo0, prod0, z0 = sems("g0_hi"), sems("g0_lo"), sems("g0_prod"), sems("g0_z")
        pad0 = sem("g0_pad")
        KH, KL, KP = 5, 4, 4

        def flat(t):
            return t[:, :, :].rearrange("p a b -> p (a b)")

        with nc.Block() as block:
            @block.scalar
            def _(act):
                with act.Fori(0, PAIRS) as it:
                    for s in range(SLOTS):
                        nc.scalar.activation(flat(Nh[s]), X[:, it * SLOTS + s].rearrange("p a b -> p (a b)"), ACT.Copy).then_inc(hi0[s], 1)
                    for s in range(SLOTS):
                        act.wait_ge(prod0[s], it * KP + 1)
                        nc.scalar.activation(Fh[s][:, :], bank2(4 * s), ACT.Copy).then_inc(hi0[s], 1)
                    for s in range(SLOTS):
                        act.wait_ge(z0[s], it + 1)
                        nc.scalar.activation(Fh[s][:, :], Z[s][:, :], ACT.Relu).then_inc(hi0[s], 1)
                    for s in range(SLOTS):
                        act.wait_ge(prod0[s], it * KP + 3)
                        nc.scalar.activation(flat(Nh[s]), bank2(4 * s), ACT.Copy).then_inc(hi0[s], 1)
                    for s in range(SLOTS):
                        act.wait_ge(prod0[s], it * KP + 4)
                        nc.scalar.activation(HT[:, it * SLOTS + s, 0:T], bank2(4 * s + 2), ACT.Relu).then_inc(hi0[s], 1)

            @block.vector
            def _(dve):
                nc.vector.memset(HT[:, :, T:TPAD], 0.0).then_inc(pad0, 1)
                with dve.Fori(0, PAIRS) as it:
                    for s in range(SLOTS):
                        dve.wait_ge(hi0[s], it * KH + 1)
                        nc.vector.tensor_tensor(flat(Nl[s]), X[:, it * SLOTS + s].rearrange("p a b -> p (a b)"),
                                                flat(Nh[s]).bitcast(F32), ALU.subtract).then_inc(lo0[s], 1)
                    for s in range(SLOTS):
                        dve.wait_ge(hi0[s], it * KH + 2)
                        nc.vector.tensor_tensor(Fl[s][:, :], bank2(4 * s), Fh[s][:, :].bitcast(F32), ALU.subtract).then_inc(lo0[s], 1)
                    for s in range(SLOTS):
                        dve.wait_ge(prod0[s], it * KP + 2)
                        nc.vector.tensor_tensor(Z[s][:, :], bank2(4 * s + 2), B0[:, :], ALU.add).then_inc(z0[s], 1)
                    for s in range(SLOTS):
                        dve.wait_ge(hi0[s], it * KH + 3)
                        nc.vector.scalar_tensor_tensor(out=Fl[s][:, :], in0=Z[s][:, :], scalar=0.0, in1=Fh[s][:, :].bitcast(F32),
                                                       op0=ALU.max, op1=ALU.subtract).then_inc(lo0[s], 1)
                    for s in range(SLOTS):
                        dve.wait_ge(hi0[s], it * KH + 4)
                        nc.vector.tensor_tensor(flat(Nl[s]), bank2(4 * s), flat(Nh[s]).bitcast(F32), ALU.subtract).then_inc(lo0[s], 1)
                    for s in range(SLOTS):
                        dve.wait_ge(prod0[s], it * KP + 4)
                        dve.wait_ge(hi0[s], it * KH + 5)

            @block.tensor
            def _(pe):
                with pe.Fori(0, PAIRS) as it:
                    for s in range(SLOTS):
                        pe.wait_ge(lo0[s], it * KL + 1)
                        times_adj(4 * s, Nh[s], Nl[s]).then_inc(prod0[s], 1)
                    for s in range(SLOTS):
                        pe.wait_ge(lo0[s], it * KL + 2)
                        for h in range(2):
                            hs = slice(h * HALF, (h + 1) * HALF)
                            mm = passes(PS[:, 4 * s + 2 + h, :], Mh[:, 0, :], Ml[:, 0, :], Fh[s][:, hs], Fl[s][:, hs], True, True)
                        mm.then_inc(prod0[s], 1)
                    for s in range(SLOTS):
                        pe.wait_ge(lo0[s], it * KL + 3)
                        for h in range(2):
                            nc.tensor.matmul(PS[:, 4 * s + h, :], onesr[:, :], bg1r[:, :], start=True, stop=False, skip_group_check=True)
                        node_major(4 * s, Fh[s], Fl[s], Mh[:, 1, :], Ml[:, 1, :], first=False).then_inc(prod0[s], 1)
                    for s in range(SLOTS):
                        pe.wait_ge(lo0[s], it * KL + 4)
                        times_adj(4 * s + 2, Nh[s], Nl[s]).then_inc(prod0[s], 1)
                    for s in range(SLOTS):
                        pe.wait_ge(hi0[s], it * KH + 5)
        st_.close()
        s0.close()

        lstm = ExitStack()
        WIh = sb(lstm, "WIh", [P, SKIPS, 4, P], F32R)
        WIl = sb(lstm, "WIl", [P, SKIPS, 4, P], F32R)
        WHh = sb(lstm, "WHh", [P, SKIPS - 1, 4, P], F32R)
        WHl = sb(lstm, "WHl", [P, SKIPS - 1, 4, P], F32R)
        ls = ExitStack()
        WIs = sb(ls, "WIs", [P, SKIPS * 4, P])
        WHs = sb(ls, "WHs", [P, (SKIPS - 1) * 4, P])
        NI, NH = SKIPS, SKIPS - 1
        lw_in, lw_t, lw_hi, lw_lo = (sem(n) for n in ("lw_in", "lw_t", "lw_hi", "lw_lo"))
        with nc.Block() as block:
            @block.sync
            def _(sp):
                sp.dma_start(WIs[:, :, :], Wih.rearrange("s (g p) d -> p (s g) d", p=P)).then_inc(lw_in, 16)
                sp.dma_start(WHs[:, :, :], Whh[1:SKIPS].rearrange("s (g p) d -> p (s g) d", p=P)).then_inc(lw_in, 16)

            @block.tensor
            def _(pe):
                pe.wait_ge(lw_in, 32)
                for n in range(NI + NH):
                    for k in range(4):
                        src = WIs[:, 4 * n + k, :] if n < NI else WHs[:, 4 * (n - NI) + k, :]
                        mm = nc.tensor.transpose(PS[:, n, k * P:(k + 1) * P], src, ident[:, :])
                    mm.then_inc(lw_t, 1)

            @block.scalar
            def _(act):
                for n in range(NI + NH):
                    act.wait_ge(lw_t, n + 1)
                    hi = WIh[:, n] if n < NI else WHh[:, n - NI]
                    nc.scalar.activation(hi.rearrange("p g o -> p (g o)"), PS[:, n, :], ACT.Copy).then_inc(lw_hi, 1)

            @block.vector
            def _(dve):
                for n in range(NI + NH):
                    dve.wait_ge(lw_hi, n + 1)
                    hi, lo = (WIh[:, n], WIl[:, n]) if n < NI else (WHh[:, n - NI], WHl[:, n - NI])
                    nc.vector.tensor_tensor(lo.rearrange("p g o -> p (g o)"), PS[:, n, :],
                                            hi.rearrange("p g o -> p (g o)").bitcast(F32), ALU.subtract).then_inc(lw_lo, 1)
        ls.close()

        XSh = [sb(lstm, f"xs_h{s}", [P, TPAD], F32R) for s in range(SLOTS)]
        XSl = [sb(lstm, f"xs_l{s}", [P, TPAD], F32R) for s in range(SLOTS)]
        HRh = [sb(lstm, f"hr_h{s}", [P, HALF], F32R) for s in range(SLOTS)]
        HRl = [sb(lstm, f"hr_l{s}", [P, HALF], F32R) for s in range(SLOTS)]
        work = X[:, :, :, :].rearrange("p (s k) a d -> p s k (a d)", s=SLOTS)
        gates = [[work[:, s, k // 2, (k % 2) * HALF:(k % 2 + 1) * HALF] for k in range(4)] for s in range(SLOTS)]
        C, IG, TC, HN = ([work[:, s, k // 2, (k % 2) * HALF:(k % 2 + 1) * HALF] for s in range(SLOTS)] for k in (4, 5, 6, 7))
        UNITS = [(1, 0, 0, HALF), (1, 0, HALF, HALF)]
        UNITS += [(p, k, 0, n) for p, n in ((2, T // 2), (3, TPAD // 3), (4, T // 4)) for k in range(p)]
        FIRST, LATER = (GATE_I, GATE_G, GATE_O), (GATE_I, GATE_G, GATE_F, GATE_O)

        def gates_of(k):
            return LATER if k else FIRST

        NGATES = sum(len(gates_of(k)) for _, k, _, _ in UNITS)
        NU = len(UNITS)
        NSTATES = sum(k < p - 1 for p, k, _, _ in UNITS)
        NSUMS = sum(k > 0 for _, k, _, _ in UNITS)
        xs_ok, gate_ok, gate_read, cell_ok, tanh_ok, h_ok, state_ok, xh_ok, fc_ok, hh_ok = (
            sems(n) for n in ("xs_ok", "gate_ok", "gate_read", "cell_ok", "tanh_ok", "h_ok", "state_ok", "xh_ok", "fc_ok", "hh_ok"))

        with nc.Block() as block:
            @block.tensor
            def _(pe):
                with pe.Fori(0, PAIRS) as it:
                    n_gates = n_states = 0
                    for u, (p, k, w0, n) in enumerate(UNITS):
                        gs = gates_of(k)
                        for s in range(SLOTS):
                            if k == 0 and w0 == 0:
                                pe.wait_ge(xs_ok[s], it * SKIPS + p)
                            if u:
                                pe.wait_ge(gate_read[s], it * NGATES + n_gates)
                            c0 = k * n + w0
                            for g in gs:
                                mm = passes(PS[:, 4 * s + g, 0:n], WIh[:, p - 1, g], WIl[:, p - 1, g],
                                            XSh[s][:, c0:c0 + n], XSl[s][:, c0:c0 + n], True, k == 0)
                                if k == 0:
                                    mm.then_inc(gate_ok[s], 1)
                            if k:
                                pe.wait_ge(state_ok[s], it * NSTATES + n_states)
                                for g in gs:
                                    passes(PS[:, 4 * s + g, 0:n], WHh[:, p - 2, g], WHl[:, p - 2, g],
                                           HRh[s][:, 0:n], HRl[s][:, 0:n], False, True).then_inc(gate_ok[s], 1)
                        n_gates += len(gs)
                        n_states += k < p - 1

            @block.scalar
            def _(act):
                nc.scalar.preload_act_table(ACT.Sigmoid)
                with act.Fori(0, PAIRS) as it:
                    n_gates = 0
                    for u, (p, k, w0, n) in enumerate(UNITS):
                        gs = gates_of(k)
                        for s in range(SLOTS):
                            if u:
                                act.wait_ge(h_ok[s], it * NU + u)
                            for j, g in enumerate(gs):
                                act.wait_ge(gate_ok[s], it * NGATES + n_gates + j + 1)
                                nc.scalar.activation(gates[s][g][:, 0:n], PS[:, 4 * s + g, 0:n],
                                                     ACT.Tanh if g == GATE_G else ACT.Sigmoid,
                                                     bias=col(C_LSTM + 4 * (p - 1) + g)).then_inc(gate_read[s], 1)
                            act.wait_ge(cell_ok[s], it * NU + u + 1)
                            nc.scalar.activation(TC[s][:, 0:n], C[s][:, 0:n], ACT.Tanh).then_inc(tanh_ok[s], 1)
                        n_gates += len(gs)

            @block.vector
            def _(dve):
                with dve.Fori(0, PAIRS) as it:
                    def inputs(s, p, n):
                        src = HT[:, it * SLOTS + s, 0:p * n].rearrange("q (w k) -> q k w", k=p)
                        dst = [t[s][:, 0:p * n].rearrange("q (k w) -> q k w", k=p) for t in (XSh, XSl)]
                        nc.vector.tensor_scalar(dst[0], src, 1.0, None, ALU.mult).then_inc(xh_ok[s], 1)
                        dve.wait_ge(xh_ok[s], it * SKIPS + p)
                        nc.vector.tensor_tensor(dst[1], src, dst[0].bitcast(F32), ALU.subtract).then_inc(xs_ok[s], 1)

                    for s in range(SLOTS):
                        inputs(s, 1, T)
                    n_gates = n_states = n_sums = 0
                    for u, (p, k, w0, n) in enumerate(UNITS):
                        gs = gates_of(k)
                        last = k == p - 1
                        for s in range(SLOTS):
                            gi, gf, gg, go = (gates[s][g][:, 0:n] for g in (GATE_I, GATE_F, GATE_G, GATE_O))
                            c, ig, tc, hn = (t[s][:, 0:n] for t in (C, IG, TC, HN))
                            dve.wait_ge(gate_read[s], it * NGATES + n_gates + 2)
                            if k == 0:
                                nc.vector.tensor_tensor(c, gi, gg, ALU.mult).then_inc(cell_ok[s], 1)
                            else:
                                nc.vector.tensor_tensor(ig, gi, gg, ALU.mult)
                                dve.wait_ge(gate_read[s], it * NGATES + n_gates + 3)
                                nc.vector.tensor_tensor(c, gf, c, ALU.mult).then_inc(fc_ok[s], 1)
                                dve.wait_ge(fc_ok[s], it * NSUMS + n_sums + 1)
                                nc.vector.tensor_tensor(c, c, ig, ALU.add).then_inc(cell_ok[s], 1)
                            dve.wait_ge(tanh_ok[s], it * NU + u + 1)
                            if last:
                                m = min(n, T // p)
                                if p == 1:
                                    dst = HT[:, it * SLOTS + s, w0:w0 + n]
                                else:
                                    dst = HT[:, it * SLOTS + s, 0:m * p].rearrange("q (w k) -> q w k", k=p)[:, :, k]
                                nc.vector.tensor_tensor(dst, go[:, 0:m], tc[:, 0:m], ALU.mult).then_inc(h_ok[s], 1)
                                if p < SKIPS and (p > 1 or w0):
                                    dve.wait_ge(h_ok[s], it * NU + u + 1)
                                    inputs(s, p + 1, UNITS[u + 1][3])
                            else:
                                nc.vector.tensor_tensor(hn, go, tc, ALU.mult).then_inc(h_ok[s], 1)
                                dve.wait_ge(h_ok[s], it * NU + u + 1)
                                nc.vector.tensor_copy(HRh[s][:, 0:n], hn).then_inc(hh_ok[s], 1)
                                dve.wait_ge(hh_ok[s], it * NSTATES + n_states + 1)
                                nc.vector.tensor_tensor(HRl[s][:, 0:n], hn, HRh[s][:, 0:n].bitcast(F32),
                                                        ALU.subtract).then_inc(state_ok[s], 1)
                        n_gates += len(gs)
                        n_states += not last
                        n_sums += k > 0
                    for s in range(SLOTS):
                        dve.wait_ge(h_ok[s], it * NU + NU)
        lstm.close()

        class Norm:

            def __init__(self):
                self.base, self.n = 0, 0
                self.stats, self.var, self.eps, self.rstd, self.done = (
                    sems(f"norm_{k}") for k in ("stats", "var", "eps", "rstd", "done"))

            def stage(self, per_pass):
                self.base += self.n * PAIRS
                self.n = per_pass

            def at(self, it, k):
                return it * self.n + (self.base + k)

            def dve(self, dve, it, s, k, rows):
                for t in range(NT):
                    mm = nc.vector.bn_stats(ST[:, s, t, :], rows[:, t, :])
                mm.then_inc(self.stats[s], 1)
                dve.wait_ge(self.stats[s], self.at(it, k))
                settle(dve)
                for t in range(NT):
                    mm = nc.vector.bn_aggr(MV[:, s, t, :], ST[:, s, t, :])
                mm.then_inc(self.var[s], 1)

            def dve_scale(self, dve, it, s, k, rows, to):
                dve.wait_ge(self.rstd[s], self.at(it, k))
                for t in range(NT):
                    mm = nc.vector.tensor_scalar(to[:, t, :], rows[:, t, :], MV[:, s, t, 0:1], RSTD[:, s, t:t + 1],
                                                 ALU.subtract, ALU.mult)
                mm.then_inc(self.done[s], 1)

            def pool(self, pool, it, s, k):
                pool.wait_ge(self.var[s], self.at(it, k))
                settle(pool)
                nc.gpsimd.tensor_scalar(VE[:, s, :], MV[:, s, :, 1], LN_EPS, None, ALU.add).then_inc(self.eps[s], 1)
                pool.wait_ge(self.eps[s], self.at(it, k))
                nc.gpsimd.tensor_tensor(RSTD[:, s, :], VE[:, s, :], neg_half[:, :], ALU.pow).then_inc(self.rstd[s], 1)

        norm = Norm()

        def flat(t):
            return t.rearrange("p a b -> p (a b)")

        l1 = ExitStack()
        Uh = [sb(l1, f"l1u_h{s}", [P, NT, D], F32R) for s in range(SLOTS)]
        Ul = [sb(l1, f"l1u_l{s}", [P, NT, D], F32R) for s in range(SLOTS)]
        Fh = [sb(l1, f"l1f_h{s}", [P, T], F32R) for s in range(SLOTS)]
        Fl = [sb(l1, f"l1f_l{s}", [P, T], F32R) for s in range(SLOTS)]
        Z = [sb(l1, f"l1z{s}", [P, T]) for s in range(SLOTS)]
        XN = [sb(l1, f"l1x{s}", [P, NT, D]) for s in range(SLOTS)]
        x1_in, t1, h1, l1o, y1, z1 = (sems(n) for n in ("x1_in", "l1_pe", "l1_act", "l1_lo", "l1_y", "l1_zh"))
        norm.stage(2)
        KP, KH, KL = 7, 6, 4

        with nc.Block() as block:
            @block.sync
            def _(sp):
                for s in range(SLOTS):
                    sp.dma_start(XN[s][:, :, :], x[s].rearrange("(t p) d -> p t d", p=P)).then_inc(x1_in[s], 16)
                with sp.Fori(1, PAIRS) as it:
                    for s in range(SLOTS):
                        sp.wait_ge(norm.done[s], norm.at(it, 0))
                        sp.dma_start(XN[s][:, :, :], x[it * SLOTS + s].rearrange("(t p) d -> p t d", p=P)).then_inc(x1_in[s], 16)

            @block.tensor
            def _(pe):
                with pe.Fori(0, PAIRS) as it:
                    for s in range(SLOTS):
                        pe.wait_ge(h1[s], it * KH + 1)
                        transposes(4 * s, [Z[s][:, t * P:(t + 1) * P] for t in range(NT)]).then_inc(t1[s], 1)
                    for s in range(SLOTS):
                        pe.wait_ge(norm.done[s], norm.at(it, 1))
                        transposes(4 * s + 2, [XN[s][:, t, :] for t in range(NT)]).then_inc(t1[s], 1)
                    for s in range(SLOTS):
                        pe.wait_ge(l1o[s], it * KL + 1)
                        node_major(4 * s, Fh[s], Fl[s], Mh[:, 3, :], Ml[:, 3, :]).then_inc(t1[s], 1)
                    for layer in range(2):
                        loop = 2 + 2 * layer

                        def own(bank, h, cs):
                            return passes(PS[:, bank + h, :], Mh[:, loop, :], Ml[:, loop, :], Fh[s][:, cs], Fl[s][:, cs], False, True)
                        for s in range(SLOTS):
                            pe.wait_ge(l1o[s], it * KL + 2 + 2 * layer)
                            times_adj(4 * s + 2, Uh[s], Ul[s], own).then_inc(t1[s], 1)
                        if layer == 0:
                            for s in range(SLOTS):
                                pe.wait_ge(l1o[s], it * KL + 3)
                                node_major(4 * s, Fh[s], Fl[s], Mh[:, 5, :], Ml[:, 5, :]).then_inc(t1[s], 1)
                    for s in range(SLOTS):
                        pe.wait_ge(h1[s], it * KH + 6)
                        transposes(4 * s, [Z[s][:, t * P:(t + 1) * P] for t in range(NT)]).then_inc(t1[s], 1)
                    for s in range(SLOTS):
                        pe.wait_ge(y1[s], it * 2 + 2)

            @block.scalar
            def _(act):
                with act.Fori(0, PAIRS) as it:
                    for s in range(SLOTS):
                        nc.scalar.activation(Z[s][:, :], HT[:, it * SLOTS + s, 0:T], ACT.Copy).then_inc(h1[s], 1)
                    for s in range(SLOTS):
                        act.wait_ge(t1[s], it * KP + 2)
                        nc.scalar.activation(Fh[s][:, :], bank2(4 * s + 2), ACT.Copy).then_inc(h1[s], 1)
                    for s in range(SLOTS):
                        act.wait_ge(t1[s], it * KP + 3)
                        nc.scalar.activation(flat(Uh[s][:, :, :]), bank2(4 * s), ACT.Copy).then_inc(h1[s], 1)
                    for s in range(SLOTS):
                        act.wait_ge(t1[s], it * KP + 4)
                        nc.scalar.activation(Z[s][:, :], bank2(4 * s + 2), ACT.Relu, bias=col(C_B1)).then_inc(h1[s], 1)
                    for s in range(SLOTS):
                        act.wait_ge(t1[s], it * KP + 5)
                        nc.scalar.activation(flat(Uh[s][:, :, :]), bank2(4 * s), ACT.Copy).then_inc(h1[s], 1)
                    for s in range(SLOTS):
                        act.wait_ge(t1[s], it * KP + 6)
                        nc.scalar.activation(Z[s][:, :], bank2(4 * s + 2), ACT.Relu, bias=col(C_B2), scale=0.5).then_inc(h1[s], 1)
                    for s in range(SLOTS):
                        act.wait_ge(t1[s], it * KP + 7)

            @block.gpsimd
            def _(pool):
                with pool.Fori(0, PAIRS) as it:
                    for k in (1, 2):
                        for s in range(SLOTS):
                            norm.pool(pool, it, s, k)

            @block.vector
            def _(dve):
                with dve.Fori(0, PAIRS) as it:
                    for s in range(SLOTS):
                        dve.wait_ge(x1_in[s], it * 16 + 16)
                        dve.wait_ge(t1[s], it * KP + 1)
                        nc.vector.tensor_tensor(flat(XN[s][:, :, :]), flat(XN[s][:, :, :]), bank2(4 * s), ALU.add).then_inc(y1[s], 1)
                        dve.wait_ge(y1[s], it * 2 + 1)
                        norm.dve(dve, it, s, 1, XN[s])
                    for s in range(SLOTS):
                        norm.dve_scale(dve, it, s, 1, XN[s], XN[s])
                    for s in range(SLOTS):
                        dve.wait_ge(h1[s], it * KH + 2)
                        nc.vector.tensor_tensor(Fl[s][:, :], bank2(4 * s + 2), Fh[s][:, :].bitcast(F32), ALU.subtract).then_inc(l1o[s], 1)
                    for s in range(SLOTS):
                        dve.wait_ge(h1[s], it * KH + 3)
                        nc.vector.tensor_tensor(flat(Ul[s][:, :, :]), bank2(4 * s), flat(Uh[s][:, :, :]).bitcast(F32), ALU.subtract).then_inc(l1o[s], 1)
                    for s in range(SLOTS):
                        dve.wait_ge(h1[s], it * KH + 4)
                        nc.vector.tensor_copy(Fh[s][:, :], Z[s][:, :]).then_inc(z1[s], 1)
                        dve.wait_ge(z1[s], it + 1)
                        nc.vector.tensor_tensor(Fl[s][:, :], Z[s][:, :], Fh[s][:, :].bitcast(F32), ALU.subtract).then_inc(l1o[s], 1)
                    for s in range(SLOTS):
                        dve.wait_ge(h1[s], it * KH + 5)
                        nc.vector.tensor_tensor(flat(Ul[s][:, :, :]), bank2(4 * s), flat(Uh[s][:, :, :]).bitcast(F32), ALU.subtract).then_inc(l1o[s], 1)
                    for s in range(SLOTS):
                        dve.wait_ge(t1[s], it * KP + 7)
                        nc.vector.scalar_tensor_tensor(out=flat(XN[s][:, :, :]), in0=flat(XN[s][:, :, :]), scalar=1.5, in1=bank2(4 * s),
                                                       op0=ALU.mult, op1=ALU.add).then_inc(y1[s], 1)
                        dve.wait_ge(y1[s], it * 2 + 2)
                        norm.dve(dve, it, s, 2, XN[s])
                    for s in range(SLOTS):
                        norm.dve_scale(dve, it, s, 2, XN[s], X[:, it * SLOTS + s])
                    for s in range(SLOTS):
                        dve.wait_ge(norm.done[s], norm.at(it, 2))
        l1.close()

        l2 = ExitStack()
        HP1 = sb(l2, "HP1", [P, B, T])
        l2a = ExitStack()
        Yh = [sb(l2a, f"l2y_h{s}", [P, T], F32R) for s in range(SLOTS)]
        Yl = [sb(l2a, f"l2y_l{s}", [P, T], F32R) for s in range(SLOTS)]
        ZZ = sb(l2a, "l2z", [P, T])
        pe2, hi2, lo2, zh2, za2, bs2 = (sems(n) for n in ("l2_pe", "l2_act", "l2_lo", "l2_zh", "l2_za", "l2_bs"))

        def tiles(t):
            return t[:, :].rearrange("p (t d) -> p t d", t=NT)

        def hidden(c, b):
            return (HT if c == 0 else HP1)[:, b, 0:T]

        with nc.Block() as block:
            @block.scalar
            def _(act):
                with act.Fori(0, PAIRS) as it:
                    for s in range(SLOTS):
                        for t in range(NT):
                            ins = nc.scalar.activation(tiles(Yh[s])[:, t, :], X[:, it * SLOTS + s, t, :], ACT.Copy, scale=dinv[:, t:t + 1])
                        ins.then_inc(hi2[s], 1)
                    for s in range(SLOTS):
                        for c in range(NHC):
                            act.wait_ge(pe2[s], it * 3 + 2 + c)
                            settle(act)
                            nc.scalar.activation(hidden(c, it * SLOTS + s), bank2(4 * s + 2 - 2 * c), ACT.Identity, bias=col(C_C1 + c)).then_inc(hi2[s], 1)

            @block.vector
            def _(dve):
                with dve.Fori(0, PAIRS) as it:
                    for s in range(SLOTS):
                        dve.wait_ge(hi2[s], it * 3 + 1)
                        for t in range(NT):
                            ins = nc.vector.scalar_tensor_tensor(out=tiles(Yl[s])[:, t, :], in0=X[:, it * SLOTS + s, t, :], scalar=dinv[:, t:t + 1],
                                                                 in1=tiles(Yh[s])[:, t, :].bitcast(F32), op0=ALU.mult, op1=ALU.subtract)
                        ins.then_inc(lo2[s], 1)
                    for s in range(SLOTS):
                        dve.wait_ge(pe2[s], it * 3 + 1)
                        nc.vector.tensor_tensor(ZZ[:, :], bank2(4 * s), dinv_row[:, :], ALU.mult).then_inc(za2[s], 1)
                        dve.wait_ge(za2[s], it + 1)
                        nc.vector.tensor_copy(Yh[s][:, :], ZZ[:, :]).then_inc(zh2[s], 1)
                        dve.wait_ge(zh2[s], it + 1)
                        nc.vector.tensor_tensor(Yl[s][:, :], ZZ[:, :], Yh[s][:, :].bitcast(F32), ALU.subtract).then_inc(lo2[s], 1)
                        dve.wait_ge(lo2[s], it * 2 + 2)
                    for s in range(SLOTS):
                        for c in range(NHC):
                            dve.wait_ge(hi2[s], it * 3 + 2 + c)
                            settle(dve)
                            for h in range(2):
                                ins = nc.vector.bn_stats(S1[:, c, (it * SLOTS + s) * 2 + h, :], hidden(c, it * SLOTS + s)[:, h * HALF:(h + 1) * HALF])
                        ins.then_inc(bs2[s], 1)

            @block.tensor
            def _(pe):
                with pe.Fori(0, PAIRS) as it:
                    for s in range(SLOTS):
                        def plus_self(bank, h, cs):
                            for t in range(4 * h, 4 * h + 4):
                                o = PS[:, bank + h, (t % 4) * P:(t % 4 + 1) * P]
                                nc.tensor.matmul(o, tiles(Yh[s])[:, t, :], identr[:, :], start=False, stop=False, skip_group_check=True)
                                mm = nc.tensor.matmul(o, tiles(Yl[s])[:, t, :], identr[:, :], start=False, stop=t % 4 == 3, skip_group_check=True)
                            return mm
                        pe.wait_ge(lo2[s], it * 2 + 1)
                        times_adj(4 * s, tiles(Yh[s]), tiles(Yl[s]), plus_self).then_inc(pe2[s], 1)
                    for s in range(SLOTS):
                        pe.wait_ge(lo2[s], it * 2 + 2)
                        for c in range(NHC):
                            for h in range(2):
                                hs = slice(h * HALF, (h + 1) * HALF)
                                mm = passes(PS[:, 4 * s + 2 - 2 * c + h, :], W1Th[:, c, :], W1Tl[:, c, :], Yh[s][:, hs], Yl[s][:, hs], True, True)
                            mm.then_inc(pe2[s], 1)
                    for s in range(SLOTS):
                        pe.wait_ge(hi2[s], it * 3 + 3)
        l2a.close()

        bn_dve, bn_pool = sem("bn_dve"), sem("bn_pool")

        def batch_norm_params(block, groups, base_dve, base_pool):
            @block.vector
            def _(dve):
                n = [base_dve]

                def done(ins):
                    n[0] += 1
                    ins.then_inc(bn_dve, 1)
                    dve.wait_ge(bn_dve, n[0])
                for r, stats, _, _ in groups:
                    done(nc.vector.bn_aggr(bnp[:, r, 0:2], stats))
                    done(nc.vector.tensor_scalar(bnp[:, r, 5:6], bnp[:, r, 1:2], BN_EPS, None, ALU.add))
                dve.wait_ge(bn_pool, base_pool + len(groups))
                for r, _, g, be in groups:
                    done(nc.vector.tensor_tensor(bnp[:, r, 3:4], bnp[:, r, 2:3], col(g), ALU.mult))
                    done(nc.vector.tensor_tensor(bnp[:, r, 4:5], bnp[:, r, 0:1], bnp[:, r, 3:4], ALU.mult))
                    done(nc.vector.tensor_tensor(bnp[:, r, 4:5], col(be), bnp[:, r, 4:5], ALU.subtract))

            @block.gpsimd
            def _(pool):
                for k, (r, _, _, _) in enumerate(groups):
                    pool.wait_ge(bn_dve, base_dve + 2 * k + 2)
                    nc.gpsimd.tensor_tensor(bnp[:, r, 2:3], bnp[:, r, 5:6], neg_half[:, 0:1], ALU.pow).then_inc(bn_pool, 1)

        def stats_of(t):
            return t.rearrange("p a b -> p (a b)")

        with nc.Block() as block:
            batch_norm_params(block, [(0, stats_of(S1[:, 0]), C_G1, C_BE1), (1, stats_of(S1[:, 1]), C_G1 + 1, C_BE1 + 1)], 0, 0)

        l2b = ExitStack()
        Rh = [sb(l2b, f"l2r_h{s}", [P, NHC, HALF], F32R) for s in range(SLOTS)]
        Rl = [sb(l2b, f"l2r_l{s}", [P, NHC, HALF], F32R) for s in range(SLOTS)]
        relu3, rh3, rl3, pe3, out3, bs3 = (sems(n) for n in ("l2b_relu", "l2b_rh", "l2b_rl", "l2b_pe", "l2b_out", "l2b_bs"))
        with nc.Block() as block:
            @block.scalar
            def _(act):
                with act.Fori(0, B) as b:
                    for s in range(SLOTS):
                        hs = slice(s * HALF, (s + 1) * HALF)
                        for c in range(NHC):
                            ins = nc.scalar.activation(hidden(c, b)[:, hs], hidden(c, b)[:, hs], ACT.Relu, bias=bnp[:, c, 4:5], scale=bnp[:, c, 3:4])
                            ins.then_inc(relu3[s], 1)
                    for s in range(SLOTS):
                        hs = slice(s * HALF, (s + 1) * HALF)
                        act.wait_ge(pe3[s], b + 1)
                        settle(act)
                        nc.scalar.activation(hidden(0, b)[:, hs], PS[:, s, :], ACT.Identity, bias=col(C_C2)).then_inc(out3[s], 1)

            @block.vector
            def _(dve):
                with dve.Fori(0, B) as b:
                    for s in range(SLOTS):
                        hs = slice(s * HALF, (s + 1) * HALF)
                        for c in range(NHC):
                            dve.wait_ge(relu3[s], b * 2 + c + 1)
                            nc.vector.tensor_copy(Rh[s][:, c, :], hidden(c, b)[:, hs]).then_inc(rh3[s], 1)
                            dve.wait_ge(rh3[s], b * 2 + c + 1)
                            nc.vector.tensor_tensor(Rl[s][:, c, :], hidden(c, b)[:, hs], Rh[s][:, c, :].bitcast(F32), ALU.subtract).then_inc(rl3[s], 1)
                    for s in range(SLOTS):
                        dve.wait_ge(out3[s], b + 1)
                        settle(dve)
                        nc.vector.bn_stats(S2[:, b * 2 + s, :], hidden(0, b)[:, s * HALF:(s + 1) * HALF]).then_inc(bs3[s], 1)

            @block.tensor
            def _(pe):
                with pe.Fori(0, B) as b:
                    for s in range(SLOTS):
                        for c in range(NHC):
                            pe.wait_ge(rl3[s], b * 2 + c + 1)
                            mm = passes(PS[:, s, :], W2Th[:, c, :], W2Tl[:, c, :], Rh[s][:, c, :], Rl[s][:, c, :], c == 0, c == NHC - 1)
                        mm.then_inc(pe3[s], 1)
                    for s in range(SLOTS):
                        pe.wait_ge(out3[s], b + 1)
        l2b.close()
        with nc.Block() as block:
            batch_norm_params(block, [(2, stats_of(S2[:, :, :]), C_G2, C_BE2)], 10, 2)
        l2.close()
        graph.close()

        l3 = ExitStack()
        PENT = sb(l3, "PENT", [P, NT, T], BF16)
        WH = sb(l3, "WH", [P, B, NT, D + 2])
        S2C = sb(l3, "S2C", [P, B, 2, NT])
        rows_dram = nc.dram_tensor("rows_dram", (B, 2 * NT, P), F32, kind="Internal").ap()
        prep = ExitStack()
        PENN = sb(prep, "PENN", [P, NT, T], BF16)
        nat = ExitStack()
        NAT2 = sb(nat, "NAT2", [P, NT, T])
        nat_in = [sem(f"nat_in{n}") for n in range(NT)]
        pn_ok, nt_ok, wh1_ok = sem("pn_ok"), sem("nt_ok"), sem("wh1_ok")
        with nc.Block() as block:
            @block.sync
            def _(sp):
                for n in range(NT):
                    sp.dma_start(NAT2[:, n, :], adj[n * P:(n + 1) * P, :]).then_inc(nat_in[n], 16)

            @block.gpsimd
            def _(pool):
                nc.gpsimd.memset(WH[:, :, :, D:D + 2], 1.0).then_inc(wh1_ok, 1)
                pool.wait_ge(wh1_ok, 1)

            @block.tensor
            def _(pe):
                for n in range(2 * NT):
                    st, h = n // 2, n % 2
                    for k in range(4):
                        if n < 2:
                            pe.wait_ge(nat_in[4 * h + k], 16)
                        if n >= 8 and k == 0:
                            pe.wait_ge(pn_ok, NT + n - 8 + 1)
                        mm = nc.tensor.transpose(PS[:, n % 8, k * P:(k + 1) * P], NAT2[:, 4 * h + k, st * P:(st + 1) * P], ident[:, :])
                    mm.then_inc(nt_ok, 1)

            @block.vector
            def _(dve):
                for n in range(NT):
                    dve.wait_ge(nat_in[n], 16)
                    nc.vector.tensor_scalar(PENN[:, n, :], NAT2[:, n, :], 0.0, BLOCKED, ALU.is_equal, ALU.mult).then_inc(pn_ok, 1)
                for n in range(2 * NT):
                    st, h = n // 2, n % 2
                    dve.wait_ge(nt_ok, n + 1)
                    nc.vector.tensor_scalar(PENT[:, st, h * HALF:(h + 1) * HALF], PS[:, n % 8, :], 0.0, BLOCKED, ALU.is_equal, ALU.mult).then_inc(pn_ok, 1)
        nat.close()

        Fh = [sb(prep, f"l3f_h{s}", [P, T], F32R) for s in range(SLOTS)]
        Fl = [sb(prep, f"l3f_l{s}", [P, T], F32R) for s in range(SLOTS)]
        XN = [sb(prep, f"l3x{s}", [P, NT, D]) for s in range(SLOTS)]
        Z = [sb(prep, f"l3z{s}", [P, T]) for s in range(SLOTS)]
        junk3 = sb(prep, "junk3", [P, T])
        SC = sb(prep, "SC", [P, SLOTS, NT, 2])
        MX = sb(prep, "MX", [P, SLOTS, NT])
        RR = sb(prep, "RR", [P, SLOTS, 2 * NT])
        RRT = sb(prep, "RRT", [2 * NT, SLOTS, P])
        pe4, act4, y4, lo4, mx4, rr4, sc4, st4, dm4 = (sems(n) for n in (
            "l3_pe", "l3_act", "l3_y", "l3_lo", "l3_mx", "l3_rr", "l3_sc", "l3_st", "l3_dma"))
        keep4 = sems("l3_keep")
        norm.stage(1)
        KA, KPE = 5, 6
        with nc.Block() as block:
            @block.scalar
            def _(act):
                with act.Fori(0, PAIRS) as it:
                    for s in range(SLOTS):
                        nc.scalar.activation(Z[s][:, :], HT[:, it * SLOTS + s, 0:T], ACT.Identity,
                                             bias=bnp[:, 2, 4:5], scale=bnp[:, 2, 3:4]).then_inc(act4[s], 1)
                    for s in range(SLOTS):
                        act.wait_ge(pe4[s], it * KPE + 2)
                        nc.scalar.activation(Fh[s][:, :], bank2(4 * s + 2), ACT.Copy).then_inc(act4[s], 1)
                        nc.scalar.activation(flat(X[:, it * SLOTS + s]), flat(XN[s][:, :, :]), ACT.Copy).then_inc(keep4[s], 1)
                    for s in range(SLOTS):
                        act.wait_ge(pe4[s], it * KPE + 3)
                        settle(act)
                        nc.scalar.activation(WH[:, it * SLOTS + s, :, 0:D], bank2(4 * s).rearrange("p (t d) -> p t d", t=NT), ACT.Copy).then_inc(act4[s], 1)
                    for s in range(SLOTS):
                        act.wait_ge(pe4[s], it * KPE + 5)
                        nc.scalar.activation(SC[:, s], PS[:, 4 * s, 0:2 * NT].rearrange("p (t k) -> p t k", k=2), ACT.Copy).then_inc(act4[s], 1)
                    for s in range(SLOTS):
                        act.wait_ge(pe4[s], it * KPE + 6)
                        nc.scalar.activation(RRT[:, s, :], PS[0:2 * NT, 4 * s, 0:P], ACT.Copy).then_inc(act4[s], 1)
                        act.wait_ge(act4[s], it * KA + KA)
                        act.dma_start(rows_dram[it * SLOTS + s], RRT[:, s, :]).then_inc(dm4[s], 16)
                        act.wait_ge(dm4[s], it * 16 + 16)

            @block.tensor
            def _(pe):
                with pe.Fori(0, PAIRS) as it:
                    for s in range(SLOTS):
                        pe.wait_ge(act4[s], it * KA + 1)
                        transposes(4 * s, [Z[s][:, t * P:(t + 1) * P] for t in range(NT)]).then_inc(pe4[s], 1)
                    for s in range(SLOTS):
                        pe.wait_ge(norm.done[s], norm.at(it, 1))
                        transposes(4 * s + 2, [XN[s][:, t, :] for t in range(NT)]).then_inc(pe4[s], 1)
                    for s in range(SLOTS):
                        pe.wait_ge(lo4[s], it + 1)
                        node_major(4 * s, Fh[s], Fl[s], W3h[:, 0:D], W3l[:, 0:D]).then_inc(pe4[s], 1)
                        for h in range(2):
                            hs = slice(h * HALF, (h + 1) * HALF)
                            mm = passes(PS[:, 4 * s + 2 + h, :], A2h[:, 1, :], A2l[:, 1, :], Fh[s][:, hs], Fl[s][:, hs], True, True)
                        mm.then_inc(pe4[s], 1)
                    for s in range(SLOTS):
                        pe.wait_ge(act4[s], it * KA + 3)
                        for t in range(NT):
                            ts = slice(t * P, (t + 1) * P)
                            mm = passes(PS[:, 4 * s, 2 * t:2 * t + 2], Fh[s][:, ts], Fl[s][:, ts], W3h[:, D:D + 2], W3l[:, D:D + 2], True, True)
                        mm.then_inc(pe4[s], 1)
                    for s in range(SLOTS):
                        pe.wait_ge(rr4[s], it * 4 + 4)
                        nc.tensor.transpose(PS[0:2 * NT, 4 * s, 0:P], RR[:, s, :], ident[:, :]).then_inc(pe4[s], 1)
                    for s in range(SLOTS):
                        pe.wait_ge(act4[s], it * KA + 5)

            @block.gpsimd
            def _(pool):
                with pool.Fori(0, PAIRS) as it:
                    for s in range(SLOTS):
                        norm.pool(pool, it, s, 1)

            @block.vector
            def _(dve):
                with dve.Fori(0, PAIRS) as it:
                    for s in range(SLOTS):
                        dve.wait_ge(pe4[s], it * KPE + 1)
                        nc.vector.tensor_tensor(flat(XN[s][:, :, :]), flat(X[:, it * SLOTS + s]), bank2(4 * s), ALU.add).then_inc(y4[s], 1)
                        dve.wait_ge(y4[s], it + 1)
                        norm.dve(dve, it, s, 1, XN[s])
                    for s in range(SLOTS):
                        norm.dve_scale(dve, it, s, 1, XN[s], XN[s])
                    for s in range(SLOTS):
                        dve.wait_ge(act4[s], it * KA + 2)
                        nc.vector.tensor_tensor(Fl[s][:, :], bank2(4 * s + 2), Fh[s][:, :].bitcast(F32), ALU.subtract).then_inc(lo4[s], 1)
                    for s in range(SLOTS):
                        dve.wait_ge(pe4[s], it * KPE + 4)
                        settle(dve)
                        for t in range(NT):
                            nc.vector.tensor_tensor_reduce(junk3[:, :], PENN[:, t, :], bank2(4 * s + 2), 1.0, 2 * BLOCKED,
                                                           ALU.add, ALU.max, MX[:, s, t:t + 1]).then_inc(mx4[s], 1)
                            dve.wait_ge(mx4[s], it * NT + t + 1)
                            settle(dve)
                    for s in range(SLOTS):
                        dve.wait_ge(act4[s], it * KA + 4)
                        s1, s2 = SC[:, s, :, 0], SC[:, s, :, 1]
                        nc.vector.tensor_copy(S2C[:, it * SLOTS + s, 0, :], s2).then_inc(sc4[s], 1)
                        nc.vector.tensor_scalar(S2C[:, it * SLOTS + s, 1, :], s2, ALPHA, None, ALU.mult).then_inc(sc4[s], 1)
                        nc.vector.tensor_tensor(MX[:, s, :], MX[:, s, :], s1, ALU.add).then_inc(rr4[s], 1)
                        dve.wait_ge(rr4[s], it * 4 + 1)
                        nc.vector.scalar_tensor_tensor(out=MX[:, s, :], in0=MX[:, s, :], scalar=ALPHA, in1=MX[:, s, :],
                                                       op0=ALU.mult, op1=ALU.max).then_inc(rr4[s], 1)
                        dve.wait_ge(rr4[s], it * 4 + 2)
                        nc.vector.tensor_tensor(RR[:, s, 0:NT], s1, MX[:, s, :], ALU.subtract).then_inc(rr4[s], 1)
                        nc.vector.scalar_tensor_tensor(out=RR[:, s, NT:2 * NT], in0=s1, scalar=ALPHA, in1=MX[:, s, :],
                                                       op0=ALU.mult, op1=ALU.subtract).then_inc(rr4[s], 1)
                        dve.wait_ge(rr4[s], it * 4 + 4)
                        dve.wait_ge(keep4[s], it + 1)
        prep.close()

        RB = [sb(l3, f"rb{s}", [P, 2 * T]) for s in range(SLOTS)]
        NV, NE, NTT = 3, 3, 2
        TT = [sb(l3, f"tt{k}", [P, T]) for k in range(NTT)]
        V = [sb(l3, f"v{k}", [P, T]) for k in range(NV)]
        E = [sb(l3, f"e{k}", [P, T]) for k in range(NE)]
        REC = sb(l3, "REC", [P, NT])
        rb_in = sems("rb_in")
        tt5, v5, vm5, e5, pe5, att5, rec5, y5, out5, attn = (sem(n) for n in (
            "l3t", "l3v", "l3vm", "l3e", "l3att_pe", "l3_att", "l3_rec", "l3_yy", "l3_out", "l3_n"))
        norm.stage(1)
        PB = SLOTS * NT

        def att(t):
            return PS[:, t // 3, (t % 3) * (D + 1):(t % 3 + 1) * (D + 1)]

        with nc.Block() as block:
            @block.sync
            def _(sp):
                def rows_of(b):
                    return rows_dram[b].rearrange("(o t) p -> o (t p)", o=1).broadcast_to([P, 2 * T])
                for s in range(SLOTS):
                    sp.dma_start(RB[s][:, :], rows_of(s)).then_inc(rb_in[s], 16)
                with sp.Fori(1, PAIRS) as it:
                    for s in range(SLOTS):
                        sp.wait_ge(v5, it * PB - PB + (s + 1) * NT)
                        sp.dma_start(RB[s][:, :], rows_of(it * SLOTS + s)).then_inc(rb_in[s], 16)
                        sp.wait_ge(norm.done[s], norm.at(it, 0))
                        sp.dma_start(out[(it - 1) * SLOTS + s].rearrange("(t p) d -> p t d", p=P), X[:, (it - 1) * SLOTS + s]).then_inc(out5, 16)
                for s in range(SLOTS):
                    sp.wait_ge(norm.done[s], norm.at(PAIRS, 0))
                    b = B - SLOTS + s
                    sp.dma_start(out[b].rearrange("(t p) d -> p t d", p=P), X[:, b]).then_inc(out5, 16)
                sp.wait_ge(out5, 16 * B)

            @block.scalar
            def _(act):
                nc.scalar.preload_act_table(ACT.Exp)

                def shifted(it, q):
                    s, jt = q // NT, q % NT
                    if jt == 0:
                        act.wait_ge(rb_in[s], it * 16 + 16)
                    settle(act)
                    nc.scalar.activation(TT[q % NTT][:, :], RB[s][:, T:2 * T], ACT.Identity,
                                         bias=S2C[:, it * SLOTS + s, 1, jt:jt + 1]).then_inc(tt5, 1)

                def exps(it, q):
                    act.wait_ge(vm5, it * PB + q + 1)
                    nc.scalar.activation(E[q % 4 if NE == 4 else q % NE][:, :], V[q % NV][:, :], ACT.Exp).then_inc(e5, 1)

                with act.Fori(0, PAIRS) as it:
                    for q in range(PB):
                        if q >= NTT:
                            act.wait_ge(v5, it * PB + q - NTT + 1)
                        shifted(it, q)
                        if q >= 2:
                            if q - 2 >= NE:
                                act.wait_ge(pe5, it * PB + q - 2 - NE + 1)
                            exps(it, q - 2)
                    for q in range(PB - 2, PB):
                        act.wait_ge(pe5, it * PB + q - NE + 1)
                        exps(it, q)
                    act.wait_ge(pe5, it * PB + PB)

            @block.gpsimd
            def _(pool):
                with pool.Fori(0, PAIRS) as it:
                    for s in range(SLOTS):
                        for jt in range(NT):
                            q = s * NT + jt
                            pool.wait_ge(v5, it * PB + q + 1)
                            nc.gpsimd.tensor_tensor(V[q % NV][:, :], V[q % NV][:, :], PENT[:, jt, :], ALU.add).then_inc(vm5, 1)
                        norm.pool(pool, it, s, 1)

            @block.vector
            def _(dve):
                with dve.Fori(0, PAIRS) as it:
                    for s in range(SLOTS):
                        for jt in range(NT):
                            q = s * NT + jt
                            if q >= NV:
                                dve.wait_ge(e5, it * PB + q - NV + 1)
                            dve.wait_ge(tt5, it * PB + q + 1)
                            nc.vector.scalar_tensor_tensor(out=V[q % NV][:, :], in0=RB[s][:, 0:T], scalar=S2C[:, it * SLOTS + s, 0, jt:jt + 1],
                                                           in1=TT[q % NTT][:, :], op0=ALU.add, op1=ALU.max).then_inc(v5, 1)
                        dve.wait_ge(pe5, it * PB + (s + 1) * NT)
                        for t in range(NT):
                            ins = nc.vector.reciprocal(REC[:, t:t + 1], att(t)[:, D:D + 1])
                        ins.then_inc(rec5, 1)
                        dve.wait_ge(rec5, it * SLOTS + s + 1)
                        rows = X[:, it * SLOTS + s]
                        for t in range(NT):
                            ins = nc.vector.scalar_tensor_tensor(out=rows[:, t, :], in0=att(t)[:, 0:D], scalar=REC[:, t:t + 1], in1=rows[:, t, :],
                                                                 op0=ALU.mult, op1=ALU.add)
                        ins.then_inc(y5, 1)
                        dve.wait_ge(y5, it * SLOTS + s + 1)
                        settle(dve)
                        norm.dve(dve, it, s, 1, rows)
                        norm.dve_scale(dve, it, s, 1, rows, rows)
                    dve.wait_ge(e5, it * PB + PB)

            @block.tensor
            def _(pe):
                with pe.Fori(0, PAIRS) as it:
                    for q in range(PB):
                        s, jt = q // NT, q % NT
                        pe.wait_ge(e5, it * PB + q + 1)
                        if q == NT:
                            pe.wait_ge(y5, it * SLOTS + 1)
                        for t in range(NT):
                            mm = nc.tensor.matmul(att(t), E[q % NE][:, t * P:(t + 1) * P], WH[:, it * SLOTS + s, jt, 0:D + 1],
                                                  start=(jt == 0 and t % 3 == 0), stop=(jt == NT - 1), skip_group_check=True)
                        mm.then_inc(pe5, 1)
                    pe.wait_ge(y5, it * SLOTS + 2)
        l3.close()



_INS = ["x", "adj", "L0_gnn_Wg0", "L0_gnn_bg0", "L0_gnn_Wg1", "L0_gnn_bg1", "L0_gnn_Wih", "L0_gnn_Whh", "L0_gnn_bih",
        "L0_gnn_bhh", "L1_gnn_w1_loop", "L1_gnn_w1_neigh", "L1_gnn_b1", "L1_gnn_w2_loop", "L1_gnn_w2_neigh",
        "L1_gnn_b2", "L2_gnn_W1", "L2_gnn_b1", "L2_gnn_g1", "L2_gnn_be1", "L2_gnn_W2", "L2_gnn_b2", "L2_gnn_g2",
        "L2_gnn_be2", "L3_gnn_W", "L3_gnn_a"]


def kernel(**inputs):
    import numpy as _np
    import concourse.bacc as _bacc
    from concourse import mybir as _mybir
    from concourse.bass_utils import run_bass_kernel_spmd as _run

    nc = _bacc.Bacc("TRN2", target_bir_lowering=False, num_devices=1)
    arrays, args = {}, []
    for name in _INS:
        a = _np.ascontiguousarray(inputs[name])
        arrays[f"in_{name}_dram"] = a
        args.append(nc.dram_tensor(f"in_{name}_dram", a.shape, _mybir.dt.from_np(a.dtype), kind="ExternalInput").ap())
    args.append(nc.dram_tensor("out_0_dram", (B, T, D), F32, kind="ExternalOutput").ap())
    program(nc, *args)
    r = _run(nc, [arrays], core_ids=[0])
    return r.results[0]["out_0_dram"]
```

```python
from contextlib import ExitStack

import concourse.bass as bass
from concourse import mybir

P = 128
B, T, D = 8, 1024, 128
NT = T // P
HALF = 512
SKIPS = 4
GATE_I, GATE_F, GATE_G, GATE_O = range(4)
HID = 256
NHC = HID // P
LN_EPS = 1e-5
BN_EPS = 1e-5
ALPHA = 0.2
BLOCKED = -1e30
TPAD = T + 2

F32 = mybir.dt.float32
F32R = mybir.dt.float32r
BF16 = mybir.dt.bfloat16
ALU = mybir.AluOpType
ACT = mybir.ActivationFunctionType
AX_X = mybir.AxisListType.X


def program(nc, x, adj, Wg0, bg0, Wg1, bg1, Wih, Whh, bih, bhh,
            w1_loop, w1_neigh, b1, w2_loop, w2_neigh, b2,
            W1, c1, g1, be1, W2, c2, g2, be2, W3, a3, out):
    root = ExitStack()

    def sb(ctx, name, shape, dt=F32):
        return ctx.enter_context(nc.sbuf_tensor(name, shape, dt))

    def sbr(ctx, name, shape, dt=F32):
        return ctx.enter_context(nc.sbuf_tensor(name, shape, dt, side="right"))

    def sem(name):
        return root.enter_context(nc.semaphore(name))

    with root:
        PS = root.enter_context(nc.psum_tensor("PS", [P, 8, HALF], F32))
        ident = sb(root, "ident", [P, P])
        identr = sb(root, "identr", [P, P], F32R)
        neg_half = sb(root, "neg_half", [P, NT])
        MATS = 6
        Mh = sb(root, "Mh", [P, MATS, D], F32R)
        Ml = sb(root, "Ml", [P, MATS, D], F32R)
        W1Th = sb(root, "W1Th", [P, NHC, P], F32R)
        W1Tl = sb(root, "W1Tl", [P, NHC, P], F32R)
        W2Th = sb(root, "W2Th", [P, NHC, P], F32R)
        W2Tl = sb(root, "W2Tl", [P, NHC, P], F32R)
        W3h = sb(root, "W3h", [P, D + 2], F32R)
        W3l = sb(root, "W3l", [P, D + 2], F32R)
        A2h = sb(root, "A2h", [P, 2, P], F32R)
        A2l = sb(root, "A2l", [P, 2, P], F32R)
        cols = sb(root, "cols", [P, 32])
        dinv = sb(root, "dinv", [P, NT])
        MV = sb(root, "MV", [P, 2, NT, 2])
        ST = sb(root, "ST", [P, 2, NT, 6])
        RSTD = sb(root, "RSTD", [P, 2, NT])
        NM = sb(root, "NM", [P, 2, NT])
        SHIFT = sb(root, "SHIFT", [P, 2, NT])
        VE = sb(root, "VE", [P, 2, NT])
        S1 = sb(root, "S1", [P, NHC, 2 * B, 6])
        S2 = sb(root, "S2", [P, 2 * B, 6])
        bnp = sb(root, "bnp", [P, 3, 6])
        C_B1, C_B2, C_C1, C_G1, C_BE1, C_C2, C_G2, C_BE2 = 0, 1, 2, 4, 6, 8, 9, 10
        C_LSTM = 11
        NROWS = 11

        def col(n):
            return cols[:, n:n + 1]

        def bank2(n):
            return PS[:, n:n + 2, :].rearrange("p a b -> p (a b)")

        passed = sem("passed")

        def settle(eng):
            eng.sem_inc(passed, 1)

        def passes(out_ap, lh, ll, rh, rl, start, stop):
            nc.tensor.matmul(out_ap, lh, rh, start=start, stop=False, skip_group_check=True)
            nc.tensor.matmul(out_ap, lh, rl, start=False, stop=False, skip_group_check=True)
            return nc.tensor.matmul(out_ap, ll, rh, start=False, stop=stop, skip_group_check=True)

        def adj_half(bank, lh, ll, h, stop=True, sources=range(NT)):
            cs = slice(h * HALF, (h + 1) * HALF)
            for st in sources:
                mm = passes(PS[:, bank + h, :], lh[:, st, :], ll[:, st, :], ATh[:, st, cs], ATl[:, st, cs],
                            st == 0, stop and st == NT - 1)
            return mm

        def times_adj(bank, lh, ll, last_terms=None):
            for h in range(2):
                cs = slice(h * HALF, (h + 1) * HALF)
                for st in range(NT):
                    mm = passes(PS[:, bank + h, :], lh[:, st, :], ll[:, st, :], ATh[:, st, cs], ATl[:, st, cs],
                                st == 0, st == NT - 1 and last_terms is None)
                if last_terms is not None:
                    mm = last_terms(bank, h, cs)
            return mm

        def node_major(bank, lh, ll, wh, wl, first=True):
            for st in range(NT):
                o = PS[:, bank + st // 4, (st % 4) * P:(st % 4 + 1) * P]
                mm = passes(o, lh[:, st * P:(st + 1) * P], ll[:, st * P:(st + 1) * P], wh, wl, first, True)
            return mm

        def transposes(bank, blocks):
            for n, block_ap in enumerate(blocks):
                mm = nc.tensor.transpose(PS[:, bank + n // 4, (n % 4) * P:(n % 4 + 1) * P], block_ap, ident[:, :])
            return mm

        dinv_row = sb(root, "dinv_row", [P, T])
        graph = ExitStack()
        ATh = sb(graph, "ATh", [P, NT, T], F32R)
        ATl = sb(graph, "ATl", [P, NT, T], F32R)
        lstm = ExitStack()
        WIh = sb(lstm, "WIh", [P, SKIPS, 4, P], F32R)
        WIl = sb(lstm, "WIl", [P, SKIPS, 4, P], F32R)
        WHh = sb(lstm, "WHh", [P, SKIPS - 1, 4, P], F32R)
        WHl = sb(lstm, "WHl", [P, SKIPS - 1, 4, P], F32R)
        s0 = ExitStack()
        B0 = sb(s0, "B0", [P, T])
        bg1r = sb(s0, "bg1r", [P, HALF], F32R)
        onesr = sb(s0, "onesr", [P, P], F32R)
        s1 = ExitStack()
        NAT = sb(s1, "NAT", [P, NT, T])
        ones = sb(s1, "ones", [P, P])
        STG = sb(s1, "STG", [P, 7, D])
        W1s = sb(s1, "W1s", [P, NHC, P])
        W2s = sb(s1, "W2s", [P, HID])
        a_rows = sb(s1, "a_rows", [P, 2, P])
        wa = sb(s1, "wa", [P, 2])
        bg0_rows = sb(s1, "bg0_rows", [P, D])
        bg0h = sb(s1, "bg0h", [P, D], F32R)
        bg0l = sb(s1, "bg0l", [P, D], F32R)
        bg1s = sb(s1, "bg1s", [1, D])
        bg1hs = sb(s1, "bg1hs", [1, D], F32R)
        bg1lo = sb(s1, "bg1lo", [1, HALF], F32R)
        bg1t = sb(s1, "bg1t", [1, D])
        vecs = sb(s1, "vecs", [16, P])
        lb = sb(s1, "lb", [16, P])
        lb2 = sb(s1, "lb2", [16, P])
        junk = sb(s1, "junk", [P, P])
        rsum = sb(s1, "rsum", [P, NT])
        csum = sb(s1, "csum", [P, NT, 2])
        dsum = sb(s1, "dsum", [P, NT])
        deg = sb(s1, "deg", [P, NT])
        diag = sb(s1, "diag", [P, NT, P])
        WIs = sb(s1, "WIs", [P, SKIPS * 4, P])
        WHs = sb(s1, "WHs", [P, (SKIPS - 1) * 4, P])
        NI, NH = SKIPS, SKIPS - 1
        lw_t, lw_hi, lw_lo = (sem(n) for n in ("lw_t", "lw_hi", "lw_lo"))

        adj_in = [sem(f"adj_in{n}") for n in range(NT)]
        mats_in, vec_in, lw_in, konst, dve0, act0, pe0, pool0, moved, diagonals = (
            sem(n) for n in ("mats_in", "vec_in", "lw_in", "konst", "dve0", "act0", "pe0", "pool0", "moved", "diagonals"))

        def row(v):
            return v.rearrange("(a n) -> a n", a=1)

        with nc.Block() as block:
            @block.sync
            def _(sp):
                for n in range(NT):
                    sp.dma_start(NAT[:, n, :], adj[n * P:(n + 1) * P, :]).then_inc(adj_in[n], 16)
                sp.dma_start(WIs[:, :, :], Wih.rearrange("s (g p) d -> p (s g) d", p=P)).then_inc(lw_in, 16)
                sp.dma_start(WHs[:, :, :], Whh[1:SKIPS].rearrange("s (g p) d -> p (s g) d", p=P)).then_inc(lw_in, 16)
                sp.wait_ge(dve0, 3)
                sp.wait_ge(konst, 7)
                sp.dma_start(bg1r[1:2, :].bitcast(F32), bg1lo[:, :].bitcast(F32)).then_inc(moved, 16)
                sp.wait_ge(moved, 16)

            @block.scalar
            def _(act):
                for n, w in enumerate((Wg0, Wg1, w1_loop, w1_neigh, w2_loop, w2_neigh, W3)):
                    act.dma_start(STG[:, n, :], w).then_inc(mats_in, 16)
                act.dma_start(W1s[:, :, :], W1.rearrange("(c p) d -> p c d", p=P)).then_inc(mats_in, 16)
                act.dma_start(W2s[:, :], W2).then_inc(mats_in, 16)
                act.dma_start(bg0_rows[:, :], row(bg0).broadcast_to([P, D])).then_inc(mats_in, 16)
                for n in range(2):
                    act.dma_start(a_rows[:, n, :], a3[n * P:(n + 1) * P, :].rearrange("o u -> u o").broadcast_to([P, P])).then_inc(mats_in, 16)
                act.dma_start(bg1s[:, :], row(bg1)).then_inc(mats_in, 16)
                n = 0
                for v in (b1, b2, c1, g1, be1, c2, g2, be2):
                    k = v.shape[0] // P
                    act.dma_start(vecs[n:n + k, :], v.rearrange("(k p) -> k p", p=P)).then_inc(vec_in, 16)
                    n += k
                act.dma_start(lb[:, :], bih.rearrange("s (g p) -> (s g) p", p=P)).then_inc(vec_in, 16)
                act.dma_start(lb2[:, :], bhh.rearrange("s (g p) -> (s g) p", p=P)).then_inc(vec_in, 16)
                for n in range(NI + NH):
                    act.wait_ge(lw_t, n + 1)
                    hi = WIh[:, n] if n < NI else WHh[:, n - NI]
                    nc.scalar.activation(hi.rearrange("p g o -> p (g o)"), PS[:, n, :], ACT.Copy).then_inc(lw_hi, 1)
                for n in range(2 * NT):
                    act.wait_ge(pe0, n + 1)
                    st, h = n // 2, n % 2
                    nc.scalar.activation(ATh[:, st, h * HALF:(h + 1) * HALF], PS[:, n % 8, :], ACT.Copy).then_inc(act0, 1)

            @block.gpsimd
            def _(pool):
                nc.gpsimd.memset(ident[:, :], 0.0).then_inc(konst, 1)
                nc.gpsimd.memset(ones[:, :], 1.0).then_inc(konst, 1)
                nc.gpsimd.memset(neg_half[:, :], -0.5).then_inc(konst, 1)
                nc.gpsimd.memset(bg1r[:, :].bitcast(F32), 0.0).then_inc(konst, 1)
                pool.wait_ge(konst, 4)
                nc.gpsimd.affine_select(out=ident[:, :], in_=ident[:, :], compare_op=ALU.not_equal, fill=1.0,
                                        base=0, pattern=[[-1, P]], channel_multiplier=1).then_inc(konst, 1)
                pool.wait_ge(konst, 5)
                nc.gpsimd.tensor_copy(identr[:, :], ident[:, :]).then_inc(konst, 1)
                nc.gpsimd.tensor_copy(onesr[:, :], ones[:, :]).then_inc(konst, 1)
                pool.wait_ge(pool0, 1)
                nc.gpsimd.tensor_tensor(dinv[:, :], deg[:, :], neg_half[:, :], ALU.pow).then_inc(pool0, 1)

            @block.vector
            def _(dve):
                count = [0]

                def done(ins):
                    count[0] += 1
                    ins.then_inc(dve0, 1)
                    dve.wait_ge(dve0, count[0])

                dve.wait_ge(mats_in, 16 * 13)
                dve.wait_ge(vec_in, 16 * 10)
                dve.wait_ge(konst, 7)
                V4 = bg1r[0:1, :].rearrange("p (r d) -> p r d", r=4)
                bg1w = bg1s[:, :].rearrange("p (r d) -> p r d", r=1).broadcast_to([1, 4, D])
                done(nc.vector.tensor_copy(bg1hs[:, :], bg1s[:, :]))
                done(nc.vector.tensor_copy(V4, bg1w))
                done(nc.vector.tensor_tensor(bg1lo[:, :].rearrange("p (r d) -> p r d", r=4), bg1w,
                                             V4.bitcast(F32), ALU.subtract))
                done(nc.vector.tensor_tensor(lb[:, :], lb[:, :], lb2[:, :], ALU.add))
                done(nc.vector.tensor_copy(Mh[:, :, :], STG[:, 0:MATS, :]))
                done(nc.vector.tensor_tensor(Ml[:, :, :], STG[:, 0:MATS, :], Mh[:, :, :].bitcast(F32), ALU.subtract))
                done(nc.vector.tensor_copy(bg0h[:, :], bg0_rows[:, :]))
                done(nc.vector.tensor_tensor(bg0l[:, :], bg0_rows[:, :], bg0h[:, :].bitcast(F32), ALU.subtract))
                for n in range(2):
                    done(nc.vector.tensor_tensor_reduce(junk[:, :], STG[:, 6, :], a_rows[:, n, :], 1.0, 0.0,
                                                        ALU.mult, ALU.add, wa[:, n:n + 1]))
                done(nc.vector.tensor_copy(W3h[:, 0:D], STG[:, 6, :]))
                done(nc.vector.tensor_copy(W3h[:, D:D + 2], wa[:, :]))
                done(nc.vector.tensor_tensor(W3l[:, 0:D], STG[:, 6, :], W3h[:, 0:D].bitcast(F32), ALU.subtract))
                done(nc.vector.tensor_tensor(W3l[:, D:D + 2], wa[:, :], W3h[:, D:D + 2].bitcast(F32), ALU.subtract))
                for n in range(2):
                    done(nc.vector.tensor_scalar(A2h[:, n, :], ones[:, :], W3h[:, D + n:D + n + 1].bitcast(F32), None, ALU.mult))
                    done(nc.vector.tensor_scalar(A2l[:, n, :], ones[:, :], W3l[:, D + n:D + n + 1].bitcast(F32), None, ALU.mult))
                for n in range(NI + NH):
                    dve.wait_ge(lw_hi, n + 1)
                    hi, lo = (WIh[:, n], WIl[:, n]) if n < NI else (WHh[:, n - NI], WHl[:, n - NI])
                    nc.vector.tensor_tensor(lo.rearrange("p g o -> p (g o)"), PS[:, n, :],
                                            hi.rearrange("p g o -> p (g o)").bitcast(F32), ALU.subtract).then_inc(lw_lo, 1)
                for n in range(2 * NT):
                    dve.wait_ge(act0, n + 1)
                    st, h = n // 2, n % 2
                    hs = slice(h * HALF, (h + 1) * HALF)
                    nc.vector.tensor_tensor(ATl[:, st, hs], PS[:, n % 8, :], ATh[:, st, hs].bitcast(F32), ALU.subtract).then_inc(dve0, 1)
                    nc.vector.tensor_reduce(csum[:, st, h:h + 1], PS[:, n % 8, :], AX_X, ALU.add).then_inc(dve0, 1)
                count[0] += 4 * NT
                for n in range(NT):
                    nc.vector.tensor_reduce(rsum[:, n:n + 1], NAT[:, n, :], AX_X, ALU.add).then_inc(dve0, 1)
                    count[0] += 1
                    done(nc.vector.tensor_tensor_reduce(junk[:, :], NAT[:, n, n * P:(n + 1) * P], ident[:, :], 1.0, 0.0,
                                                        ALU.mult, ALU.add, dsum[:, n:n + 1]))
                dve.wait_ge(dve0, count[0])
                done(nc.vector.tensor_tensor(deg[:, :], rsum[:, :], csum[:, :, 0], ALU.add))
                done(nc.vector.tensor_tensor(deg[:, :], deg[:, :], csum[:, :, 1], ALU.add))
                done(nc.vector.scalar_tensor_tensor(out=deg[:, :], in0=deg[:, :], scalar=1.0, in1=dsum[:, :],
                                                    op0=ALU.add, op1=ALU.subtract))
                nc.vector.tensor_copy(junk[:, 0:NT], deg[:, :]).then_inc(pool0, 1)
                dve.wait_ge(pe0, 2 * NT + 1)
                sq = PS[:, 0, :].rearrange("p (c d) -> p c d", c=4)
                done(nc.vector.tensor_copy(W1Th[:, :, :], sq[:, 0:2, :]))
                done(nc.vector.tensor_tensor(W1Tl[:, :, :], sq[:, 0:2, :], W1Th[:, :, :].bitcast(F32), ALU.subtract))
                done(nc.vector.tensor_copy(W2Th[:, :, :], sq[:, 2:4, :]))
                done(nc.vector.tensor_tensor(W2Tl[:, :, :], sq[:, 2:4, :], W2Th[:, :, :].bitcast(F32), ALU.subtract))
                done(nc.vector.tensor_copy(cols[:, 0:NROWS], PS[:, 1, 0:NROWS]))
                done(nc.vector.tensor_copy(cols[:, C_LSTM:C_LSTM + 16], PS[:, 1, 16:32]))
                done(nc.vector.tensor_scalar(col(C_B2), col(C_B2), 0.5, None, ALU.mult))
                dve.wait_ge(pe0, 2 * NT + 2)
                done(nc.vector.tensor_copy(B0[:, :], bank2(2)))
                dve.wait_ge(pool0, 2)
                for n in range(NT):
                    nc.vector.tensor_scalar(diag[:, n, :], ident[:, :], dinv[:, n:n + 1], None, ALU.mult).then_inc(diagonals, 1)
                dve.wait_ge(pe0, 2 * NT + 3)
                nc.vector.tensor_copy(dinv_row[:, :], bank2(4)).then_inc(dve0, 1)

            @block.tensor
            def _(pe):
                pe.wait_ge(konst, 7)
                pe.wait_ge(lw_in, 32)
                for n in range(NI + NH):
                    for k in range(4):
                        src = WIs[:, 4 * n + k, :] if n < NI else WHs[:, 4 * (n - NI) + k, :]
                        mm = nc.tensor.transpose(PS[:, n, k * P:(k + 1) * P], src, ident[:, :])
                    mm.then_inc(lw_t, 1)
                for n in range(NT):
                    pe.wait_ge(adj_in[n], 16)
                for n in range(2 * NT):
                    st, h = n // 2, n % 2
                    if n < NI + NH:
                        pe.wait_ge(lw_lo, n + 1)
                    if n >= 8:
                        pe.wait_ge(dve0, 18 + 2 * (n - 8) + 2)
                    for k in range(4):
                        mm = nc.tensor.transpose(PS[:, n % 8, k * P:(k + 1) * P],
                                                 NAT[:, 4 * h + k, st * P:(st + 1) * P], ident[:, :])
                    mm.then_inc(pe0, 1)
                pe.wait_ge(dve0, 18 + 4 * NT)
                for c in range(NHC):
                    nc.tensor.transpose(PS[:, 0, c * P:(c + 1) * P], W1s[:, c, :], ident[:, :])
                    nc.tensor.transpose(PS[:, 0, (2 + c) * P:(3 + c) * P], W2s[:, c * P:(c + 1) * P], ident[:, :])
                nc.tensor.transpose(PS[:, 1, 0:NROWS], vecs[0:NROWS, :], ident[0:NROWS, 0:NROWS])
                nc.tensor.transpose(PS[:, 1, 16:32], lb[:, :], ident[0:16, 0:16]).then_inc(pe0, 1)
                for h in range(2):
                    hs = slice(h * HALF, (h + 1) * HALF)
                    for st in range(NT):
                        mm = passes(PS[:, 2 + h, :], bg0h[:, :], bg0l[:, :], ATh[:, st, hs], ATl[:, st, hs], st == 0, st == NT - 1)
                mm.then_inc(pe0, 1)
                pe.wait_ge(diagonals, NT)
                for h in range(2):
                    mm = nc.tensor.matmul(PS[:, 4 + h, :], ones[:, :], diag[:, 4 * h:4 * h + 4, :], start=True, stop=True)
                mm.then_inc(pe0, 1)
        s1.close()

        class Signal:

            def __init__(self, name, n, unit=1, credit=0):
                self.sem, self.n, self.unit, self.credit = sem(name), n, unit, credit

            def reach(self, eng, b, k):
                i, plus, mul = b if len(b) == 3 else (*b, 1)
                eng.wait_ge(self.sem, i * (mul * self.n * self.unit) + ((plus * self.n + k) * self.unit + self.credit))

        class Norm:

            def __init__(self, name, n, slot):
                self.n, self.slot = n, slot
                self.stats, self.var, self.eps, self.rstd, self.shift = (
                    Signal(f"{name}_{k}", n) for k in ("stats", "var", "eps", "rstd", "shift"))
                self.finished = [Signal(f"{name}_finished{k}", 1) for k in range(n)]

            def done(self, eng, b, k):
                self.finished[k - 1].reach(eng, b, 1)

            def dve_stats(self, dve, b, k, rows):
                s = self.slot + k - 1
                settle(dve)
                for t in range(NT):
                    ins = nc.vector.bn_stats(ST[:, s, t, :], rows[:, t, :])
                ins.then_inc(self.stats.sem, 1)
                self.stats.reach(dve, b, k)
                settle(dve)
                for t in range(NT):
                    ins = nc.vector.bn_aggr(MV[:, s, t, :], ST[:, s, t, :])
                ins.then_inc(self.var.sem, 1)

            def scale(self, eng, engine, b, k, rows, to):
                s = self.slot + k - 1
                self.rstd.reach(eng, b, k)
                if engine is nc.gpsimd:
                    settle(eng)
                for t in range(NT):
                    ins = engine.tensor_scalar(to[:, t, :], rows[:, t, :], MV[:, s, t, 0:1], RSTD[:, s, t:t + 1],
                                               ALU.subtract, ALU.mult)
                ins.then_inc(self.finished[k - 1].sem, 1)

            def act_scale(self, act, b, k, rows, to, signal, half):
                s = self.slot + k - 1
                if half == 0:
                    self.shift.reach(act, b, k)
                for t in range(half * NT // 2, (half + 1) * NT // 2):
                    ins = nc.scalar.activation(to[:, t, :], rows[:, t, :], ACT.Identity,
                                               bias=SHIFT[:, s, t:t + 1], scale=RSTD[:, s, t:t + 1])
                ins.then_inc(signal, 1)

            def pool(self, pool, b, k, shifts=False):
                s = self.slot + k - 1
                self.var.reach(pool, b, k)
                settle(pool)
                if shifts:
                    nc.gpsimd.tensor_scalar(NM[:, s, :], MV[:, s, :, 0], -1.0, None, ALU.mult)
                nc.gpsimd.tensor_scalar(VE[:, s, :], MV[:, s, :, 1], LN_EPS, None, ALU.add).then_inc(self.eps.sem, 1)
                self.eps.reach(pool, b, k)
                nc.gpsimd.tensor_tensor(RSTD[:, s, :], VE[:, s, :], neg_half[:, :], ALU.pow).then_inc(self.rstd.sem, 1)
                if shifts:
                    self.rstd.reach(pool, b, k)
                    nc.gpsimd.tensor_tensor(SHIFT[:, s, :], NM[:, s, :], RSTD[:, s, :], ALU.mult).then_inc(self.shift.sem, 1)

        def flat(t):
            return t.rearrange("p a b -> p (a b)")

        def tiles(t):
            return t[:, :].rearrange("p (t d) -> p t d", t=NT)

        x1_dram = nc.dram_tensor("x1_dram", (B, P, NT * D), F32, kind="Internal").ap()
        fused = ExitStack()
        XL = sb(fused, "XL", [P, NT, D])
        N0h, N0l = (sb(fused, n, [P, NT, D], F32R) for n in ("N0h", "N0l"))
        F0h, F0l = (sb(fused, n, [P, T], F32R) for n in ("F0h", "F0l"))
        Z0 = sb(fused, "Z0", [P, T])
        HN = sb(fused, "HN", [P, TPAD])
        XN = sb(fused, "XN", [P, NT, D])
        N1h, N1l = (sb(fused, n, [P, NT, D], F32R) for n in ("N1h", "N1l"))
        F1h, F1l = (sb(fused, n, [P, T], F32R) for n in ("F1h", "F1l"))
        Z1 = sb(fused, "Z1", [P, T])
        HT = sb(fused, "HT", [P, TPAD])
        XSh, XSl = (sb(fused, n, [P, TPAD], F32R) for n in ("XSh", "XSl"))
        HRh, HRl = (sb(fused, n, [P, HALF], F32R) for n in ("HRh", "HRl"))
        gates = [sb(fused, f"gate{k}", [P, HALF]) for k in range(4)]
        C, IG, TC, HS = (sb(fused, n, [P, HALF]) for n in ("C", "IG", "TC", "HS"))
        PT, PL = 4, 6

        UNITS = [(1, 0, 0, HALF), (1, 0, HALF, HALF)]
        UNITS += [(p, k, 0, n) for p, n in ((2, T // 2), (3, TPAD // 3), (4, T // 4)) for k in range(p)]
        NU = len(UNITS)

        def gates_of(k):
            return (GATE_I, GATE_G, GATE_F, GATE_O) if k else (GATE_I, GATE_G, GATE_O)

        NGATES = sum(len(gates_of(k)) for _, k, _, _ in UNITS)
        NSTATES = sum(k < p - 1 for p, k, _, _ in UNITS)
        NSUMS = sum(k > 0 for _, k, _, _ in UNITS)
        GATES_BEFORE = [sum(len(gates_of(k)) for _, k, _, _ in UNITS[:u]) for u in range(NU + 1)]
        STATES_BEFORE = [sum(k < p - 1 for p, k, _, _ in UNITS[:u]) for u in range(NU + 1)]
        SUMS_BEFORE = [sum(k > 0 for _, k, _, _ in UNITS[:u]) for u in range(NU + 1)]

        xl_in = Signal("xl_in", 1, 16)
        xn_in = Signal("xn_in", 1, 16)
        x1_out = Signal("x1_out", 1, 16)
        pl = Signal("lead_pe", 4)
        al = Signal("lead_act", 4)
        dl = Signal("lead_dve", 4)
        px = Signal("lead_x", 1)
        pxh = Signal("lead_xh", 1)
        pt = Signal("trail_pe", 7)
        at = Signal("trail_act", 6)
        dt_ = Signal("trail_dve", 5)
        y2 = Signal("trail_y2", 1)
        xs_h = Signal("xs_h", SKIPS)
        xs_ok = Signal("xs_ok", SKIPS)
        gate_ok = Signal("gate_ok", NGATES)
        gate_read = Signal("gate_read", NGATES)
        fc_ok = Signal("fc_ok", NSUMS)
        cell_ok = Signal("cell_ok", NU)
        tanh_ok = Signal("tanh_ok", NU)
        h_ok = Signal("h_ok", NU)
        hr_h = Signal("hr_h", NSTATES)
        state_ok = Signal("state_ok", NSTATES)

        def later(b, u):
            return u > 0 or not isinstance(b[0], int) or b[0] + b[1] > 0

        def pe_lead_adj_x(pe, g, h):
            if h == 0:
                px.reach(pe, g, 1)
                if later(g, 0):
                    al.reach(pe, (g[0], g[1] - 1), 4)
            mm = adj_half(PL, N0h, N0l, h)
            if h == 1:
                mm.then_inc(pl.sem, 1)

        def pe_lead_wg0(pe, g):
            dl.reach(pe, g, 1)
            for h in range(2):
                hs = slice(h * HALF, (h + 1) * HALF)
                mm = passes(PS[:, PL + h, :], Mh[:, 0, :], Ml[:, 0, :], F0h[:, hs], F0l[:, hs], True, True)
            mm.then_inc(pl.sem, 1)

        def pe_lead_wg1(pe, g):
            dl.reach(pe, g, 3)
            for h in range(2):
                nc.tensor.matmul(PS[:, PL + h, :], onesr[:, :], bg1r[:, :], start=True, stop=False, skip_group_check=True)
            node_major(PL, F0h, F0l, Mh[:, 1, :], Ml[:, 1, :], first=False).then_inc(pl.sem, 1)

        def pe_lead_adj(pe, g, h):
            if h == 0:
                dl.reach(pe, g, 4)
            mm = adj_half(PL, N0h, N0l, h)
            if h == 1:
                mm.then_inc(pl.sem, 1)

        def pe_trail_ht(pe, l):
            h_ok.reach(pe, l, NU)
            y2.reach(pe, l, 1)
            transposes(PT, [HT[:, t * P:(t + 1) * P] for t in range(NT)]).then_inc(pt.sem, 1)

        def pe_trail_x1(pe, l):
            norm.done(pe, l, 1)
            transposes(PT, [XN[:, t, :] for t in range(NT)]).then_inc(pt.sem, 1)

        def pe_trail_neigh(pe, l, layer):
            dt_.reach(pe, l, (2, 4)[layer])
            node_major(PT, F1h, F1l, Mh[:, 3 + 2 * layer, :], Ml[:, 3 + 2 * layer, :]).then_inc(pt.sem, 1)

        def pe_trail_conv(pe, l, layer, first, last):
            for h in range(2):
                sources = range(max(first, h * NT) - h * NT, min(last, h * NT + NT - 1) - h * NT + 1)
                if 0 in sources and h == 0:
                    dt_.reach(pe, l, (3, 5)[layer])
                if sources:
                    adj_half(PT, N1h, N1l, h, stop=False, sources=sources)
                if NT - 1 in sources:
                    hs = slice(h * HALF, (h + 1) * HALF)
                    mm = passes(PS[:, PT + h, :], Mh[:, 2 + 2 * layer, :], Ml[:, 2 + 2 * layer, :], F1h[:, hs], F1l[:, hs], False, True)
            if last == 2 * NT - 1:
                mm.then_inc(pt.sem, 1)

        def pe_trail_back(pe, l):
            at.reach(pe, l, 6)
            transposes(PT, [Z1[:, t * P:(t + 1) * P] for t in range(NT)]).then_inc(pt.sem, 1)

        def pe_unit(pe, b, u):
            p, k, w0, n = UNITS[u]
            if k == 0 and w0 == 0:
                xs_ok.reach(pe, b, p)
            if later(b, u):
                gate_read.reach(pe, b, GATES_BEFORE[u])
            c0 = k * n + w0
            for g in gates_of(k):
                mm = passes(PS[:, g, 0:n], WIh[:, p - 1, g], WIl[:, p - 1, g], XSh[:, c0:c0 + n], XSl[:, c0:c0 + n], True, k == 0)
                if k == 0:
                    mm.then_inc(gate_ok.sem, 1)
            if k:
                state_ok.reach(pe, b, STATES_BEFORE[u])
                for g in gates_of(k):
                    passes(PS[:, g, 0:n], WHh[:, p - 2, g], WHl[:, p - 2, g], HRh[:, 0:n], HRl[:, 0:n], False, True)\
                        .then_inc(gate_ok.sem, 1)

        def pe_fill(pe, u, g, l):
            if l and u == 0:
                pe_trail_ht(pe, l)
            if g and u == 1:
                pe_lead_adj_x(pe, g, 0)
                pe_lead_adj_x(pe, g, 1)
            if u == 2:
                if g:
                    pe_lead_wg0(pe, g)
                if l:
                    pe_trail_x1(pe, l)
            if u == 3:
                if l:
                    pe_trail_neigh(pe, l, 0)
                if g:
                    pe_lead_wg1(pe, g)
                if l:
                    pe_trail_conv(pe, l, 0, 0, 7)
            if l and u == 4:
                pe_trail_conv(pe, l, 0, 8, 15)
            if g and u == 5:
                pe_lead_adj(pe, g, 0)
            if u == 6:
                if g:
                    pe_lead_adj(pe, g, 1)
                if l:
                    pe_trail_neigh(pe, l, 1)
            if l and u in (7, 8, 9):
                pe_trail_conv(pe, l, 1, *((0, 5), (6, 10), (11, 15))[u - 7])
            if l and u == 10:
                pe_trail_back(pe, l)

        def act_unit(act, b, u):
            p, k, w0, n = UNITS[u]
            if later(b, u):
                h_ok.reach(act, b, u)
            for j, g in enumerate(gates_of(k)):
                gate_ok.reach(act, b, GATES_BEFORE[u] + j + 1)
                nc.scalar.activation(gates[g][:, 0:n], PS[:, g, 0:n], ACT.Tanh if g == GATE_G else ACT.Sigmoid,
                                     bias=col(C_LSTM + 4 * (p - 1) + g)).then_inc(gate_read.sem, 1)
            cell_ok.reach(act, b, u + 1)
            nc.scalar.activation(TC[:, 0:n], C[:, 0:n], ACT.Tanh).then_inc(tanh_ok.sem, 1)

        def act_fill(act, u, g, l):
            if g and u == 1:
                pl.reach(act, g, 1)
                nc.scalar.activation(F0h[:, :], bank2(PL), ACT.Copy).then_inc(al.sem, 1)
            if u == 2:
                if g:
                    dl.reach(act, g, 2)
                    nc.scalar.activation(F0h[:, :], Z0[:, :], ACT.Relu).then_inc(al.sem, 1)
                if l:
                    pt.reach(act, l, 2)
                    nc.scalar.activation(F1h[:, :], bank2(PT), ACT.Copy).then_inc(at.sem, 1)
            if u == 3:
                if l:
                    pt.reach(act, l, 3)
                    nc.scalar.activation(flat(N1h[:, :, :]), bank2(PT), ACT.Copy).then_inc(at.sem, 1)
                if g:
                    pl.reach(act, g, 3)
                    nc.scalar.activation(flat(N0h[:, :, :]), bank2(PL), ACT.Copy).then_inc(al.sem, 1)
            if l and u == 4:
                pt.reach(act, l, 4)
                x1_out.reach(act, l, 1)
                nc.scalar.activation(F1h[:, :], bank2(PT), ACT.Relu, bias=col(C_B1)).then_inc(at.sem, 1)
                nc.scalar.activation(Z1[:, :], bank2(PT), ACT.Relu, bias=col(C_B1)).then_inc(at.sem, 1)
            if u == 6:
                if g:
                    pl.reach(act, g, 4)
                    nc.scalar.activation(HN[:, 0:T], bank2(PL), ACT.Relu).then_inc(al.sem, 1)
                if l:
                    pt.reach(act, l, 5)
                    nc.scalar.activation(flat(N1h[:, :, :]), bank2(PT), ACT.Copy).then_inc(at.sem, 1)
            if l and u == 9:
                pt.reach(act, l, 6)
                nc.scalar.activation(Z1[:, :], bank2(PT), ACT.Relu, bias=col(C_B2), scale=0.5).then_inc(at.sem, 1)

        def dve_inputs(dve, b, p, n):
            src = (HN if p == 1 else HT)[:, 0:p * n].rearrange("q (w k) -> q k w", k=p)
            hi, lo = (t[:, 0:p * n].rearrange("q (k w) -> q k w", k=p) for t in (XSh, XSl))
            nc.vector.tensor_copy(hi, src).then_inc(xs_h.sem, 1)
            xs_h.reach(dve, b, p)
            nc.vector.tensor_tensor(lo, src, hi.bitcast(F32), ALU.subtract).then_inc(xs_ok.sem, 1)

        def dve_unit(dve, b, u, l):
            p, k, w0, n = UNITS[u]
            gi, gf, gg, go = (gates[g][:, 0:n] for g in (GATE_I, GATE_F, GATE_G, GATE_O))
            c, ig, tc, hs = (t[:, 0:n] for t in (C, IG, TC, HS))
            gate_read.reach(dve, b, GATES_BEFORE[u] + 2)
            if k == 0:
                nc.vector.tensor_tensor(c, gi, gg, ALU.mult).then_inc(cell_ok.sem, 1)
            else:
                nc.vector.tensor_tensor(ig, gi, gg, ALU.mult)
                gate_read.reach(dve, b, GATES_BEFORE[u] + 3)
                nc.vector.tensor_tensor(c, gf, c, ALU.mult).then_inc(fc_ok.sem, 1)
                fc_ok.reach(dve, b, SUMS_BEFORE[u] + 1)
                nc.vector.tensor_tensor(c, c, ig, ALU.add).then_inc(cell_ok.sem, 1)
            if l and u == 0:
                pt.reach(dve, l, 1)
            tanh_ok.reach(dve, b, u + 1)
            if k == p - 1:
                m = min(n, T // p)
                dst = HT[:, w0:w0 + n] if p == 1 else HT[:, 0:m * p].rearrange("q (w k) -> q w k", k=p)[:, :, k]
                nc.vector.tensor_tensor(dst, go[:, 0:m], tc[:, 0:m], ALU.mult).then_inc(h_ok.sem, 1)
            else:
                nc.vector.tensor_tensor(hs, go, tc, ALU.mult).then_inc(h_ok.sem, 1)
                h_ok.reach(dve, b, u + 1)
                nc.vector.tensor_copy(HRh[:, 0:n], hs).then_inc(hr_h.sem, 1)
                hr_h.reach(dve, b, STATES_BEFORE[u] + 1)
                nc.vector.tensor_tensor(HRl[:, 0:n], hs, HRh[:, 0:n].bitcast(F32), ALU.subtract).then_inc(state_ok.sem, 1)

        def dve_next_inputs(dve, b, u):
            p, k, w0, n = UNITS[u]
            if k == p - 1 and p < SKIPS and (p > 1 or w0):
                h_ok.reach(dve, b, u + 1)
                dve_inputs(dve, b, p + 1, UNITS[u + 1][3])

        def dve_low(lo, full, hi):
            return nc.vector.tensor_tensor(lo, full, hi.bitcast(F32), ALU.subtract)

        def dve_fill(dve, u, g, l):
            if l and u == 0:
                xn_in.reach(dve, l, 1)
                pt.reach(dve, l, 1)
                nc.vector.tensor_tensor(flat(XN[:, :, :]), flat(XN[:, :, :]), bank2(PT), ALU.add).then_inc(dt_.sem, 1)
            if u == 1:
                if l:
                    dt_.reach(dve, l, 1)
                    norm.dve_stats(dve, l, 1, XN)
                if g:
                    al.reach(dve, g, 1)
                    dve_low(F0l[:, :], bank2(PL), F0h[:, :]).then_inc(dl.sem, 1)
                if l:
                    norm.scale(dve, nc.vector, l, 1, XN, XN)
            if u == 2:
                if g:
                    pl.reach(dve, g, 2)
                    nc.vector.tensor_tensor(Z0[:, :], bank2(PL), B0[:, :], ALU.add).then_inc(dl.sem, 1)
                if l:
                    at.reach(dve, l, 1)
                    dve_low(F1l[:, :], bank2(PT), F1h[:, :]).then_inc(dt_.sem, 1)
                if g:
                    al.reach(dve, g, 2)
                    nc.vector.scalar_tensor_tensor(out=F0l[:, :], in0=Z0[:, :], scalar=0.0, in1=F0h[:, :].bitcast(F32),
                                                   op0=ALU.max, op1=ALU.subtract).then_inc(dl.sem, 1)
            if u == 3:
                if l:
                    at.reach(dve, l, 2)
                    dve_low(flat(N1l[:, :, :]), bank2(PT), flat(N1h[:, :, :])).then_inc(dt_.sem, 1)
                if g:
                    al.reach(dve, g, 3)
                    dve_low(flat(N0l[:, :, :]), bank2(PL), flat(N0h[:, :, :])).then_inc(dl.sem, 1)
            if l and u == 4:
                at.reach(dve, l, 4)
                dve_low(F1l[:, :], Z1[:, :], F1h[:, :]).then_inc(dt_.sem, 1)
            if l and u == 6:
                at.reach(dve, l, 5)
                dve_low(flat(N1l[:, :, :]), bank2(PT), flat(N1h[:, :, :])).then_inc(dt_.sem, 1)
            if l and u == 10:
                pt.reach(dve, l, 7)
                nc.vector.scalar_tensor_tensor(out=Z1[:, :], in0=flat(XN[:, :, :]), scalar=1.5, in1=bank2(PT),
                                               op0=ALU.mult, op1=ALU.add).then_inc(y2.sem, 1)
                y2.reach(dve, l, 2)
                norm.dve_stats(dve, l, 2, tiles(Z1))

        norm = Norm("norm", 2, 0)
        with nc.Block() as block:
            @block.tensor
            def _(pe):
                def batch(b, g, l):
                    for u in range(NU):
                        pe_unit(pe, b, u)
                        pe_fill(pe, u, g, l)

                for u in range(NU):
                    pe_fill(pe, u, (0, 0), None)
                batch((0, 0), (0, 1), None)
                with pe.Fori(1, B - 1) as i:
                    batch((i, 0), (i, 1), (i, -1))
                batch((B - 1, 0), None, (B - 1, -1))
                for u in range(NU):
                    pe_fill(pe, u, None, (B - 1, 0))

            @block.scalar
            def _(act):
                nc.scalar.preload_act_table(ACT.Sigmoid)
                act.sem_inc(x1_out.sem, 16)

                def batch(b, g, l):
                    for u in range(NU):
                        act_unit(act, b, u)
                        act_fill(act, u, g, l)

                for u in range(NU):
                    act_fill(act, u, (0, 0), None)
                batch((0, 0), (0, 1), None)
                with act.Fori(1, B - 1) as i:
                    batch((i, 0), (i, 1), (i, -1))
                batch((B - 1, 0), None, (B - 1, -1))
                for u in range(NU):
                    act_fill(act, u, None, (B - 1, 0))

            @block.vector
            def _(dve):
                def next_inputs(b, g):
                    if b:
                        gate_ok.reach(dve, b, GATES_BEFORE[NU - 1] + 1)
                    al.reach(dve, g, 4)
                    dve_inputs(dve, g, 1, T)

                def batch(b, g, l):
                    for u in range(NU):
                        if g and u == NU - 1:
                            next_inputs(b, g)
                        dve_unit(dve, b, u, l)
                        if u in (1, 6):
                            dve_next_inputs(dve, b, u)
                        dve_fill(dve, u, g, l)
                        if u not in (1, 6):
                            dve_next_inputs(dve, b, u)

                nc.vector.memset(HT[:, T:TPAD], 0.0)
                dve.sem_inc(y2.sem, 1)
                for u in range(NU):
                    dve_fill(dve, u, (0, 0), None)
                next_inputs(None, (0, 0))
                batch((0, 0), (0, 1), None)
                with dve.Fori(1, B - 1) as i:
                    batch((i, 0), (i, 1), (i, -1))
                batch((B - 1, 0), None, (B - 1, -1))
                for u in range(NU):
                    dve_fill(dve, u, None, (B - 1, 0))

            @block.gpsimd
            def _(pool):
                def split_x(g):
                    xl_in.reach(pool, g, 1)
                    if later(g, 0):
                        pl.reach(pool, (g[0], g[1] - 1), 4)
                    settle(pool)
                    nc.gpsimd.tensor_copy(flat(N0h[:, :, :]), flat(XL[:, :, :])).then_inc(pxh.sem, 1)
                    pxh.reach(pool, g, 1)
                    nc.gpsimd.tensor_tensor(flat(N0l[:, :, :]), flat(XL[:, :, :]), flat(N0h[:, :, :]).bitcast(F32),
                                            ALU.subtract).then_inc(px.sem, 1)

                def second_scale(l):
                    norm.scale(pool, nc.gpsimd, l, 2, tiles(Z1), tiles(Z1))

                for g in range(3):
                    split_x((g, 0))
                norm.pool(pool, (0, 0), 1)
                split_x((3, 0))
                norm.pool(pool, (0, 0), 2)
                with pool.Fori(2, B - 2) as i:
                    norm.pool(pool, (i, -1), 1)
                    second_scale((i, -2))
                    split_x((i, 2))
                    norm.pool(pool, (i, -1), 2)
                for l in range(B - 3, B):
                    norm.pool(pool, (l, 0), 1)
                    second_scale((l - 1, 0))
                    norm.pool(pool, (l, 0), 2)
                second_scale((B - 1, 0))

            @block.sync
            def _(sp):
                def load_lead(g):
                    sp.dma_start(XL[:, :, :], x[g].rearrange("(t p) d -> p t d", p=P)).then_inc(xl_in.sem, 16)

                def load_trail(l):
                    sp.dma_start(XN[:, :, :], x[l].rearrange("(t p) d -> p t d", p=P)).then_inc(xn_in.sem, 16)

                def store(l, at_):
                    norm.done(sp, l, 2)
                    sp.dma_start(x1_dram[at_], Z1[:, :]).then_inc(x1_out.sem, 16)

                load_lead(0)
                load_trail(0)
                for g in range(2):
                    px.reach(sp, (g, 0), 1)
                    load_lead(g + 1)
                with sp.Fori(0, B - 3) as l:
                    px.reach(sp, (l, 2), 1)
                    load_lead(l + 3)
                    y2.reach(sp, (l, 0), 2)
                    load_trail(l + 1)
                    store((l, 0), l)
                for l in range(B - 3, B):
                    if l < B - 1:
                        y2.reach(sp, (l, 0), 2)
                        load_trail(l + 1)
                    store((l, 0), l)
                sp.wait_ge(x1_out.sem, 16 * (B + 1))
        fused.close()
        s0.close()
        lstm.close()

        late = ExitStack()
        TW = NT * (D + 2)
        HW = sbr(late, "HW", [P, B, TW])
        PENT = sbr(late, "PENT", [P, NT, T], BF16)
        l2 = ExitStack()
        HP1 = sb(l2, "HP1", [P, B, T])
        l2a = ExitStack()
        X2 = [sb(l2a, f"x2_{s}", [P, NT, D]) for s in range(2)]
        Yh, Yl = ([sb(l2a, f"{n}{s}", [P, NT, D], F32R) for s in range(2)] for n in ("Yh", "Yl"))
        Ah, Al = (sb(l2a, n, [P, T], F32R) for n in ("Ah", "Al"))
        ZZ = sb(l2a, "ZZ", [P, T])
        diag_in, diag_hi = sem("diag_in"), sem("diag_hi")
        diag_ok = sem("diag_ok")
        x2_in = [sem(f"x2_in{s}") for s in range(2)]
        y_hi, y_lo = Signal("y_hi", 1), Signal("y_lo", 1)
        agg_ok = Signal("agg_ok", 1)
        zz_ok, a_hi, a_lo = Signal("zz_ok", 1), Signal("a_hi", 1), Signal("a_lo", 1)
        w1_ok = Signal("w1_ok", NHC)
        hid_ok = Signal("hid_ok", NHC)
        hid_read = sem("hid_read")
        pent_ok = sem("pent_ok")

        def hidden(c, b):
            return HW[:, b, 0:T] if c == 0 else HP1[:, b, :]

        def index(b):
            i, plus, mul = b
            return i * mul + plus

        def step_pairs(eng, body):
            with eng.Fori(0, B // 2 - 1) as i:
                for s in range(2):
                    body((i, s, 2), s, True)
            for s in range(2):
                body((B - 2 + s, 0, 1), s, False)

        def ahead(b, n):
            i, plus, mul = b
            return (i, plus + n, mul)

        with nc.Block() as block:
            @block.sync
            def _(sp):
                def load(b, s):
                    sp.dma_start(flat(X2[s][:, :, :]), x1_dram[index(b)]).then_inc(x2_in[s], 16)
                for s in range(2):
                    load((s, 0, 1), s)
                with sp.Fori(0, B // 2 - 1) as i:
                    for s in range(2):
                        y_lo.reach(sp, (i, s, 2), 1)
                        load((i, s + 2, 2), s)

            @block.scalar
            def _(act):
                def y_high(b, s, pair):
                    act.wait_ge(x2_in[s], pair * 16 + 16)
                    for t in range(NT):
                        ins = nc.scalar.activation(Yh[s][:, t, :], X2[s][:, t, :], ACT.Copy, scale=dinv[:, t:t + 1])
                    ins.then_inc(y_hi.sem, 1)

                def body(b, s, more):
                    zz_ok.reach(act, b, 1)
                    nc.scalar.activation(Ah[:, :], ZZ[:, :], ACT.Copy).then_inc(a_hi.sem, 1)
                    if more:
                        y_high(ahead(b, 2), s, b[0] + 1)
                    for c in range(NHC):
                        w1_ok.reach(act, b, c + 1)
                        settle(act)
                        nc.scalar.activation(hidden(c, index(b)), bank2(4 + 2 * c), ACT.Identity, bias=col(C_C1 + c)).then_inc(hid_ok.sem, 1)

                for s in range(2):
                    y_high((s, 0, 1), s, 0)
                step_pairs(act, body)

            @block.vector
            def _(dve):
                def blocks(t):
                    v = flat(t[:, :, :])
                    w = T + P
                    return [(v[:, 0:(NT - 1) * w].rearrange("p (t w) -> p t w", w=w)[:, :, 0:P], slice(0, NT - 1)),
                            (v[:, NT * T - P:NT * T].rearrange("p (t w) -> p t w", w=P), slice(NT - 1, NT))]
                DG = ZZ[:, :].rearrange("p (t w) -> p t w", w=P)
                both = list(zip(blocks(ATh), blocks(ATl)))
                for (hi, ts), (lo, _) in both:
                    nc.vector.tensor_tensor(DG[:, ts], hi.bitcast(F32), lo.bitcast(F32), ALU.add).then_inc(diag_in, 1)
                dve.wait_ge(diag_in, 2)
                nc.vector.tensor_tensor(DG, DG, ident[:, :].rearrange("p (o w) -> p o w", o=1).broadcast_to([P, NT, P]), ALU.add).then_inc(diag_in, 1)
                dve.wait_ge(diag_in, 3)
                for (hi, ts), _ in both:
                    nc.vector.tensor_copy(hi, DG[:, ts]).then_inc(diag_hi, 1)
                dve.wait_ge(diag_hi, 2)
                for (hi, ts), (lo, _) in both:
                    nc.vector.tensor_tensor(lo, DG[:, ts], hi.bitcast(F32), ALU.subtract).then_inc(diag_ok, 1)
                dve.wait_ge(diag_ok, 2)

                def y_low(b, s):
                    y_hi.reach(dve, b, 1)
                    for t in range(NT):
                        ins = nc.vector.scalar_tensor_tensor(out=Yl[s][:, t, :], in0=X2[s][:, t, :], scalar=dinv[:, t:t + 1],
                                                             in1=Yh[s][:, t, :].bitcast(F32), op0=ALU.mult, op1=ALU.subtract)
                    ins.then_inc(y_lo.sem, 1)

                def body(b, s, more):
                    agg_ok.reach(dve, b, 1)
                    nc.vector.tensor_tensor(ZZ[:, :], bank2(2 * s), dinv_row[:, :], ALU.mult).then_inc(zz_ok.sem, 1)
                    a_hi.reach(dve, b, 1)
                    nc.vector.tensor_tensor(Al[:, :], ZZ[:, :], Ah[:, :].bitcast(F32), ALU.subtract).then_inc(a_lo.sem, 1)
                    if more:
                        y_low(ahead(b, 2), s)
                    for c in range(NHC):
                        hid_ok.reach(dve, b, c + 1)
                        settle(dve)
                        for h in range(2):
                            nc.vector.bn_stats(S1[:, c, index(b) * 2 + h, :], hidden(c, index(b))[:, h * HALF:(h + 1) * HALF]).then_inc(hid_read, 1)

                for s in range(2):
                    y_low((s, 0, 1), s)
                step_pairs(dve, body)
                dve.wait_ge(hid_read, 2 * NHC * B)

            @block.tensor
            def _(pe):
                def agg(b, s, h):
                    if h == 0:
                        y_lo.reach(pe, b, 1)
                    mm = adj_half(2 * s, Yh[s], Yl[s], h)
                    if h == 1:
                        mm.then_inc(agg_ok.sem, 1)

                def body(b, s, more):
                    following = more or s == 0
                    if following:
                        agg(ahead(b, 1), 1 - s, 0)
                    a_lo.reach(pe, b, 1)
                    for c in range(NHC):
                        for h in range(2):
                            hs = slice(h * HALF, (h + 1) * HALF)
                            mm = passes(PS[:, 4 + 2 * c + h, :], W1Th[:, c, :], W1Tl[:, c, :], Ah[:, hs], Al[:, hs], True, True)
                        mm.then_inc(w1_ok.sem, 1)
                    if following:
                        agg(ahead(b, 1), 1 - s, 1)

                pe.wait_ge(diag_ok, 2)
                agg((0, 0, 1), 0, 0)
                agg((0, 0, 1), 0, 1)
                step_pairs(pe, body)

            @block.gpsimd
            def _(pool):
                pool.wait_ge(diag_ok, 2)
                for n in range(NT):
                    nc.gpsimd.tensor_scalar(PENT[:, n, :], ATh[:, n, :].bitcast(F32), 0.0, BLOCKED, ALU.is_equal, ALU.mult).then_inc(pent_ok, 1)
                pool.wait_ge(pent_ok, NT)
        l2a.close()

        bn_dve, bn_pool = sem("bn_dve"), sem("bn_pool")

        def batch_norm_params(block, groups, base_dve, base_pool):
            @block.vector
            def _(dve):
                n = [base_dve]

                def done(ins):
                    n[0] += 1
                    ins.then_inc(bn_dve, 1)
                    dve.wait_ge(bn_dve, n[0])
                for r, stats, _, _ in groups:
                    done(nc.vector.bn_aggr(bnp[:, r, 0:2], stats))
                    done(nc.vector.tensor_scalar(bnp[:, r, 5:6], bnp[:, r, 1:2], BN_EPS, None, ALU.add))
                dve.wait_ge(bn_pool, base_pool + len(groups))
                for r, _, g, be in groups:
                    done(nc.vector.tensor_tensor(bnp[:, r, 3:4], bnp[:, r, 2:3], col(g), ALU.mult))
                    done(nc.vector.tensor_tensor(bnp[:, r, 4:5], bnp[:, r, 0:1], bnp[:, r, 3:4], ALU.mult))
                    done(nc.vector.tensor_tensor(bnp[:, r, 4:5], col(be), bnp[:, r, 4:5], ALU.subtract))

            @block.gpsimd
            def _(pool):
                for k, (r, _, _, _) in enumerate(groups):
                    pool.wait_ge(bn_dve, base_dve + 2 * k + 2)
                    nc.gpsimd.tensor_tensor(bnp[:, r, 2:3], bnp[:, r, 5:6], neg_half[:, 0:1], ALU.pow).then_inc(bn_pool, 1)

        with nc.Block() as block:
            batch_norm_params(block, [(0, flat(S1[:, 0]), C_G1, C_BE1), (1, flat(S1[:, 1]), C_G1 + 1, C_BE1 + 1)], 0, 0)

        PENN = sbr(late, "PENN", [P, NT, T], BF16)
        l2b = ExitStack()
        Rh, Rl = ([sb(l2b, f"{n}{s}", [P, NHC, HALF], F32R) for s in range(2)] for n in ("Rh", "Rl"))
        NAT2 = sb(l2b, "NAT2", [P, 2, T])
        nat_in = [sem(f"nat_in{s}") for s in range(2)]
        penn_ok = sem("penn_ok")
        relu_ok = Signal("relu_ok", 2 * NHC)
        rh0, rh1 = Signal("relu_high0", 2), Signal("relu_high1", 2)
        rl = Signal("relu_low", 2 * NHC)
        w2_ok, y3_ok = Signal("w2_ok", 2), Signal("w2_read", 2)
        s2_ok = sem("stats2_ok")
        halves = [slice(s * HALF, (s + 1) * HALF) for s in range(2)]
        with nc.Block() as block:
            @block.sync
            def _(sp):
                for n in range(NT):
                    if n >= 2:
                        sp.wait_ge(penn_ok, n - 1)
                    sp.dma_start(NAT2[:, n % 2, :], adj[n * P:(n + 1) * P, :]).then_inc(nat_in[n % 2], 16)

            @block.gpsimd
            def _(pool):
                for n in range(NT):
                    pool.wait_ge(nat_in[n % 2], 16 * (n // 2 + 1))
                    nc.gpsimd.tensor_scalar(PENN[:, n, :], NAT2[:, n % 2, :], 0.0, BLOCKED, ALU.is_equal, ALU.mult).then_inc(penn_ok, 1)
                pool.wait_ge(penn_ok, NT)

            @block.scalar
            def _(act):
                def relus(b):
                    for s in range(2):
                        for c in range(NHC):
                            v = hidden(c, index(b))[:, halves[s]]
                            nc.scalar.activation(v, v, ACT.Relu, bias=bnp[:, c, 4:5], scale=bnp[:, c, 3:4]).then_inc(relu_ok.sem, 1)
                        if later(b[:2], 0):
                            w2_ok.reach(act, ahead(b, -1), s + 1)
                        relu_ok.reach(act, b, NHC * (s + 1))
                        settle(act)
                        nc.scalar.activation(Rh[s][:, 1, :], hidden(1, index(b))[:, halves[s]], ACT.Copy).then_inc(rh1.sem, 1)

                def results(b):
                    for s in range(2):
                        w2_ok.reach(act, b, s + 1)
                        settle(act)
                        nc.scalar.activation(hidden(0, index(b))[:, halves[s]], PS[:, s, :], ACT.Identity, bias=col(C_C2)).then_inc(y3_ok.sem, 1)

                relus((0, 0, 1))
                with act.Fori(1, B) as i:
                    relus((i, 0, 1))
                    results((i, -1, 1))
                results((B - 1, 0, 1))

            @block.vector
            def _(dve):
                def splits(b):
                    for s in range(2):
                        relu_ok.reach(dve, b, NHC * s + 1)
                        if later(b[:2], 0):
                            w2_ok.reach(dve, ahead(b, -1), s + 1)
                        settle(dve)
                        v = [hidden(c, index(b))[:, halves[s]] for c in range(NHC)]
                        nc.vector.tensor_copy(Rh[s][:, 0, :], v[0]).then_inc(rh0.sem, 1)
                        rh0.reach(dve, b, s + 1)
                        nc.vector.tensor_tensor(Rl[s][:, 0, :], v[0], Rh[s][:, 0, :].bitcast(F32), ALU.subtract).then_inc(rl.sem, 1)
                        rh1.reach(dve, b, s + 1)
                        nc.vector.tensor_tensor(Rl[s][:, 1, :], v[1], Rh[s][:, 1, :].bitcast(F32), ALU.subtract).then_inc(rl.sem, 1)

                def stats(b):
                    for s in range(2):
                        y3_ok.reach(dve, b, s + 1)
                        settle(dve)
                        nc.vector.bn_stats(S2[:, index(b) * 2 + s, :], hidden(0, index(b))[:, halves[s]]).then_inc(s2_ok, 1)

                splits((0, 0, 1))
                with dve.Fori(1, B) as i:
                    splits((i, 0, 1))
                    stats((i, -1, 1))
                stats((B - 1, 0, 1))
                dve.wait_ge(s2_ok, 2 * B)

            @block.tensor
            def _(pe):
                def products(b):
                    for s in range(2):
                        if later(b[:2], 0):
                            y3_ok.reach(pe, ahead(b, -1), s + 1)
                        for c in range(NHC):
                            rl.reach(pe, b, NHC * s + c + 1)
                            mm = passes(PS[:, s, :], W2Th[:, c, :], W2Tl[:, c, :], Rh[s][:, c, :], Rl[s][:, c, :], c == 0, c == NHC - 1)
                        mm.then_inc(w2_ok.sem, 1)

                products((0, 0, 1))
                with pe.Fori(1, B) as i:
                    products((i, 0, 1))
        l2b.close()
        with nc.Block() as block:
            batch_norm_params(block, [(2, flat(S2[:, :, :]), C_G2, C_BE2)], 10, 2)
        l2.close()
        graph.close()

        l3 = ExitStack()
        x3_dram = nc.dram_tensor("x3_dram", (B, P, NT * D), F32, kind="Internal").ap()
        rows_dram = nc.dram_tensor("rows_dram", (B, 2 * NT, P), F32, kind="Internal").ap()
        S2C = sb(l3, "S2C", [P, B, 2, NT])
        RB = sb(l3, "RB", [P, B, 2 * T])
        Z3 = sb(l3, "Z3", [P, T])
        X3 = sb(l3, "X3", [P, NT, D])
        F3h, F3l = (sb(l3, n, [P, T], F32R) for n in ("F3h", "F3l"))
        junk3 = sb(l3, "junk3", [P, T])
        MX = sb(l3, "MX", [P, NT])
        RR = sb(l3, "RR", [P, 2 * NT])
        RRT = sb(l3, "RRT", [2 * NT, P])
        NTT, NV = 2, 4
        TT = [sb(l3, f"tt{k}", [P, T]) for k in range(NTT)]
        V = [sb(l3, f"v{k}", [P, T]) for k in range(NV)]
        ATT = sb(l3, "ATT", [P, NT, D + 1])
        REC = sb(l3, "REC", [P, NT])
        XR = sb(l3, "XR", [P, NT, D])
        x3_in, x3_out = Signal("x3_in", 1, 16), Signal("x3_out", 1, 16)
        xr_in = Signal("xr_in", 1, 16)
        rows_out, rb_in = Signal("rows_out", 1, 16), Signal("rb_in", 1, 16)
        out_ok = Signal("out_ok", 1, 16)
        z_ok, zt_ok = Signal("z_ok", 1), Signal("zt_ok", 1)
        y_ok = Signal("y3", 1)
        x3_ok, x3t_ok = Signal("x3_ok", 2), Signal("x3t_ok", 1)
        f_hi, f_lo = Signal("f3_hi", 1), Signal("f3_lo", 1)
        wh_pe, s2_pe = Signal("wh_pe", 1), Signal("s2_pe", 1)
        wh_ok = Signal("wh_ok", 2)
        mx = Signal("mx", NT)
        small = Signal("rows_dve", 6)
        rr_pe, rrt_ok = Signal("rr_pe", 1), Signal("rrt_ok", 1)
        ones2_ok, ones_ok = sem("ones2_ok"), Signal("ones_ok", 1)
        tt_ok = Signal("tt_ok", NT)
        v_ok = Signal("v_ok", NT, credit=NTT)
        m_ok = Signal("m_ok", NT)
        e_ok = Signal("e_ok", NT)
        att_pe = Signal("att_pe", NT, credit=NV)
        att_ok = Signal("att_ok", 2, credit=2)
        rec_ok, sum_ok = Signal("rec_ok", 1), Signal("sum_ok", 1)
        res_ok = Signal("res_ok", 2)
        front_norm, back_norm = Norm("front", 1, 0), Norm("back", 1, 1)

        ones2 = sb(l3, "ones2", [P, NT, 1])

        PARTS = ((0, 2, 3), (2, 3, 2))

        def att(t):
            return PS[:, t // 3, (t % 3) * (D + 1):(t % 3 + 1) * (D + 1)]

        def tiles_of(b):
            return HW[:, index(b), :].rearrange("p (t d) -> p t d", t=NT)

        def wh(b, jt):
            return HW[:, index(b), jt * (D + 2):jt * (D + 2) + D + 1]

        def turns(eng, step, n=NT, last=B - 2):
            def turn(i, stages="cmfko"):
                for q in range(n):
                    step(q, *((i, plus, 1) if name in stages else None
                              for name, plus in (("c", 0), ("m", 1), ("f", 2), ("k", -1), ("o", -2))))
            for i, stages in ((-2, "f"), (-1, "mf"), (0, "cmf"), (1, "cmfk")):
                turn(i, stages)
            with eng.Fori(2, last) as i:
                turn(i)
            for i in range(last, B - 2):
                turn(i)
            for i, stages in ((B - 2, "cmko"), (B - 1, "cko"), (B, "ko"), (B + 1, "o")):
                turn(i, stages)

        with nc.Block() as block:
            @block.sync
            def _(sp):
                def step(q, c, m, f, k, o):
                    if o:
                        res_ok.reach(sp, o, 2)
                        sp.dma_start(out[index(o)].rearrange("(t p) d -> p t d", p=P), XR[:, :, :]).then_inc(out_ok.sem, 16)
                        out_ok.reach(sp, o, 1)
                        settle(sp)
                    if k:
                        sp.dma_start(flat(XR[:, :, :]), x3_dram[index(k)]).then_inc(xr_in.sem, 16)
                    if f:
                        x3_ok.reach(sp, f, 2)
                        sp.dma_start(x3_dram[index(f)], flat(X3[:, :, :])).then_inc(x3_out.sem, 16)
                    if m:
                        rrt_ok.reach(sp, m, 1)
                        sp.dma_start(rows_dram[index(m)], RRT[:, :]).then_inc(rows_out.sem, 16)
                        rows_out.reach(sp, m, 1)
                        settle(sp)
                        sp.dma_start(RB[:, index(m), :], rows_dram[index(m)].rearrange("(o t) p -> o (t p)", o=1).broadcast_to([P, 2 * T])).then_inc(rb_in.sem, 16)
                    if f and not (isinstance(f[0], int) and f[0] + f[1] == B - 1):
                        x3_out.reach(sp, f, 1)
                        settle(sp)
                        x3t_ok.reach(sp, f, 1)
                        sp.dma_start(flat(X3[:, :, :]), x1_dram[index(ahead(f, 1))]).then_inc(x3_in.sem, 16)

                sp.dma_start(flat(X3[:, :, :]), x1_dram[0]).then_inc(x3_in.sem, 16)
                turns(sp, step, n=1, last=B - 3)

            @block.scalar
            def _(act):
                nc.scalar.preload_act_table(ACT.Exp)

                def exps(b, j):
                    m_ok.reach(act, b, j + 1)
                    nc.scalar.activation(V[j % NV][:, :], V[j % NV][:, :], ACT.Exp).then_inc(e_ok.sem, 1)

                def step(q, c, m, f, k, o):
                    if f and q == 0:
                        settle(act)
                        nc.scalar.activation(Z3[:, :], HW[:, index(f), 0:T], ACT.Identity, bias=bnp[:, 2, 4:5], scale=bnp[:, 2, 3:4]).then_inc(z_ok.sem, 1)
                    if k and q == 3:
                        att_pe.reach(act, k, NT)
                        for b0, b1, n in PARTS:
                            t0, t1 = 3 * b0, 3 * b0 + n * (b1 - b0)
                            nc.scalar.activation(flat(ATT[:, t0:t1, :]).rearrange("p (b n) -> p b n", b=b1 - b0),
                                                 PS[:, b0:b1, 0:n * (D + 1)], ACT.Copy).then_inc(att_ok.sem, 1)
                    if c:
                        if q == 0:
                            rb_in.reach(act, c, 1)
                        v_ok.reach(act, c, q - NTT + 1)
                        settle(act)
                        nc.scalar.activation(TT[q % NTT][:, :], RB[:, index(c), T:2 * T], ACT.Identity,
                                             bias=S2C[:, index(c), 1, q:q + 1]).then_inc(tt_ok.sem, 1)
                    if q < 2 and k:
                        exps(k, NT - 2 + q)
                    if q >= 2 and c:
                        exps(c, q - 2)
                    if o and q in (1, 2):
                        back_norm.act_scale(act, o, 1, XR, XR, res_ok.sem, q - 1)
                    if f and q in (3, 4):
                        front_norm.act_scale(act, f, 1, X3, X3, x3_ok.sem, q - 3)
                    if m and q == 6:
                        rr_pe.reach(act, m, 1)
                        nc.scalar.activation(RRT[:, :], PS[0:2 * NT, 7, 0:P], ACT.Copy).then_inc(rrt_ok.sem, 1)
                    if f and q == 5:
                        x3t_ok.reach(act, f, 1)
                        nc.scalar.activation(F3h[:, :], bank2(5), ACT.Copy).then_inc(f_hi.sem, 1)
                    if f and q == 7:
                        wh_pe.reach(act, f, 1)
                        settle(act)
                        for b0, b1, n in PARTS:
                            t0, t1 = 3 * b0, 3 * b0 + n * (b1 - b0)
                            nc.scalar.activation(HW[:, index(f), t0 * (D + 2):t1 * (D + 2)].rearrange("p (b n) -> p b n", b=b1 - b0),
                                                 PS[:, 5 + b0:5 + b1, 0:n * (D + 2)], ACT.Copy).then_inc(wh_ok.sem, 1)

                act.sem_inc(att_ok.sem, att_ok.credit)
                turns(act, step)

            @block.gpsimd
            def _(pool):
                def step(q, c, m, f, k, o):
                    if c:
                        v_ok.reach(pool, c, q + 1)
                        nc.gpsimd.tensor_tensor(V[q % NV][:, :], V[q % NV][:, :], PENT[:, q, :], ALU.add).then_inc(m_ok.sem, 1)
                    if f and q == 2:
                        front_norm.pool(pool, f, 1, shifts=True)
                    if m and q == 6:
                        small.reach(pool, m, 6)
                        settle(pool)
                        nc.gpsimd.tensor_copy(tiles_of(m)[:, :, D:D + 1], ones2[:, :, :]).then_inc(ones_ok.sem, 1)
                    if k and q == 7:
                        back_norm.pool(pool, k, 1, shifts=True)
                nc.gpsimd.memset(ones2[:, :, :], 1.0).then_inc(ones2_ok, 1)
                pool.wait_ge(ones2_ok, 1)
                turns(pool, step)

            @block.vector
            def _(dve):
                MAXIMA = (0, 1, 1, 3, 5, 7, 8, 8, 8)

                def step(q, c, m, f, k, o):
                    if c:
                        att_pe.reach(dve, c, q - NV + 1)
                        tt_ok.reach(dve, c, q + 1)
                        nc.vector.scalar_tensor_tensor(out=V[q % NV][:, :], in0=RB[:, index(c), 0:T], scalar=S2C[:, index(c), 0, q:q + 1],
                                                       in1=TT[q % NTT][:, :], op0=ALU.add, op1=ALU.max).then_inc(v_ok.sem, 1)
                    if f and q == 5:
                        f_hi.reach(dve, f, 1)
                        nc.vector.tensor_tensor(F3l[:, :], bank2(5), F3h[:, :].bitcast(F32), ALU.subtract).then_inc(f_lo.sem, 1)
                    if m:
                        if q == 0:
                            s2_pe.reach(dve, m, 1)
                        for t in range(MAXIMA[q], MAXIMA[q + 1]):
                            settle(dve)
                            nc.vector.tensor_tensor_reduce(junk3[:, :], PENN[:, t, :], bank2(3), 1.0, 2 * BLOCKED,
                                                           ALU.add, ALU.max, MX[:, t:t + 1]).then_inc(mx.sem, 1)
                            mx.reach(dve, m, t + 1)
                        if q == 5:
                            wh_ok.reach(dve, m, 2)
                            settle(dve)
                            s1, s2 = tiles_of(m)[:, :, D], tiles_of(m)[:, :, D + 1]
                            nc.vector.tensor_tensor(MX[:, :], MX[:, :], s1, ALU.add).then_inc(small.sem, 1)
                            nc.vector.tensor_copy(S2C[:, index(m), 0, :], s2).then_inc(small.sem, 1)
                            small.reach(dve, m, 2)
                            nc.vector.scalar_tensor_tensor(out=MX[:, :], in0=MX[:, :], scalar=ALPHA, in1=MX[:, :],
                                                           op0=ALU.mult, op1=ALU.max).then_inc(small.sem, 1)
                            nc.vector.tensor_scalar(S2C[:, index(m), 1, :], s2, ALPHA, None, ALU.mult).then_inc(small.sem, 1)
                            small.reach(dve, m, 4)
                            nc.vector.tensor_tensor(RR[:, 0:NT], s1, MX[:, :], ALU.subtract).then_inc(small.sem, 1)
                            nc.vector.scalar_tensor_tensor(out=RR[:, NT:2 * NT], in0=s1, scalar=ALPHA, in1=MX[:, :],
                                                           op0=ALU.mult, op1=ALU.subtract).then_inc(small.sem, 1)
                            small.reach(dve, m, 6)
                    if f and q == 0:
                        x3_in.reach(dve, f, 1)
                        zt_ok.reach(dve, f, 1)
                        nc.vector.tensor_tensor(flat(X3[:, :, :]), flat(X3[:, :, :]), bank2(5), ALU.add).then_inc(y_ok.sem, 1)
                    if f and q == 1:
                        y_ok.reach(dve, f, 1)
                        front_norm.dve_stats(dve, f, 1, X3)
                    if k and q == 6:
                        att_ok.reach(dve, k, 2)
                        settle(dve)
                        nc.vector.reciprocal(REC[:, :], ATT[:, :, D]).then_inc(rec_ok.sem, 1)
                        xr_in.reach(dve, k, 1)
                        rec_ok.reach(dve, k, 1)
                        for t in range(NT):
                            ins = nc.vector.scalar_tensor_tensor(out=XR[:, t, :], in0=ATT[:, t, 0:D], scalar=REC[:, t:t + 1], in1=XR[:, t, :],
                                                                 op0=ALU.mult, op1=ALU.add)
                        ins.then_inc(sum_ok.sem, 1)
                    if k and q == 7:
                        sum_ok.reach(dve, k, 1)
                        back_norm.dve_stats(dve, k, 1, XR)
                dve.sem_inc(v_ok.sem, v_ok.credit)
                turns(dve, step)

            @block.tensor
            def _(pe):
                def sums(b, j):
                    e_ok.reach(pe, b, j + 1)
                    if j == 0:
                        ones_ok.reach(pe, b, 1)
                        att_ok.reach(pe, ahead(b, -1), 2)
                    for t in range(NT):
                        mm = nc.tensor.matmul(att(t), V[j % NV][:, t * P:(t + 1) * P], wh(b, j),
                                              start=(j == 0 and t % 3 == 0), stop=(j == NT - 1), skip_group_check=True)
                    mm.then_inc(att_pe.sem, 1)

                def step(q, c, m, f, k, o):
                    if q < 3 and k:
                        sums(k, NT - 3 + q)
                    if q >= 3 and c:
                        sums(c, q - 3)
                    if f and q == 0:
                        z_ok.reach(pe, f, 1)
                        if later(f, 0):
                            wh_ok.reach(pe, ahead(f, -1), 2)
                        transposes(5, [Z3[:, t * P:(t + 1) * P] for t in range(NT)]).then_inc(zt_ok.sem, 1)
                    if f and q == 4:
                        x3_ok.reach(pe, f, 2)
                        transposes(5, [X3[:, t, :] for t in range(NT)]).then_inc(x3t_ok.sem, 1)
                    if m and q == 5:
                        small.reach(pe, m, 6)
                        nc.tensor.transpose(PS[0:2 * NT, 7, 0:P], RR[:, :], ident[:, :]).then_inc(rr_pe.sem, 1)
                    if f and q == 6:
                        f_lo.reach(pe, f, 1)
                        for h in range(2):
                            hs = slice(h * HALF, (h + 1) * HALF)
                            mm = passes(PS[:, 3 + h, :], A2h[:, 1, :], A2l[:, 1, :], F3h[:, hs], F3l[:, hs], True, True)
                        mm.then_inc(s2_pe.sem, 1)
                        if m:
                            rrt_ok.reach(pe, m, 1)
                        for t in range(NT):
                            ts = slice(t * P, (t + 1) * P)
                            mm = passes(PS[:, 5 + t // 3, (t % 3) * (D + 2):(t % 3 + 1) * (D + 2)], F3h[:, ts], F3l[:, ts], W3h[:, :], W3l[:, :], True, True)
                        mm.then_inc(wh_pe.sem, 1)

                pe.sem_inc(att_pe.sem, att_pe.credit)
                turns(pe, step)
        l3.close()
        late.close()


_INS = ["x", "adj", "L0_gnn_Wg0", "L0_gnn_bg0", "L0_gnn_Wg1", "L0_gnn_bg1", "L0_gnn_Wih", "L0_gnn_Whh", "L0_gnn_bih",
        "L0_gnn_bhh", "L1_gnn_w1_loop", "L1_gnn_w1_neigh", "L1_gnn_b1", "L1_gnn_w2_loop", "L1_gnn_w2_neigh",
        "L1_gnn_b2", "L2_gnn_W1", "L2_gnn_b1", "L2_gnn_g1", "L2_gnn_be1", "L2_gnn_W2", "L2_gnn_b2", "L2_gnn_g2",
        "L2_gnn_be2", "L3_gnn_W", "L3_gnn_a"]


def kernel(**inputs):
    import numpy as _np
    import concourse.bacc as _bacc
    from concourse import mybir as _mybir
    from concourse.bass_utils import run_bass_kernel_spmd as _run

    nc = _bacc.Bacc("TRN2", target_bir_lowering=False, num_devices=1)
    arrays, args = {}, []
    for name in _INS:
        a = _np.ascontiguousarray(inputs[name])
        arrays[f"in_{name}_dram"] = a
        args.append(nc.dram_tensor(f"in_{name}_dram", a.shape, _mybir.dt.from_np(a.dtype), kind="ExternalInput").ap())
    args.append(nc.dram_tensor("out_0_dram", (B, T, D), F32, kind="ExternalOutput").ap())
    program(nc, *args)
    r = _run(nc, [arrays], core_ids=[0])
    return r.results[0]["out_0_dram"]
```

```python
from contextlib import ExitStack

import concourse.bass as bass
from concourse import mybir

P = 128
B, T, D = 8, 1024, 128
NT = T // P
HALF = 512
SKIPS = 4
GATE_I, GATE_F, GATE_G, GATE_O = range(4)
HID = 256
NHC = HID // P
LN_EPS = 1e-5
BN_EPS = 1e-5
ALPHA = 0.2
BLOCKED = -1e30
TPAD = T + 2

F32 = mybir.dt.float32
F32R = mybir.dt.float32r
BF16 = mybir.dt.bfloat16
ALU = mybir.AluOpType
ACT = mybir.ActivationFunctionType
AX_X = mybir.AxisListType.X


def program(nc, x, adj, Wg0, bg0, Wg1, bg1, Wih, Whh, bih, bhh,
            w1_loop, w1_neigh, b1, w2_loop, w2_neigh, b2,
            W1, c1, g1, be1, W2, c2, g2, be2, W3, a3, out):
    root = ExitStack()

    def sb(ctx, name, shape, dt=F32):
        return ctx.enter_context(nc.sbuf_tensor(name, shape, dt))

    def sbr(ctx, name, shape, dt=F32):
        return ctx.enter_context(nc.sbuf_tensor(name, shape, dt, side="right"))

    def sem(name):
        return root.enter_context(nc.semaphore(name))

    with root:
        PS = root.enter_context(nc.psum_tensor("PS", [P, 8, HALF], F32))
        ident = sb(root, "ident", [P, P])
        identr = sb(root, "identr", [P, P], F32R)
        neg_half = sb(root, "neg_half", [P, NT])
        MATS = 6
        Mh = sb(root, "Mh", [P, MATS, D], F32R)
        Ml = sb(root, "Ml", [P, MATS, D], F32R)
        W1Th = sb(root, "W1Th", [P, NHC, P], F32R)
        W1Tl = sb(root, "W1Tl", [P, NHC, P], F32R)
        W2Th = sb(root, "W2Th", [P, NHC, P], F32R)
        W2Tl = sb(root, "W2Tl", [P, NHC, P], F32R)
        W3h = sb(root, "W3h", [P, D + 2], F32R)
        W3l = sb(root, "W3l", [P, D + 2], F32R)
        A2h = sb(root, "A2h", [P, 2, P], F32R)
        A2l = sb(root, "A2l", [P, 2, P], F32R)
        cols = sb(root, "cols", [P, 32])
        dinv = sb(root, "dinv", [P, NT])
        ST = sb(root, "ST", [P, 2, NT, 6])
        MV = sb(root, "MV", [P, 2, NT, 2])
        VE = sb(root, "VE", [P, 2, NT])
        RSTD = sb(root, "RSTD", [P, 2, NT])
        NM = sb(root, "NM", [P, 2, NT])
        SHIFT = sb(root, "SHIFT", [P, 2, NT])
        S1 = sb(root, "S1", [P, NHC, 2 * B, 6])
        S2 = sb(root, "S2", [P, 2 * B, 6])
        bnp = sb(root, "bnp", [P, 3, 6])
        C_B1, C_B2, C_C1, C_G1, C_BE1, C_C2, C_G2, C_BE2 = 0, 1, 2, 4, 6, 8, 9, 10
        C_LSTM = 11
        NROWS = 11

        def col(n):
            return cols[:, n:n + 1]

        def bank2(n):
            return PS[:, n:n + 2, :].rearrange("p a b -> p (a b)")

        passed = sem("passed")

        def settle(eng):
            eng.sem_inc(passed, 1)

        def passes(out_ap, lh, ll, rh, rl, start, stop):
            nc.tensor.matmul(out_ap, lh, rh, start=start, stop=False, skip_group_check=True)
            nc.tensor.matmul(out_ap, lh, rl, start=False, stop=False, skip_group_check=True)
            return nc.tensor.matmul(out_ap, ll, rh, start=False, stop=stop, skip_group_check=True)

        def adj_half(bank, lh, ll, h, stop=True, sources=range(NT)):
            cs = slice(h * HALF, (h + 1) * HALF)
            for st in sources:
                mm = passes(PS[:, bank + h, :], lh[:, st, :], ll[:, st, :], ATh[:, st, cs], ATl[:, st, cs],
                            st == 0, stop and st == NT - 1)
            return mm

        def times_adj(bank, lh, ll, last_terms=None):
            for h in range(2):
                cs = slice(h * HALF, (h + 1) * HALF)
                for st in range(NT):
                    mm = passes(PS[:, bank + h, :], lh[:, st, :], ll[:, st, :], ATh[:, st, cs], ATl[:, st, cs],
                                st == 0, st == NT - 1 and last_terms is None)
                if last_terms is not None:
                    mm = last_terms(bank, h, cs)
            return mm

        def node_major(bank, lh, ll, wh, wl, first=True):
            for st in range(NT):
                o = PS[:, bank + st // 4, (st % 4) * P:(st % 4 + 1) * P]
                mm = passes(o, lh[:, st * P:(st + 1) * P], ll[:, st * P:(st + 1) * P], wh, wl, first, True)
            return mm

        def transposes(bank, blocks):
            for n, block_ap in enumerate(blocks):
                mm = nc.tensor.transpose(PS[:, bank + n // 4, (n % 4) * P:(n % 4 + 1) * P], block_ap, ident[:, :])
            return mm

        dinv_row = sb(root, "dinv_row", [P, T])
        graph = ExitStack()
        ATh = sb(graph, "ATh", [P, NT, T], F32R)
        ATl = sb(graph, "ATl", [P, NT, T], F32R)
        s0 = ExitStack()
        B0 = sb(s0, "B0", [P, T])
        bg1r = sb(s0, "bg1r", [P, HALF], F32R)
        onesr = sb(s0, "onesr", [P, P], F32R)
        XL = sb(s0, "XL", [P, NT, D])
        N0h, N0l = (sb(s0, n, [P, NT, D], F32R) for n in ("N0h", "N0l"))
        lstm = ExitStack()
        WIh = sb(lstm, "WIh", [P, SKIPS, 4, P], F32R)
        WIl = sb(lstm, "WIl", [P, SKIPS, 4, P], F32R)
        WHh = sb(lstm, "WHh", [P, SKIPS - 1, 4, P], F32R)
        WHl = sb(lstm, "WHl", [P, SKIPS - 1, 4, P], F32R)
        s1 = ExitStack()
        NAT = sb(s1, "NAT", [P, NT, T])
        ones = sb(s1, "ones", [P, P])
        STG = sb(s1, "STG", [P, 7, D])
        W1s = sb(s1, "W1s", [P, NHC, P])
        W2s = sb(s1, "W2s", [P, HID])
        a_rows = sb(s1, "a_rows", [P, 2, P])
        wa = sb(s1, "wa", [P, 2])
        bg0_rows = sb(s1, "bg0_rows", [P, D])
        bg0h = sb(s1, "bg0h", [P, D], F32R)
        bg0l = sb(s1, "bg0l", [P, D], F32R)
        bg1s = sb(s1, "bg1s", [1, D])
        bg1hs = sb(s1, "bg1hs", [1, D], F32R)
        bg1lo = sb(s1, "bg1lo", [1, HALF], F32R)
        vecs = sb(s1, "vecs", [16, P])
        lb = sb(s1, "lb", [16, P])
        lb2 = sb(s1, "lb2", [16, P])
        junk = sb(s1, "junk", [P, P])
        ajunk = sb(s1, "ajunk", [P, HALF])
        rsum = sb(s1, "rsum", [P, NT])
        csum = sb(s1, "csum", [P, NT, 2])
        dsum = sb(s1, "dsum", [P, NT])
        deg = sb(s1, "deg", [P, NT])
        diag = sb(s1, "diag", [P, NT, P])
        WIs = sb(s1, "WIs", [P, SKIPS * 4, P])
        WHs = sb(s1, "WHs", [P, (SKIPS - 1) * 4, P])
        NI, NH = SKIPS, SKIPS - 1
        lw_t, lw_hi, lw_lo = (sem(n) for n in ("lw_t", "lw_hi", "lw_lo"))

        adj_in = [sem(f"adj_in{n}") for n in range(NT)]
        mats_in, bg0_in, vec_in, lw_in, konst, dve0, pool0, moved, diagonals = (
            sem(n) for n in ("mats_in", "bg0_in", "vec_in", "lw_in", "konst", "dve0", "pool0", "moved", "diagonals"))
        adj_t, adj_hi, adj_lo, col_sum, row_sum = (sem(n) for n in ("adj_t", "adj_hi", "adj_lo", "col_sum", "row_sum"))
        x0_in, x0_hi, x0_lo = sem("x0_in"), sem("x0_hi"), sem("x0_lo")
        bg0_ok, squares_t, b0_t, row_t = (sem(n) for n in ("bg0_ok", "squares_t", "b0_t", "row_t"))
        PT, PL = 4, 6
        LW_BANKS = (0, 1, 4, 5, 6, 7, 0)

        def row(v):
            return v.rearrange("(a n) -> a n", a=1)

        def adj_block(n):
            return n % NT, n // NT

        with nc.Block() as block:
            @block.sync
            def _(sp):
                for n in range(NT):
                    sp.dma_start(NAT[:, n, :], adj[n * P:(n + 1) * P, :]).then_inc(adj_in[n], 16)
                    if n == 3:
                        sp.dma_start(bg0_rows[:, :], row(bg0).broadcast_to([P, D])).then_inc(bg0_in, 16)
                sp.dma_start(WIs[:, :, :], Wih.rearrange("s (g p) d -> p (s g) d", p=P)).then_inc(lw_in, 16)
                sp.dma_start(WHs[:, :, :], Whh[1:SKIPS].rearrange("s (g p) d -> p (s g) d", p=P)).then_inc(lw_in, 16)
                for n, w in enumerate((Wg0, Wg1, w1_loop, w1_neigh, w2_loop, w2_neigh, W3)):
                    sp.dma_start(STG[:, n, :], w).then_inc(mats_in, 16)
                sp.dma_start(W1s[:, :, :], W1.rearrange("(c p) d -> p c d", p=P)).then_inc(mats_in, 16)
                sp.dma_start(W2s[:, :], W2).then_inc(mats_in, 16)
                for n in range(2):
                    sp.dma_start(a_rows[:, n, :], a3[n * P:(n + 1) * P, :].rearrange("o u -> u o").broadcast_to([P, P])).then_inc(mats_in, 16)
                sp.dma_start(bg1s[:, :], row(bg1)).then_inc(mats_in, 16)
                sp.dma_start(XL[:, :, :], x[0].rearrange("(t p) d -> p t d", p=P)).then_inc(x0_in, 16)
                sp.wait_ge(dve0, 3)
                sp.wait_ge(konst, 7)
                sp.dma_start(bg1r[1:2, :].bitcast(F32), bg1lo[:, :].bitcast(F32)).then_inc(moved, 16)
                sp.wait_ge(moved, 16)

            @block.scalar
            def _(act):
                n = 0
                for v in (b1, b2, c1, g1, be1, c2, g2, be2):
                    k = v.shape[0] // P
                    act.dma_start(vecs[n:n + k, :], v.rearrange("(k p) -> k p", p=P)).then_inc(vec_in, 16)
                    n += k
                act.dma_start(lb[:, :], bih.rearrange("s (g p) -> (s g) p", p=P)).then_inc(vec_in, 16)
                act.dma_start(lb2[:, :], bhh.rearrange("s (g p) -> (s g) p", p=P)).then_inc(vec_in, 16)
                for h in range(2):
                    for n in range(NT * h, NT * h + NT):
                        act.wait_ge(adj_t, n + 1)
                        st, _ = adj_block(n)
                        nc.scalar.activation(ATh[:, st, h * HALF:(h + 1) * HALF], PS[:, n % 8, :], ACT.Copy).then_inc(adj_hi, 1)
                        if n:
                            act.wait_ge(col_sum, n)
                        nc.scalar.activation(ajunk[:, :], PS[:, n % 8, :], ACT.Copy, accum_out=csum[:, st, h:h + 1]).then_inc(col_sum, 1)
                act.wait_ge(col_sum, 2 * NT)
                for n in range(NI + NH):
                    act.wait_ge(lw_t, n + 1)
                    hi = WIh[:, n] if n < NI else WHh[:, n - NI]
                    nc.scalar.activation(hi.rearrange("p g o -> p (g o)"), PS[:, LW_BANKS[n], :], ACT.Copy).then_inc(lw_hi, 1)
                act.wait_ge(x0_in, 16)
                nc.scalar.activation(N0h[:, :, :], XL[:, :, :], ACT.Copy).then_inc(x0_hi, 1)

            @block.gpsimd
            def _(pool):
                nc.gpsimd.memset(ident[:, :], 0.0).then_inc(konst, 1)
                nc.gpsimd.memset(ones[:, :], 1.0).then_inc(konst, 1)
                nc.gpsimd.memset(neg_half[:, :], -0.5).then_inc(konst, 1)
                nc.gpsimd.memset(bg1r[:, :].bitcast(F32), 0.0).then_inc(konst, 1)
                pool.wait_ge(konst, 4)
                nc.gpsimd.affine_select(out=ident[:, :], in_=ident[:, :], compare_op=ALU.not_equal, fill=1.0,
                                        base=0, pattern=[[-1, P]], channel_multiplier=1).then_inc(konst, 1)
                pool.wait_ge(konst, 5)
                nc.gpsimd.tensor_copy(identr[:, :], ident[:, :]).then_inc(konst, 1)
                nc.gpsimd.tensor_copy(onesr[:, :], ones[:, :]).then_inc(konst, 1)
                pool.wait_ge(pool0, 1)
                nc.gpsimd.tensor_tensor(dinv[:, :], deg[:, :], neg_half[:, :], ALU.pow).then_inc(pool0, 1)

            @block.vector
            def _(dve):
                count = [0]

                def done(ins):
                    count[0] += 1
                    ins.then_inc(dve0, 1)
                    dve.wait_ge(dve0, count[0])

                def adj_low(n):
                    dve.wait_ge(adj_hi, n + 1)
                    dve.wait_ge(col_sum, n + 1)
                    st, h = adj_block(n)
                    hs = slice(h * HALF, (h + 1) * HALF)
                    nc.vector.tensor_tensor(ATl[:, st, hs], PS[:, n % 8, :], ATh[:, st, hs].bitcast(F32), ALU.subtract).then_inc(adj_lo, 1)

                dve.wait_ge(konst, 7)
                dve.wait_ge(bg0_in, 16)
                nc.vector.tensor_copy(bg0h[:, :], bg0_rows[:, :]).then_inc(bg0_ok, 1)
                dve.wait_ge(bg0_ok, 1)
                nc.vector.tensor_tensor(bg0l[:, :], bg0_rows[:, :], bg0h[:, :].bitcast(F32), ALU.subtract).then_inc(bg0_ok, 1)
                for h in range(2):
                    for n in range(4 * h, 4 * h + 4):
                        dve.wait_ge(adj_in[n], 16)
                        nc.vector.tensor_reduce(rsum[:, n:n + 1], NAT[:, n, :], AX_X, ALU.add).then_inc(row_sum, 1)
                    for n in range(NT * h, NT * h + NT):
                        adj_low(n)
                dve.wait_ge(adj_lo, 2 * NT)
                dve.wait_ge(mats_in, 16 * 12)
                dve.wait_ge(vec_in, 16 * 10)
                V4 = bg1r[0:1, :].rearrange("p (r d) -> p r d", r=4)
                bg1w = bg1s[:, :].rearrange("p (r d) -> p r d", r=1).broadcast_to([1, 4, D])
                done(nc.vector.tensor_copy(bg1hs[:, :], bg1s[:, :]))
                done(nc.vector.tensor_copy(V4, bg1w))
                done(nc.vector.tensor_tensor(bg1lo[:, :].rearrange("p (r d) -> p r d", r=4), bg1w,
                                             V4.bitcast(F32), ALU.subtract))
                done(nc.vector.tensor_tensor(lb[:, :], lb[:, :], lb2[:, :], ALU.add))
                for n in range(NI + NH):
                    dve.wait_ge(lw_hi, n + 1)
                    hi, lo = (WIh[:, n], WIl[:, n]) if n < NI else (WHh[:, n - NI], WHl[:, n - NI])
                    nc.vector.tensor_tensor(lo.rearrange("p g o -> p (g o)"), PS[:, LW_BANKS[n], :],
                                            hi.rearrange("p g o -> p (g o)").bitcast(F32), ALU.subtract).then_inc(lw_lo, 1)
                dve.wait_ge(x0_hi, 1)
                nc.vector.tensor_tensor(N0l[:, :, :], XL[:, :, :], N0h[:, :, :].bitcast(F32), ALU.subtract).then_inc(x0_lo, 1)
                dve.wait_ge(x0_lo, 1)
                for n in range(NT):
                    done(nc.vector.tensor_tensor_reduce(junk[:, :], NAT[:, n, n * P:(n + 1) * P], ident[:, :], 1.0, 0.0,
                                                        ALU.mult, ALU.add, dsum[:, n:n + 1]))
                dve.wait_ge(row_sum, NT)
                dve.wait_ge(col_sum, 2 * NT)
                done(nc.vector.tensor_tensor(deg[:, :], rsum[:, :], csum[:, :, 0], ALU.add))
                done(nc.vector.tensor_tensor(deg[:, :], deg[:, :], csum[:, :, 1], ALU.add))
                done(nc.vector.scalar_tensor_tensor(out=deg[:, :], in0=deg[:, :], scalar=1.0, in1=dsum[:, :],
                                                    op0=ALU.add, op1=ALU.subtract))
                nc.vector.tensor_copy(junk[:, 0:NT], deg[:, :]).then_inc(pool0, 1)
                done(nc.vector.tensor_copy(Mh[:, :, :], STG[:, 0:MATS, :]))
                done(nc.vector.tensor_tensor(Ml[:, :, :], STG[:, 0:MATS, :], Mh[:, :, :].bitcast(F32), ALU.subtract))
                dve.wait_ge(pool0, 2)
                for n in range(NT):
                    nc.vector.tensor_scalar(diag[:, n, :], ident[:, :], dinv[:, n:n + 1], None, ALU.mult).then_inc(diagonals, 1)
                for n in range(2):
                    done(nc.vector.tensor_tensor_reduce(junk[:, :], STG[:, 6, :], a_rows[:, n, :], 1.0, 0.0,
                                                        ALU.mult, ALU.add, wa[:, n:n + 1]))
                done(nc.vector.tensor_copy(W3h[:, 0:D], STG[:, 6, :]))
                done(nc.vector.tensor_copy(W3h[:, D:D + 2], wa[:, :]))
                done(nc.vector.tensor_tensor(W3l[:, 0:D], STG[:, 6, :], W3h[:, 0:D].bitcast(F32), ALU.subtract))
                done(nc.vector.tensor_tensor(W3l[:, D:D + 2], wa[:, :], W3h[:, D:D + 2].bitcast(F32), ALU.subtract))
                for n in range(2):
                    done(nc.vector.tensor_scalar(A2h[:, n, :], ones[:, :], W3h[:, D + n:D + n + 1].bitcast(F32), None, ALU.mult))
                    done(nc.vector.tensor_scalar(A2l[:, n, :], ones[:, :], W3l[:, D + n:D + n + 1].bitcast(F32), None, ALU.mult))
                dve.wait_ge(squares_t, 1)
                sq = PS[:, 5, :].rearrange("p (c d) -> p c d", c=4)
                done(nc.vector.tensor_copy(W1Th[:, :, :], sq[:, 0:2, :]))
                done(nc.vector.tensor_tensor(W1Tl[:, :, :], sq[:, 0:2, :], W1Th[:, :, :].bitcast(F32), ALU.subtract))
                done(nc.vector.tensor_copy(W2Th[:, :, :], sq[:, 2:4, :]))
                done(nc.vector.tensor_tensor(W2Tl[:, :, :], sq[:, 2:4, :], W2Th[:, :, :].bitcast(F32), ALU.subtract))
                done(nc.vector.tensor_copy(cols[:, 0:NROWS], PS[:, 4, 0:NROWS]))
                done(nc.vector.tensor_copy(cols[:, C_LSTM:C_LSTM + 16], PS[:, 4, 16:32]))
                done(nc.vector.tensor_scalar(col(C_B2), col(C_B2), 0.5, None, ALU.mult))
                dve.wait_ge(b0_t, 1)
                nc.vector.tensor_copy(B0[:, :], bank2(2)).then_inc(dve0, 1)
                dve.wait_ge(row_t, 1)
                nc.vector.tensor_copy(dinv_row[:, :], bank2(0)).then_inc(dve0, 1)
                dve.wait_ge(dve0, count[0] + 2)

            @block.tensor
            def _(pe):
                def weights(n):
                    for k in range(4):
                        src = WIs[:, 4 * n + k, :] if n < NI else WHs[:, 4 * (n - NI) + k, :]
                        mm = nc.tensor.transpose(PS[:, LW_BANKS[n], k * P:(k + 1) * P], src, ident[:, :])
                    mm.then_inc(lw_t, 1)

                pe.wait_ge(konst, 7)
                for n in range(2 * NT):
                    st, h = adj_block(n)
                    if st == 0:
                        for k in range(4):
                            pe.wait_ge(adj_in[4 * h + k], 16)
                    if n >= 8:
                        pe.wait_ge(col_sum, n - 8 + 1)
                        pe.wait_ge(adj_lo, n - 8 + 1)
                    for k in range(4):
                        mm = nc.tensor.transpose(PS[:, n % 8, k * P:(k + 1) * P],
                                                 NAT[:, 4 * h + k, st * P:(st + 1) * P], ident[:, :])
                    mm.then_inc(adj_t, 1)
                pe.wait_ge(lw_in, 32)
                pe.wait_ge(adj_lo, 2 * NT)
                pe.wait_ge(col_sum, 2 * NT)
                for n in range(NI + NH - 1):
                    weights(n)
                pe.wait_ge(bg0_ok, 2)

                def bg0_adj(h):
                    hs = slice(h * HALF, (h + 1) * HALF)
                    for st in range(NT):
                        mm = passes(PS[:, 2 + h, :], bg0h[:, :], bg0l[:, :], ATh[:, st, hs], ATl[:, st, hs], st == 0, st == NT - 1)
                    return mm
                bg0_adj(0)
                pe.wait_ge(lw_lo, 1)
                weights(NI + NH - 1)
                pe.wait_ge(lw_lo, NI + NH - 1)
                pe.wait_ge(mats_in, 16 * 12)
                pe.wait_ge(dve0, 4)
                for c in range(NHC):
                    nc.tensor.transpose(PS[:, 5, c * P:(c + 1) * P], W1s[:, c, :], ident[:, :])
                    nc.tensor.transpose(PS[:, 5, (2 + c) * P:(3 + c) * P], W2s[:, c * P:(c + 1) * P], ident[:, :])
                nc.tensor.transpose(PS[:, 4, 0:NROWS], vecs[0:NROWS, :], ident[0:NROWS, 0:NROWS])
                nc.tensor.transpose(PS[:, 4, 16:32], lb[:, :], ident[0:16, 0:16]).then_inc(squares_t, 1)
                bg0_adj(1).then_inc(b0_t, 1)
                pe.wait_ge(x0_lo, 1)
                for h in range(2):
                    adj_half(PL, N0h, N0l, h)
                pe.wait_ge(lw_lo, NI + NH)
                pe.wait_ge(diagonals, NT)
                for h in range(2):
                    mm = nc.tensor.matmul(PS[:, h, :], ones[:, :], diag[:, 4 * h:4 * h + 4, :], start=True, stop=True)
                mm.then_inc(row_t, 1)
        s1.close()

        class Signal:

            def __init__(self, name, n, unit=1, credit=0):
                self.sem, self.n, self.unit, self.credit = sem(name), n, unit, credit

            def reach(self, eng, b, k):
                i, plus, mul = b if len(b) == 3 else (*b, 1)
                eng.wait_ge(self.sem, i * (mul * self.n * self.unit) + ((plus * self.n + k) * self.unit + self.credit))

        class Norm:

            def __init__(self, name, n, slot):
                self.n, self.slot = n, slot
                self.stats, self.var, self.eps, self.rstd, self.shift = (
                    Signal(f"{name}_{k}", n) for k in ("stats", "var", "eps", "rstd", "shift"))
                self.finished = [Signal(f"{name}_finished{k}", 1) for k in range(n)]

            def done(self, eng, b, k):
                self.finished[k - 1].reach(eng, b, 1)

            def dve_stats(self, dve, b, k, rows):
                s = self.slot + k - 1
                settle(dve)
                for t in range(NT):
                    ins = nc.vector.bn_stats(ST[:, s, t, :], rows[:, t, :])
                ins.then_inc(self.stats.sem, 1)
                self.stats.reach(dve, b, k)
                settle(dve)
                for t in range(NT):
                    ins = nc.vector.bn_aggr(MV[:, s, t, :], ST[:, s, t, :])
                ins.then_inc(self.var.sem, 1)

            def scale(self, eng, engine, b, k, rows, to):
                s = self.slot + k - 1
                self.rstd.reach(eng, b, k)
                if engine is nc.gpsimd:
                    settle(eng)
                for t in range(NT):
                    ins = engine.tensor_scalar(to[:, t, :], rows[:, t, :], MV[:, s, t, 0:1], RSTD[:, s, t:t + 1],
                                               ALU.subtract, ALU.mult)
                ins.then_inc(self.finished[k - 1].sem, 1)

            def act_scale(self, act, b, k, rows, to, signal, half):
                s = self.slot + k - 1
                if half == 0:
                    self.shift.reach(act, b, k)
                for t in range(half * NT // 2, (half + 1) * NT // 2):
                    ins = nc.scalar.activation(to[:, t, :], rows[:, t, :], ACT.Identity,
                                               bias=SHIFT[:, s, t:t + 1], scale=RSTD[:, s, t:t + 1])
                ins.then_inc(signal, 1)

            def pool(self, pool, b, k, shifts=False):
                s = self.slot + k - 1
                self.var.reach(pool, b, k)
                settle(pool)
                if shifts:
                    nc.gpsimd.tensor_scalar(NM[:, s, :], MV[:, s, :, 0], -1.0, None, ALU.mult)
                nc.gpsimd.tensor_scalar(VE[:, s, :], MV[:, s, :, 1], LN_EPS, None, ALU.add).then_inc(self.eps.sem, 1)
                self.eps.reach(pool, b, k)
                nc.gpsimd.tensor_tensor(RSTD[:, s, :], VE[:, s, :], neg_half[:, :], ALU.pow).then_inc(self.rstd.sem, 1)
                if shifts:
                    self.rstd.reach(pool, b, k)
                    nc.gpsimd.tensor_tensor(SHIFT[:, s, :], NM[:, s, :], RSTD[:, s, :], ALU.mult).then_inc(self.shift.sem, 1)

        def flat(t):
            return t.rearrange("p a b -> p (a b)")

        def tiles(t):
            return t[:, :].rearrange("p (t d) -> p t d", t=NT)

        x1_dram = nc.dram_tensor("x1_dram", (B, P, NT * D), F32, kind="Internal").ap()
        fused = ExitStack()
        F0h, F0l = (sb(fused, n, [P, T], F32R) for n in ("F0h", "F0l"))
        Z0 = sb(fused, "Z0", [P, T])
        HN = sb(fused, "HN", [P, TPAD])
        XN = sb(fused, "XN", [P, NT, D])
        N1h, N1l = (sb(fused, n, [P, NT, D], F32R) for n in ("N1h", "N1l"))
        F1h, F1l = (sb(fused, n, [P, T], F32R) for n in ("F1h", "F1l"))
        Z1 = sb(fused, "Z1", [P, T])
        HT = sb(fused, "HT", [P, TPAD])
        XSh, XSl = (sb(fused, n, [P, TPAD], F32R) for n in ("XSh", "XSl"))
        HRh, HRl = (sb(fused, n, [P, HALF], F32R) for n in ("HRh", "HRl"))
        gates = [sb(fused, f"gate{k}", [P, HALF]) for k in range(4)]
        C, IG, TC, HS = (sb(fused, n, [P, HALF]) for n in ("C", "IG", "TC", "HS"))

        UNITS = [(1, 0, 0, HALF), (1, 0, HALF, HALF)]
        UNITS += [(p, k, 0, n) for p, n in ((2, T // 2), (3, TPAD // 3), (4, T // 4)) for k in range(p)]
        NU = len(UNITS)

        def gates_of(k):
            return (GATE_I, GATE_G, GATE_F, GATE_O) if k else (GATE_I, GATE_G, GATE_O)

        NGATES = sum(len(gates_of(k)) for _, k, _, _ in UNITS)
        NSTATES = sum(k < p - 1 for p, k, _, _ in UNITS)
        NSUMS = sum(k > 0 for _, k, _, _ in UNITS)
        GATES_BEFORE = [sum(len(gates_of(k)) for _, k, _, _ in UNITS[:u]) for u in range(NU + 1)]
        STATES_BEFORE = [sum(k < p - 1 for p, k, _, _ in UNITS[:u]) for u in range(NU + 1)]
        SUMS_BEFORE = [sum(k > 0 for _, k, _, _ in UNITS[:u]) for u in range(NU + 1)]

        xl_in = Signal("xl_in", 1, 16)
        xn_in = Signal("xn_in", 1, 16)
        x1_out = Signal("x1_out", 1, 16)
        pl = Signal("lead_pe", 4)
        al = Signal("lead_act", 4)
        dl = Signal("lead_dve", 4)
        px = Signal("lead_x", 1)
        pxh = Signal("lead_xh", 1)
        pt = Signal("trail_pe", 7)
        at = Signal("trail_act", 6)
        dt_ = Signal("trail_dve", 5)
        y2 = Signal("trail_y2", 1)
        xs_h = Signal("xs_h", SKIPS)
        xs_ok = Signal("xs_ok", SKIPS)
        gate_ok = Signal("gate_ok", NGATES)
        gate_read = Signal("gate_read", NGATES)
        fc_ok = Signal("fc_ok", NSUMS)
        cell_ok = Signal("cell_ok", NU)
        tanh_ok = Signal("tanh_ok", NU)
        h_ok = Signal("h_ok", NU)
        hr_h = Signal("hr_h", NSTATES)
        state_ok = Signal("state_ok", NSTATES)

        def later(b, u):
            return u > 0 or not isinstance(b[0], int) or b[0] + b[1] > 0

        def pe_lead_adj_x(pe, g, h, sources=range(NT)):
            if h == 0 and 0 in sources:
                px.reach(pe, g, 1)
                if later(g, 0):
                    al.reach(pe, (g[0], g[1] - 1), 4)
            mm = adj_half(PL, N0h, N0l, h, sources=sources)
            if h == 1:
                mm.then_inc(pl.sem, 1)

        def pe_lead_wg0(pe, g):
            dl.reach(pe, g, 1)
            for h in range(2):
                hs = slice(h * HALF, (h + 1) * HALF)
                mm = passes(PS[:, PL + h, :], Mh[:, 0, :], Ml[:, 0, :], F0h[:, hs], F0l[:, hs], True, True)
            mm.then_inc(pl.sem, 1)

        def pe_lead_wg1(pe, g):
            dl.reach(pe, g, 3)
            for h in range(2):
                nc.tensor.matmul(PS[:, PL + h, :], onesr[:, :], bg1r[:, :], start=True, stop=False, skip_group_check=True)
            node_major(PL, F0h, F0l, Mh[:, 1, :], Ml[:, 1, :], first=False).then_inc(pl.sem, 1)

        def pe_lead_adj(pe, g, h):
            if h == 0:
                dl.reach(pe, g, 4)
            mm = adj_half(PL, N0h, N0l, h)
            if h == 1:
                mm.then_inc(pl.sem, 1)

        def pe_trail_ht(pe, l):
            h_ok.reach(pe, l, NU)
            y2.reach(pe, l, 1)
            transposes(PT, [HT[:, t * P:(t + 1) * P] for t in range(NT)]).then_inc(pt.sem, 1)

        def pe_trail_x1(pe, l):
            norm.done(pe, l, 1)
            transposes(PT, [XN[:, t, :] for t in range(NT)]).then_inc(pt.sem, 1)

        def pe_trail_neigh(pe, l, layer):
            dt_.reach(pe, l, (2, 4)[layer])
            node_major(PT, F1h, F1l, Mh[:, 3 + 2 * layer, :], Ml[:, 3 + 2 * layer, :]).then_inc(pt.sem, 1)

        def pe_trail_conv(pe, l, layer, first, last):
            for h in range(2):
                sources = range(max(first, h * NT) - h * NT, min(last, h * NT + NT - 1) - h * NT + 1)
                if 0 in sources and h == 0:
                    dt_.reach(pe, l, (3, 5)[layer])
                if sources:
                    adj_half(PT, N1h, N1l, h, stop=False, sources=sources)
                if NT - 1 in sources:
                    hs = slice(h * HALF, (h + 1) * HALF)
                    mm = passes(PS[:, PT + h, :], Mh[:, 2 + 2 * layer, :], Ml[:, 2 + 2 * layer, :], F1h[:, hs], F1l[:, hs], False, True)
            if last == 2 * NT - 1:
                mm.then_inc(pt.sem, 1)

        def pe_trail_back(pe, l):
            at.reach(pe, l, 6)
            transposes(PT, [Z1[:, t * P:(t + 1) * P] for t in range(NT)]).then_inc(pt.sem, 1)

        def pe_unit(pe, b, u):
            p, k, w0, n = UNITS[u]
            if k == 0 and w0 == 0:
                xs_ok.reach(pe, b, p)
            if later(b, u):
                gate_read.reach(pe, b, GATES_BEFORE[u])
            c0 = k * n + w0
            for g in gates_of(k):
                mm = passes(PS[:, g, 0:n], WIh[:, p - 1, g], WIl[:, p - 1, g], XSh[:, c0:c0 + n], XSl[:, c0:c0 + n], True, k == 0)
                if k == 0:
                    mm.then_inc(gate_ok.sem, 1)
            if k:
                state_ok.reach(pe, b, STATES_BEFORE[u])
                for g in gates_of(k):
                    passes(PS[:, g, 0:n], WHh[:, p - 2, g], WHl[:, p - 2, g], HRh[:, 0:n], HRl[:, 0:n], False, True)\
                        .then_inc(gate_ok.sem, 1)

        def pe_fill(pe, u, g, l):
            if u == 0:
                if g:
                    pe_lead_adj_x(pe, g, 0, range(2))
                if l:
                    pe_trail_ht(pe, l)
            if g and u == 1:
                pe_lead_adj_x(pe, g, 0, range(2, NT))
                pe_lead_adj_x(pe, g, 1)
            if u == 2:
                if g:
                    pe_lead_wg0(pe, g)
                if l:
                    pe_trail_x1(pe, l)
            if u == 3:
                if l:
                    pe_trail_neigh(pe, l, 0)
                if g:
                    pe_lead_wg1(pe, g)
                if l:
                    pe_trail_conv(pe, l, 0, 0, 7)
            if l and u == 4:
                pe_trail_conv(pe, l, 0, 8, 15)
            if g and u == 5:
                pe_lead_adj(pe, g, 0)
            if u == 6:
                if l:
                    pe_trail_neigh(pe, l, 1)
                if g:
                    pe_lead_adj(pe, g, 1)
            if l and u in (7, 8, 9):
                pe_trail_conv(pe, l, 1, *((0, 5), (6, 10), (11, 15))[u - 7])
            if l and u == 10:
                pe_trail_back(pe, l)

        def act_unit(act, b, u):
            p, k, w0, n = UNITS[u]
            if later(b, u):
                h_ok.reach(act, b, u)
            for j, g in enumerate(gates_of(k)):
                gate_ok.reach(act, b, GATES_BEFORE[u] + j + 1)
                nc.scalar.activation(gates[g][:, 0:n], PS[:, g, 0:n], ACT.Tanh if g == GATE_G else ACT.Sigmoid,
                                     bias=col(C_LSTM + 4 * (p - 1) + g)).then_inc(gate_read.sem, 1)
            cell_ok.reach(act, b, u + 1)
            nc.scalar.activation(TC[:, 0:n], C[:, 0:n], ACT.Tanh).then_inc(tanh_ok.sem, 1)

        def act_fill(act, u, g, l):
            if g and u == 1:
                pl.reach(act, g, 1)
                nc.scalar.activation(F0h[:, :], bank2(PL), ACT.Copy).then_inc(al.sem, 1)
            if u == 2:
                if l:
                    pt.reach(act, l, 2)
                    nc.scalar.activation(F1h[:, :], bank2(PT), ACT.Copy).then_inc(at.sem, 1)
                if g:
                    dl.reach(act, g, 2)
                    nc.scalar.activation(F0h[:, :], Z0[:, :], ACT.Relu).then_inc(al.sem, 1)
            if u == 3:
                if l:
                    pt.reach(act, l, 3)
                    nc.scalar.activation(flat(N1h[:, :, :]), bank2(PT), ACT.Copy).then_inc(at.sem, 1)
                if g:
                    pl.reach(act, g, 3)
                    nc.scalar.activation(flat(N0h[:, :, :]), bank2(PL), ACT.Copy).then_inc(al.sem, 1)
            if l and u == 4:
                pt.reach(act, l, 4)
                x1_out.reach(act, l, 1)
                nc.scalar.activation(F1h[:, :], bank2(PT), ACT.Relu, bias=col(C_B1)).then_inc(at.sem, 1)
                nc.scalar.activation(Z1[:, :], bank2(PT), ACT.Relu, bias=col(C_B1)).then_inc(at.sem, 1)
            if u == 6:
                if l:
                    pt.reach(act, l, 5)
                    nc.scalar.activation(flat(N1h[:, :, :]), bank2(PT), ACT.Copy).then_inc(at.sem, 1)
                if g:
                    pl.reach(act, g, 4)
                    nc.scalar.activation(HN[:, 0:T], bank2(PL), ACT.Relu).then_inc(al.sem, 1)
            if l and u == 9:
                pt.reach(act, l, 6)
                nc.scalar.activation(Z1[:, :], bank2(PT), ACT.Relu, bias=col(C_B2), scale=0.5).then_inc(at.sem, 1)

        def dve_inputs(dve, b, p, n):
            src = (HN if p == 1 else HT)[:, 0:p * n].rearrange("q (w k) -> q k w", k=p)
            hi, lo = (t[:, 0:p * n].rearrange("q (k w) -> q k w", k=p) for t in (XSh, XSl))
            nc.vector.tensor_copy(hi, src).then_inc(xs_h.sem, 1)
            xs_h.reach(dve, b, p)
            nc.vector.tensor_tensor(lo, src, hi.bitcast(F32), ALU.subtract).then_inc(xs_ok.sem, 1)

        def dve_unit(dve, b, u, l):
            p, k, w0, n = UNITS[u]
            gi, gf, gg, go = (gates[g][:, 0:n] for g in (GATE_I, GATE_F, GATE_G, GATE_O))
            c, ig, tc, hs = (t[:, 0:n] for t in (C, IG, TC, HS))
            gate_read.reach(dve, b, GATES_BEFORE[u] + 2)
            if k == 0:
                nc.vector.tensor_tensor(c, gi, gg, ALU.mult).then_inc(cell_ok.sem, 1)
            else:
                nc.vector.tensor_tensor(ig, gi, gg, ALU.mult)
                gate_read.reach(dve, b, GATES_BEFORE[u] + 3)
                nc.vector.tensor_tensor(c, gf, c, ALU.mult).then_inc(fc_ok.sem, 1)
                fc_ok.reach(dve, b, SUMS_BEFORE[u] + 1)
                nc.vector.tensor_tensor(c, c, ig, ALU.add).then_inc(cell_ok.sem, 1)
            if l and u == 0:
                pt.reach(dve, l, 1)
            tanh_ok.reach(dve, b, u + 1)
            if k == p - 1:
                m = min(n, T // p)
                dst = HT[:, w0:w0 + n] if p == 1 else HT[:, 0:m * p].rearrange("q (w k) -> q w k", k=p)[:, :, k]
                nc.vector.tensor_tensor(dst, go[:, 0:m], tc[:, 0:m], ALU.mult).then_inc(h_ok.sem, 1)
            else:
                nc.vector.tensor_tensor(hs, go, tc, ALU.mult).then_inc(h_ok.sem, 1)
                h_ok.reach(dve, b, u + 1)
                nc.vector.tensor_copy(HRh[:, 0:n], hs).then_inc(hr_h.sem, 1)
                hr_h.reach(dve, b, STATES_BEFORE[u] + 1)
                nc.vector.tensor_tensor(HRl[:, 0:n], hs, HRh[:, 0:n].bitcast(F32), ALU.subtract).then_inc(state_ok.sem, 1)

        def dve_next_inputs(dve, b, u):
            p, k, w0, n = UNITS[u]
            if k == p - 1 and p < SKIPS and (p > 1 or w0):
                h_ok.reach(dve, b, u + 1)
                dve_inputs(dve, b, p + 1, UNITS[u + 1][3])

        def dve_low(lo, full, hi):
            return nc.vector.tensor_tensor(lo, full, hi.bitcast(F32), ALU.subtract)

        def dve_fill(dve, u, g, l):
            if l and u == 0:
                xn_in.reach(dve, l, 1)
                pt.reach(dve, l, 1)
                nc.vector.tensor_tensor(flat(XN[:, :, :]), flat(XN[:, :, :]), bank2(PT), ALU.add).then_inc(dt_.sem, 1)
            if u == 1:
                if l:
                    dt_.reach(dve, l, 1)
                    norm.dve_stats(dve, l, 1, XN)
                if g:
                    al.reach(dve, g, 1)
                    dve_low(F0l[:, :], bank2(PL), F0h[:, :]).then_inc(dl.sem, 1)
                if l:
                    norm.scale(dve, nc.vector, l, 1, XN, XN)
            if u == 2:
                if g:
                    pl.reach(dve, g, 2)
                    nc.vector.tensor_tensor(Z0[:, :], bank2(PL), B0[:, :], ALU.add).then_inc(dl.sem, 1)
                if l:
                    at.reach(dve, l, 1)
                    dve_low(F1l[:, :], bank2(PT), F1h[:, :]).then_inc(dt_.sem, 1)
                if g:
                    al.reach(dve, g, 2)
                    nc.vector.scalar_tensor_tensor(out=F0l[:, :], in0=Z0[:, :], scalar=0.0, in1=F0h[:, :].bitcast(F32),
                                                   op0=ALU.max, op1=ALU.subtract).then_inc(dl.sem, 1)
            if u == 3:
                if l:
                    at.reach(dve, l, 2)
                    dve_low(flat(N1l[:, :, :]), bank2(PT), flat(N1h[:, :, :])).then_inc(dt_.sem, 1)
                if g:
                    al.reach(dve, g, 3)
                    dve_low(flat(N0l[:, :, :]), bank2(PL), flat(N0h[:, :, :])).then_inc(dl.sem, 1)
            if l and u == 4:
                at.reach(dve, l, 4)
                dve_low(F1l[:, :], Z1[:, :], F1h[:, :]).then_inc(dt_.sem, 1)
            if l and u == 6:
                at.reach(dve, l, 5)
                dve_low(flat(N1l[:, :, :]), bank2(PT), flat(N1h[:, :, :])).then_inc(dt_.sem, 1)
            if l and u == 10:
                pt.reach(dve, l, 7)
                nc.vector.scalar_tensor_tensor(out=Z1[:, :], in0=flat(XN[:, :, :]), scalar=1.5, in1=bank2(PT),
                                               op0=ALU.mult, op1=ALU.add).then_inc(y2.sem, 1)
                y2.reach(dve, l, 2)
                norm.dve_stats(dve, l, 2, tiles(Z1))

        x2_in = [sem(f"x2_in{s}") for s in range(2)]
        y_hi, y_lo = Signal("y_hi", 1), Signal("y_lo", 1)
        diag_in, diag_hi, diag_ok = sem("diag_in"), sem("diag_hi"), sem("diag_ok")
        agg_ok = Signal("agg_ok", 1)
        AGG = (PL, 0)

        def y_high(act, b, s, pair, X2, Yh):
            act.wait_ge(x2_in[s], pair * 16 + 16)
            for t in range(NT):
                ins = nc.scalar.activation(Yh[:, t, :], X2[:, t, :], ACT.Copy, scale=dinv[:, t:t + 1])
            ins.then_inc(y_hi.sem, 1)

        def y_low(dve, b, s, X2, Yh, Yl):
            y_hi.reach(dve, b, 1)
            for t in range(NT):
                ins = nc.vector.scalar_tensor_tensor(out=Yl[:, t, :], in0=X2[:, t, :], scalar=dinv[:, t:t + 1],
                                                     in1=Yh[:, t, :].bitcast(F32), op0=ALU.mult, op1=ALU.subtract)
            ins.then_inc(y_lo.sem, 1)

        def pe_early_agg(pe, s, hi, lo, h):
            if h == 0:
                y_lo.reach(pe, (s, 0), 1)
            adj_half(AGG[s], hi, lo, h, stop=False)
            for t in range(4 * h, 4 * h + 4):
                o = PS[:, AGG[s] + h, (t % 4) * P:(t % 4 + 1) * P]
                nc.tensor.matmul(o, hi[:, t, :], identr[:, :], start=False, stop=False, skip_group_check=True)
                mm = nc.tensor.matmul(o, lo[:, t, :], identr[:, :], start=False, stop=t % 4 == 3, skip_group_check=True)
            if h == 1:
                mm.then_inc(agg_ok.sem, 1)

        norm = Norm("norm", 2, 0)
        with nc.Block() as block:
            @block.tensor
            def _(pe):
                def batch(b, g, l):
                    for u in range(NU):
                        pe_unit(pe, b, u)
                        pe_fill(pe, u, g, l)
                        if g is None and u in (1, 6):
                            pe_early_agg(pe, 0, N0h, N0l, u // 6)

                pe.sem_inc(pl.sem, 1)
                for u in range(2, NU):
                    pe_fill(pe, u, (0, 0), None)
                batch((0, 0), (0, 1), None)
                with pe.Fori(1, B - 1) as i:
                    batch((i, 0), (i, 1), (i, -1))
                batch((B - 1, 0), None, (B - 1, -1))
                for u in range(NU):
                    pe_fill(pe, u, None, (B - 1, 0))
                    if u == 0:
                        gate_read.reach(pe, (B - 1, 0), NGATES)
                        for h in range(2):
                            pe_early_agg(pe, 1, tiles(F0h), tiles(F0l), h)

            @block.scalar
            def _(act):
                nc.scalar.preload_act_table(ACT.Sigmoid)
                act.sem_inc(x1_out.sem, 16)

                def batch(b, g, l, last_lead=False):
                    for u in range(NU):
                        act_unit(act, b, u)
                        act_fill(act, u, g, l)
                        if last_lead and u == 8:
                            y_high(act, (0, 0, 1), 0, 0, XL, N0h)
                        if g is None and u == 3:
                            y_high(act, (1, 0, 1), 1, 0, tiles(Z0), tiles(F0h))

                for u in range(NU):
                    act_fill(act, u, (0, 0), None)
                batch((0, 0), (0, 1), None)
                with act.Fori(1, B - 2) as i:
                    batch((i, 0), (i, 1), (i, -1))
                batch((B - 2, 0), (B - 1, 0), (B - 3, 0), last_lead=True)
                batch((B - 1, 0), None, (B - 1, -1))
                for u in range(NU):
                    act_fill(act, u, None, (B - 1, 0))

            @block.vector
            def _(dve):
                def next_inputs(b, g):
                    if b:
                        gate_ok.reach(dve, b, GATES_BEFORE[NU - 1] + 1)
                    al.reach(dve, g, 4)
                    dve_inputs(dve, g, 1, T)

                def batch(b, g, l, last_lead=False):
                    for u in range(NU):
                        if g and u == NU - 1:
                            next_inputs(b, g)
                        dve_unit(dve, b, u, l)
                        if u in (1, 6):
                            dve_next_inputs(dve, b, u)
                        dve_fill(dve, u, g, l)
                        if u not in (1, 6):
                            dve_next_inputs(dve, b, u)
                        if last_lead and u == 9:
                            y_low(dve, (0, 0, 1), 0, XL, N0h, N0l)
                        if g is None and u == 4:
                            y_low(dve, (1, 0, 1), 1, tiles(Z0), tiles(F0h), tiles(F0l))

                nc.vector.memset(HT[:, T:TPAD], 0.0)
                dve.sem_inc(y2.sem, 1)
                for u in range(NU):
                    dve_fill(dve, u, (0, 0), None)
                next_inputs(None, (0, 0))
                batch((0, 0), (0, 1), None)
                with dve.Fori(1, B - 2) as i:
                    batch((i, 0), (i, 1), (i, -1))
                batch((B - 2, 0), (B - 1, 0), (B - 3, 0), last_lead=True)
                batch((B - 1, 0), None, (B - 1, -1))
                for u in range(NU):
                    dve_fill(dve, u, None, (B - 1, 0))
                norm.scale(dve, nc.vector, (B - 1, 0), 2, tiles(Z1), tiles(Z1))
                y_lo.reach(dve, (1, 0), 1)
                agg_ok.reach(dve, (1, 0), 1)
                def blocks(t):
                    v = flat(t[:, :, :])
                    w = T + P
                    return [(v[:, 0:(NT - 1) * w].rearrange("p (t w) -> p t w", w=w)[:, :, 0:P], slice(0, NT - 1)),
                            (v[:, NT * T - P:NT * T].rearrange("p (t w) -> p t w", w=P), slice(NT - 1, NT))]
                DG = Z0[:, :].rearrange("p (t w) -> p t w", w=P)
                both = list(zip(blocks(ATh), blocks(ATl)))
                for (hi, ts), (lo, _) in both:
                    nc.vector.tensor_tensor(DG[:, ts], hi.bitcast(F32), lo.bitcast(F32), ALU.add).then_inc(diag_in, 1)
                dve.wait_ge(diag_in, 2)
                nc.vector.tensor_tensor(DG, DG, ident[:, :].rearrange("p (o w) -> p o w", o=1).broadcast_to([P, NT, P]), ALU.add).then_inc(diag_in, 1)
                dve.wait_ge(diag_in, 3)
                for (hi, ts), _ in both:
                    nc.vector.tensor_copy(hi, DG[:, ts]).then_inc(diag_hi, 1)
                dve.wait_ge(diag_hi, 2)
                for (hi, ts), (lo, _) in both:
                    nc.vector.tensor_tensor(lo, DG[:, ts], hi.bitcast(F32), ALU.subtract).then_inc(diag_ok, 1)
                dve.wait_ge(diag_ok, 2)


            @block.gpsimd
            def _(pool):
                def split_x(g):
                    xl_in.reach(pool, g, 1)
                    if later(g, 0):
                        pl.reach(pool, (g[0], g[1] - 1), 4)
                    settle(pool)
                    nc.gpsimd.tensor_copy(flat(N0h[:, :, :]), flat(XL[:, :, :])).then_inc(pxh.sem, 1)
                    pxh.reach(pool, g, 1)
                    nc.gpsimd.tensor_tensor(flat(N0l[:, :, :]), flat(XL[:, :, :]), flat(N0h[:, :, :]).bitcast(F32),
                                            ALU.subtract).then_inc(px.sem, 1)

                def second_scale(l):
                    norm.scale(pool, nc.gpsimd, l, 2, tiles(Z1), tiles(Z1))

                pool.sem_inc(pxh.sem, 1)
                pool.sem_inc(px.sem, 1)
                for g in range(1, 3):
                    split_x((g, 0))
                norm.pool(pool, (0, 0), 1)
                split_x((3, 0))
                norm.pool(pool, (0, 0), 2)
                with pool.Fori(2, B - 2) as i:
                    norm.pool(pool, (i, -1), 1)
                    second_scale((i, -2))
                    split_x((i, 2))
                    norm.pool(pool, (i, -1), 2)
                for l in range(B - 3, B):
                    norm.pool(pool, (l, 0), 1)
                    second_scale((l - 1, 0))
                    norm.pool(pool, (l, 0), 2)

            @block.sync
            def _(sp):
                def load_lead(g):
                    sp.dma_start(XL[:, :, :], x[g].rearrange("(t p) d -> p t d", p=P)).then_inc(xl_in.sem, 16)

                def load_trail(l):
                    sp.dma_start(XN[:, :, :], x[l].rearrange("(t p) d -> p t d", p=P)).then_inc(xn_in.sem, 16)

                def store(l, at_):
                    norm.done(sp, l, 2)
                    sp.dma_start(x1_dram[at_], Z1[:, :]).then_inc(x1_out.sem, 16)

                sp.sem_inc(xl_in.sem, 16)
                load_trail(0)
                for g in range(2):
                    px.reach(sp, (g, 0), 1)
                    load_lead(g + 1)
                with sp.Fori(0, B - 3) as l:
                    px.reach(sp, (l, 2), 1)
                    load_lead(l + 3)
                    y2.reach(sp, (l, 0), 2)
                    load_trail(l + 1)
                    store((l, 0), l)
                pl.reach(sp, (B - 1, 0), 1)
                sp.dma_start(flat(XL[:, :, :]), x1_dram[0]).then_inc(x2_in[0], 16)
                dl.reach(sp, (B - 1, 0), 3)
                sp.dma_start(Z0[:, :], x1_dram[1]).then_inc(x2_in[1], 16)
                for l in range(B - 3, B):
                    if l < B - 1:
                        y2.reach(sp, (l, 0), 2)
                        load_trail(l + 1)
                    store((l, 0), l)
                sp.wait_ge(x1_out.sem, 16 * (B + 1))
                sp.wait_ge(x2_in[0], 16)
                sp.wait_ge(x2_in[1], 16)
        fused.close()
        lstm.close()
        late = ExitStack()
        TW = NT * (D + 2)
        HW = sbr(late, "HW", [P, B, TW])
        PENT = sbr(late, "PENT", [P, NT, T], BF16)
        l2 = ExitStack()
        HP1 = sb(l2, "HP1", [P, B, T])
        l2a = ExitStack()
        X2 = [XL, sb(l2a, "x2", [P, NT, D])]
        Yh, Yl = ([first, sb(l2a, n, [P, NT, D], F32R)] for n, first in (("Yh", N0h), ("Yl", N0l)))
        Ah, Al = (sb(l2a, n, [P, T], F32R) for n in ("Ah", "Al"))
        ZZ = B0
        zz_ok, a_hi, a_lo = Signal("zz_ok", 1), Signal("a_hi", 1), Signal("a_lo", 1)
        w1_ok = Signal("w1_ok", NHC)
        hid_ok = Signal("hid_ok", NHC)
        hid_read = sem("hid_read")
        pent_ok = sem("pent_ok")

        def hidden(c, b):
            return HW[:, b, 0:T] if c == 0 else HP1[:, b, :]

        def index(b):
            i, plus, mul = b
            return i * mul + plus

        def step_pairs(eng, body, peel=False):
            if peel:
                for s in range(2):
                    body((0, s, 2), s, True)
            with eng.Fori(int(peel), B // 2 - 1) as i:
                for s in range(2):
                    body((i, s, 2), s, True)
            for s in range(2):
                body((B - 2 + s, 0, 1), s, False)

        def ahead(b, n):
            i, plus, mul = b
            return (i, plus + n, mul)

        with nc.Block() as block:
            @block.sync
            def _(sp):
                def load(b, s):
                    sp.dma_start(flat(X2[s][:, :, :]), x1_dram[index(b)]).then_inc(x2_in[s], 16)
                with sp.Fori(0, B // 2 - 1) as i:
                    for s in range(2):
                        y_lo.reach(sp, (i, s, 2), 1)
                        load((i, s + 2, 2), s)

            @block.scalar
            def _(act):
                def body(b, s, more):
                    zz_ok.reach(act, b, 1)
                    nc.scalar.activation(Ah[:, :], ZZ[:, :], ACT.Copy).then_inc(a_hi.sem, 1)
                    if more:
                        y_high(act, ahead(b, 2), s, b[0] + 1, X2[s], Yh[s])
                    for c in range(NHC):
                        w1_ok.reach(act, b, c + 1)
                        settle(act)
                        nc.scalar.activation(hidden(c, index(b)), bank2(2 + 2 * c), ACT.Identity, bias=col(C_C1 + c)).then_inc(hid_ok.sem, 1)

                step_pairs(act, body)

            @block.vector
            def _(dve):
                def body(b, s, more):
                    agg_ok.reach(dve, b, 1)
                    nc.vector.tensor_tensor(ZZ[:, :], bank2(AGG[s]), dinv_row[:, :], ALU.mult).then_inc(zz_ok.sem, 1)
                    a_hi.reach(dve, b, 1)
                    nc.vector.tensor_tensor(Al[:, :], ZZ[:, :], Ah[:, :].bitcast(F32), ALU.subtract).then_inc(a_lo.sem, 1)
                    if more:
                        y_low(dve, ahead(b, 2), s, X2[s], Yh[s], Yl[s])
                    for c in range(NHC):
                        hid_ok.reach(dve, b, c + 1)
                        settle(dve)
                        for h in range(2):
                            nc.vector.bn_stats(S1[:, c, index(b) * 2 + h, :], hidden(c, index(b))[:, h * HALF:(h + 1) * HALF]).then_inc(hid_read, 1)

                step_pairs(dve, body)
                dve.wait_ge(hid_read, 2 * NHC * B)

            @block.tensor
            def _(pe):
                def agg(b, s, h):
                    if h == 0:
                        y_lo.reach(pe, b, 1)
                    mm = adj_half(AGG[s], Yh[s], Yl[s], h)
                    if h == 1:
                        mm.then_inc(agg_ok.sem, 1)

                def body(b, s, more):
                    following = (more or s == 0) and later((b[0], b[1]), 0)
                    if following:
                        agg(ahead(b, 1), 1 - s, 0)
                    a_lo.reach(pe, b, 1)
                    for c in range(NHC):
                        for h in range(2):
                            hs = slice(h * HALF, (h + 1) * HALF)
                            mm = passes(PS[:, 2 + 2 * c + h, :], W1Th[:, c, :], W1Tl[:, c, :], Ah[:, hs], Al[:, hs], True, True)
                        mm.then_inc(w1_ok.sem, 1)
                    if following:
                        agg(ahead(b, 1), 1 - s, 1)

                step_pairs(pe, body, peel=True)

            @block.gpsimd
            def _(pool):
                for n in range(NT):
                    nc.gpsimd.tensor_scalar(PENT[:, n, :], ATh[:, n, :].bitcast(F32), 0.0, BLOCKED, ALU.is_equal, ALU.mult).then_inc(pent_ok, 1)
                pool.wait_ge(pent_ok, NT)
        l2a.close()

        bn_dve, bn_pool = sem("bn_dve"), sem("bn_pool")

        def batch_norm_params(block, groups, base_dve, base_pool):
            @block.vector
            def _(dve):
                n = [base_dve]

                def done(ins):
                    n[0] += 1
                    ins.then_inc(bn_dve, 1)
                    dve.wait_ge(bn_dve, n[0])
                for r, stats, _, _ in groups:
                    done(nc.vector.bn_aggr(bnp[:, r, 0:2], stats))
                    done(nc.vector.tensor_scalar(bnp[:, r, 5:6], bnp[:, r, 1:2], BN_EPS, None, ALU.add))
                dve.wait_ge(bn_pool, base_pool + len(groups))
                for r, _, g, be in groups:
                    done(nc.vector.tensor_tensor(bnp[:, r, 3:4], bnp[:, r, 2:3], col(g), ALU.mult))
                    done(nc.vector.tensor_tensor(bnp[:, r, 4:5], bnp[:, r, 0:1], bnp[:, r, 3:4], ALU.mult))
                    done(nc.vector.tensor_tensor(bnp[:, r, 4:5], col(be), bnp[:, r, 4:5], ALU.subtract))

            @block.gpsimd
            def _(pool):
                for k, (r, _, _, _) in enumerate(groups):
                    pool.wait_ge(bn_dve, base_dve + 2 * k + 2)
                    nc.gpsimd.tensor_tensor(bnp[:, r, 2:3], bnp[:, r, 5:6], neg_half[:, 0:1], ALU.pow).then_inc(bn_pool, 1)

        with nc.Block() as block:
            batch_norm_params(block, [(0, flat(S1[:, 0]), C_G1, C_BE1), (1, flat(S1[:, 1]), C_G1 + 1, C_BE1 + 1)], 0, 0)

        PENN = sbr(late, "PENN", [P, NT, T], BF16)
        l2b = ExitStack()
        Rh, Rl = ([flat(first[:, :, :]).rearrange("p (c n) -> p c n", c=NHC), sb(l2b, n, [P, NHC, HALF], F32R)]
                  for n, first in (("Rh", N0h), ("Rl", N0l)))
        NAT2 = [flat(XL[:, :, :]), B0]
        nat_in = [sem(f"nat_in{s}") for s in range(2)]
        penn_ok = sem("penn_ok")
        relu_ok = Signal("relu_ok", 2 * NHC)
        rh0, rh1 = Signal("relu_high0", 2), Signal("relu_high1", 2)
        rl = Signal("relu_low", 2 * NHC)
        w2_ok, y3_ok = Signal("w2_ok", 2), Signal("w2_read", 2)
        s2_ok = sem("stats2_ok")
        halves = [slice(s * HALF, (s + 1) * HALF) for s in range(2)]
        with nc.Block() as block:
            @block.sync
            def _(sp):
                for n in range(NT):
                    if n >= 2:
                        sp.wait_ge(penn_ok, n - 1)
                    sp.dma_start(NAT2[n % 2][:, :], adj[n * P:(n + 1) * P, :]).then_inc(nat_in[n % 2], 16)

            @block.gpsimd
            def _(pool):
                for n in range(NT):
                    pool.wait_ge(nat_in[n % 2], 16 * (n // 2 + 1))
                    nc.gpsimd.tensor_scalar(PENN[:, n, :], NAT2[n % 2][:, :], 0.0, BLOCKED, ALU.is_equal, ALU.mult).then_inc(penn_ok, 1)
                pool.wait_ge(penn_ok, NT)

            @block.scalar
            def _(act):
                def relus(b, halves_of=range(2)):
                    for s in halves_of:
                        for c in range(NHC):
                            v = hidden(c, index(b))[:, halves[s]]
                            nc.scalar.activation(v, v, ACT.Relu, bias=bnp[:, c, 4:5], scale=bnp[:, c, 3:4]).then_inc(relu_ok.sem, 1)
                        if later(b[:2], 0):
                            w2_ok.reach(act, ahead(b, -1), s + 1)
                        relu_ok.reach(act, b, NHC * (s + 1))
                        settle(act)
                        nc.scalar.activation(Rh[s][:, 1, :], hidden(1, index(b))[:, halves[s]], ACT.Copy).then_inc(rh1.sem, 1)

                def results(b, halves_of=range(2)):
                    for s in halves_of:
                        w2_ok.reach(act, b, s + 1)
                        settle(act)
                        nc.scalar.activation(hidden(0, index(b))[:, halves[s]], PS[:, s, :], ACT.Identity, bias=col(C_C2)).then_inc(y3_ok.sem, 1)

                relus((0, 0, 1))
                with act.Fori(1, B) as i:
                    for s in range(2):
                        relus((i, 0, 1), [s])
                        results((i, -1, 1), [s])
                results((B - 1, 0, 1))

            @block.vector
            def _(dve):
                def splits(b, halves_of=range(2)):
                    for s in halves_of:
                        relu_ok.reach(dve, b, NHC * s + 1)
                        if later(b[:2], 0):
                            w2_ok.reach(dve, ahead(b, -1), s + 1)
                        settle(dve)
                        v = [hidden(c, index(b))[:, halves[s]] for c in range(NHC)]
                        nc.vector.tensor_copy(Rh[s][:, 0, :], v[0]).then_inc(rh0.sem, 1)
                        rh0.reach(dve, b, s + 1)
                        nc.vector.tensor_tensor(Rl[s][:, 0, :], v[0], Rh[s][:, 0, :].bitcast(F32), ALU.subtract).then_inc(rl.sem, 1)
                        rh1.reach(dve, b, s + 1)
                        nc.vector.tensor_tensor(Rl[s][:, 1, :], v[1], Rh[s][:, 1, :].bitcast(F32), ALU.subtract).then_inc(rl.sem, 1)

                def stats(b, halves_of=range(2)):
                    for s in halves_of:
                        y3_ok.reach(dve, b, s + 1)
                        settle(dve)
                        nc.vector.bn_stats(S2[:, index(b) * 2 + s, :], hidden(0, index(b))[:, halves[s]]).then_inc(s2_ok, 1)

                splits((0, 0, 1))
                with dve.Fori(1, B) as i:
                    for s in range(2):
                        splits((i, 0, 1), [s])
                        stats((i, -1, 1), [s])
                stats((B - 1, 0, 1))
                dve.wait_ge(s2_ok, 2 * B)

            @block.tensor
            def _(pe):
                def products(b):
                    for s in range(2):
                        if later(b[:2], 0):
                            y3_ok.reach(pe, ahead(b, -1), s + 1)
                        for c in range(NHC):
                            rl.reach(pe, b, NHC * s + c + 1)
                            mm = passes(PS[:, s, :], W2Th[:, c, :], W2Tl[:, c, :], Rh[s][:, c, :], Rl[s][:, c, :], c == 0, c == NHC - 1)
                        mm.then_inc(w2_ok.sem, 1)

                products((0, 0, 1))
                with pe.Fori(1, B) as i:
                    products((i, 0, 1))
        l2b.close()
        with nc.Block() as block:
            batch_norm_params(block, [(2, flat(S2[:, :, :]), C_G2, C_BE2)], 10, 2)
        l2.close()
        s0.close()
        graph.close()

        l3 = ExitStack()
        x3_dram = nc.dram_tensor("x3_dram", (B, P, NT * D), F32, kind="Internal").ap()
        rows_dram = nc.dram_tensor("rows_dram", (B, 2 * NT, P), F32, kind="Internal").ap()
        S2C = sb(l3, "S2C", [P, B, 2, NT])
        RB = sb(l3, "RB", [P, B, 2 * T])
        Z3 = sb(l3, "Z3", [P, T])
        X3 = sb(l3, "X3", [P, NT, D])
        F3h, F3l = (sb(l3, n, [P, T], F32R) for n in ("F3h", "F3l"))
        junk3 = sb(l3, "junk3", [P, T])
        MX = sb(l3, "MX", [P, NT])
        RR = sb(l3, "RR", [P, 2 * NT])
        RRT = sb(l3, "RRT", [2 * NT, P])
        NTT, NV = 2, 4
        TT = [sb(l3, f"tt{k}", [P, T]) for k in range(NTT)]
        V = [sb(l3, f"v{k}", [P, T]) for k in range(NV)]
        ATT = sb(l3, "ATT", [P, NT, D + 1])
        REC = sb(l3, "REC", [P, NT])
        XR = sb(l3, "XR", [P, NT, D])
        x3_in, x3_out = Signal("x3_in", 1, 16), Signal("x3_out", 1, 16)
        xr_in = Signal("xr_in", 1, 16)
        rows_out, rb_in = Signal("rows_out", 1, 16), Signal("rb_in", 1, 16)
        out_ok = Signal("out_ok", 1, 16)
        z_ok, zt_ok = Signal("z_ok", 1), Signal("zt_ok", 1)
        y_ok = Signal("y3", 1)
        x3_ok, x3t_ok = Signal("x3_ok", 2), Signal("x3t_ok", 1)
        f_hi, f_lo = Signal("f3_hi", 1), Signal("f3_lo", 1)
        wh_pe, s2_pe = Signal("wh_pe", 1), Signal("s2_pe", 1)
        wh_ok = Signal("wh_ok", 2)
        mx = Signal("mx", NT)
        small = Signal("rows_dve", 6)
        rr_pe, rrt_ok = Signal("rr_pe", 1), Signal("rrt_ok", 1)
        ones2_ok, ones_ok = sem("ones2_ok"), Signal("ones_ok", 1)
        tt_ok = Signal("tt_ok", NT)
        v_ok = Signal("v_ok", NT, credit=NTT)
        m_ok = Signal("m_ok", NT)
        e_ok = Signal("e_ok", NT)
        att_pe = Signal("att_pe", NT, credit=NV)
        att_ok = Signal("att_ok", 2, credit=2)
        rec_ok, sum_ok = Signal("rec_ok", 1), Signal("sum_ok", 1)
        res_ok = Signal("res_ok", 2)
        front_norm, back_norm = Norm("front", 1, 0), Norm("back", 1, 1)

        ones2 = sb(l3, "ones2", [P, NT, 1])

        PARTS = ((0, 2, 3), (2, 3, 2))

        def att(t):
            return PS[:, t // 3, (t % 3) * (D + 1):(t % 3 + 1) * (D + 1)]

        def tiles_of(b):
            return HW[:, index(b), :].rearrange("p (t d) -> p t d", t=NT)

        def wh(b, jt):
            return HW[:, index(b), jt * (D + 2):jt * (D + 2) + D + 1]

        def turns(eng, step, n=NT, last=B - 2):
            def turn(i, stages="cmfko"):
                for q in range(n):
                    step(q, *((i, plus, 1) if name in stages else None
                              for name, plus in (("c", 0), ("m", 1), ("f", 2), ("k", -1), ("o", -2))))
            for i, stages in ((-2, "f"), (-1, "mf"), (0, "cmf"), (1, "cmfk")):
                turn(i, stages)
            with eng.Fori(2, last) as i:
                turn(i)
            for i in range(last, B - 2):
                turn(i)
            for i, stages in ((B - 2, "cmko"), (B - 1, "cko"), (B, "ko"), (B + 1, "o")):
                turn(i, stages)

        with nc.Block() as block:
            @block.sync
            def _(sp):
                def step(q, c, m, f, k, o):
                    if o:
                        res_ok.reach(sp, o, 2)
                        sp.dma_start(out[index(o)].rearrange("(t p) d -> p t d", p=P), XR[:, :, :]).then_inc(out_ok.sem, 16)
                        out_ok.reach(sp, o, 1)
                        settle(sp)
                    if k:
                        sp.dma_start(flat(XR[:, :, :]), x3_dram[index(k)]).then_inc(xr_in.sem, 16)
                    if f:
                        x3_ok.reach(sp, f, 2)
                        sp.dma_start(x3_dram[index(f)], flat(X3[:, :, :])).then_inc(x3_out.sem, 16)
                    if m:
                        rrt_ok.reach(sp, m, 1)
                        sp.dma_start(rows_dram[index(m)], RRT[:, :]).then_inc(rows_out.sem, 16)
                        rows_out.reach(sp, m, 1)
                        settle(sp)
                        sp.dma_start(RB[:, index(m), :], rows_dram[index(m)].rearrange("(o t) p -> o (t p)", o=1).broadcast_to([P, 2 * T])).then_inc(rb_in.sem, 16)
                    if f and not (isinstance(f[0], int) and f[0] + f[1] == B - 1):
                        x3_out.reach(sp, f, 1)
                        settle(sp)
                        x3t_ok.reach(sp, f, 1)
                        sp.dma_start(flat(X3[:, :, :]), x1_dram[index(ahead(f, 1))]).then_inc(x3_in.sem, 16)

                sp.dma_start(flat(X3[:, :, :]), x1_dram[0]).then_inc(x3_in.sem, 16)
                turns(sp, step, n=1, last=B - 3)

            @block.scalar
            def _(act):
                nc.scalar.preload_act_table(ACT.Exp)

                def exps(b, j):
                    m_ok.reach(act, b, j + 1)
                    nc.scalar.activation(V[j % NV][:, :], V[j % NV][:, :], ACT.Exp).then_inc(e_ok.sem, 1)

                def step(q, c, m, f, k, o):
                    if f and q == 0:
                        settle(act)
                        nc.scalar.activation(Z3[:, :], HW[:, index(f), 0:T], ACT.Identity, bias=bnp[:, 2, 4:5], scale=bnp[:, 2, 3:4]).then_inc(z_ok.sem, 1)
                    if k and q == 3:
                        att_pe.reach(act, k, NT)
                        for b0, b1, n in PARTS:
                            t0, t1 = 3 * b0, 3 * b0 + n * (b1 - b0)
                            nc.scalar.activation(flat(ATT[:, t0:t1, :]).rearrange("p (b n) -> p b n", b=b1 - b0),
                                                 PS[:, b0:b1, 0:n * (D + 1)], ACT.Copy).then_inc(att_ok.sem, 1)
                    if c:
                        if q == 0:
                            rb_in.reach(act, c, 1)
                        v_ok.reach(act, c, q - NTT + 1)
                        settle(act)
                        nc.scalar.activation(TT[q % NTT][:, :], RB[:, index(c), T:2 * T], ACT.Identity,
                                             bias=S2C[:, index(c), 1, q:q + 1]).then_inc(tt_ok.sem, 1)
                    if q < 2 and k:
                        exps(k, NT - 2 + q)
                    if q >= 2 and c:
                        exps(c, q - 2)
                    if o and q in (1, 2):
                        back_norm.act_scale(act, o, 1, XR, XR, res_ok.sem, q - 1)
                    if f and q in (3, 4):
                        front_norm.act_scale(act, f, 1, X3, X3, x3_ok.sem, q - 3)
                    if m and q == 6:
                        rr_pe.reach(act, m, 1)
                        nc.scalar.activation(RRT[:, :], PS[0:2 * NT, 3, 0:P], ACT.Copy).then_inc(rrt_ok.sem, 1)
                    if f and q == 5:
                        x3t_ok.reach(act, f, 1)
                        nc.scalar.activation(F3h[:, :], bank2(5), ACT.Copy).then_inc(f_hi.sem, 1)
                    if f and q == 7:
                        wh_pe.reach(act, f, 1)
                        settle(act)
                        for b0, b1, n in PARTS:
                            t0, t1 = 3 * b0, 3 * b0 + n * (b1 - b0)
                            nc.scalar.activation(HW[:, index(f), t0 * (D + 2):t1 * (D + 2)].rearrange("p (b n) -> p b n", b=b1 - b0),
                                                 PS[:, 5 + b0:5 + b1, 0:n * (D + 2)], ACT.Copy).then_inc(wh_ok.sem, 1)

                act.sem_inc(att_ok.sem, att_ok.credit)
                turns(act, step)

            @block.gpsimd
            def _(pool):
                def step(q, c, m, f, k, o):
                    if f and q == 2:
                        front_norm.pool(pool, f, 1, shifts=True)
                    if c:
                        v_ok.reach(pool, c, q + 1)
                        nc.gpsimd.tensor_tensor(V[q % NV][:, :], V[q % NV][:, :], PENT[:, q, :], ALU.add).then_inc(m_ok.sem, 1)
                    if m and q == 6:
                        small.reach(pool, m, 6)
                        settle(pool)
                        nc.gpsimd.tensor_copy(tiles_of(m)[:, :, D:D + 1], ones2[:, :, :]).then_inc(ones_ok.sem, 1)
                    if k and q == 7:
                        back_norm.pool(pool, k, 1, shifts=True)
                nc.gpsimd.memset(ones2[:, :, :], 1.0).then_inc(ones2_ok, 1)
                pool.wait_ge(ones2_ok, 1)
                turns(pool, step)

            @block.vector
            def _(dve):
                MAXIMA = (0, 2, 3, 5, 7, 8, 8, 8, 8)

                def step(q, c, m, f, k, o):
                    if c:
                        att_pe.reach(dve, c, q - NV + 1)
                        tt_ok.reach(dve, c, q + 1)
                        nc.vector.scalar_tensor_tensor(out=V[q % NV][:, :], in0=RB[:, index(c), 0:T], scalar=S2C[:, index(c), 0, q:q + 1],
                                                       in1=TT[q % NTT][:, :], op0=ALU.add, op1=ALU.max).then_inc(v_ok.sem, 1)
                    if f and q == 6:
                        f_hi.reach(dve, f, 1)
                        nc.vector.tensor_tensor(F3l[:, :], bank2(5), F3h[:, :].bitcast(F32), ALU.subtract).then_inc(f_lo.sem, 1)
                    if m:
                        if q == 0:
                            s2_pe.reach(dve, m, 1)
                        for t in range(MAXIMA[q], MAXIMA[q + 1]):
                            settle(dve)
                            nc.vector.tensor_tensor_reduce(junk3[:, :], PENN[:, t, :], bank2(3), 1.0, 2 * BLOCKED,
                                                           ALU.add, ALU.max, MX[:, t:t + 1]).then_inc(mx.sem, 1)
                            mx.reach(dve, m, t + 1)
                        if q == 5:
                            wh_ok.reach(dve, m, 2)
                            settle(dve)
                            s1, s2 = tiles_of(m)[:, :, D], tiles_of(m)[:, :, D + 1]
                            nc.vector.tensor_tensor(MX[:, :], MX[:, :], s1, ALU.add).then_inc(small.sem, 1)
                            nc.vector.tensor_copy(S2C[:, index(m), 0, :], s2).then_inc(small.sem, 1)
                            small.reach(dve, m, 2)
                            nc.vector.scalar_tensor_tensor(out=MX[:, :], in0=MX[:, :], scalar=ALPHA, in1=MX[:, :],
                                                           op0=ALU.mult, op1=ALU.max).then_inc(small.sem, 1)
                            nc.vector.tensor_scalar(S2C[:, index(m), 1, :], s2, ALPHA, None, ALU.mult).then_inc(small.sem, 1)
                            small.reach(dve, m, 4)
                            nc.vector.tensor_tensor(RR[:, 0:NT], s1, MX[:, :], ALU.subtract).then_inc(small.sem, 1)
                            nc.vector.scalar_tensor_tensor(out=RR[:, NT:2 * NT], in0=s1, scalar=ALPHA, in1=MX[:, :],
                                                           op0=ALU.mult, op1=ALU.subtract).then_inc(small.sem, 1)
                            small.reach(dve, m, 6)
                    if f and q == 0:
                        x3_in.reach(dve, f, 1)
                        zt_ok.reach(dve, f, 1)
                        nc.vector.tensor_tensor(flat(X3[:, :, :]), flat(X3[:, :, :]), bank2(5), ALU.add).then_inc(y_ok.sem, 1)
                    if f and q == 1:
                        y_ok.reach(dve, f, 1)
                        front_norm.dve_stats(dve, f, 1, X3)
                    if k and q == 6:
                        att_ok.reach(dve, k, 2)
                        settle(dve)
                        nc.vector.reciprocal(REC[:, :], ATT[:, :, D]).then_inc(rec_ok.sem, 1)
                        xr_in.reach(dve, k, 1)
                        rec_ok.reach(dve, k, 1)
                        for t in range(NT):
                            ins = nc.vector.scalar_tensor_tensor(out=XR[:, t, :], in0=ATT[:, t, 0:D], scalar=REC[:, t:t + 1], in1=XR[:, t, :],
                                                                 op0=ALU.mult, op1=ALU.add)
                        ins.then_inc(sum_ok.sem, 1)
                    if k and q == 7:
                        sum_ok.reach(dve, k, 1)
                        back_norm.dve_stats(dve, k, 1, XR)
                dve.sem_inc(v_ok.sem, v_ok.credit)
                turns(dve, step)

            @block.tensor
            def _(pe):
                def sums(b, j):
                    e_ok.reach(pe, b, j + 1)
                    if j == 0:
                        ones_ok.reach(pe, b, 1)
                        att_ok.reach(pe, ahead(b, -1), 2)
                    for t in range(NT):
                        mm = nc.tensor.matmul(att(t), V[j % NV][:, t * P:(t + 1) * P], wh(b, j),
                                              start=(j == 0 and t % 3 == 0), stop=(j == NT - 1), skip_group_check=True)
                    mm.then_inc(att_pe.sem, 1)

                def step(q, c, m, f, k, o):
                    if f and q == 7:
                        f_lo.reach(pe, f, 1)
                        for t in range(NT):
                            ts = slice(t * P, (t + 1) * P)
                            mm = passes(PS[:, 5 + t // 3, (t % 3) * (D + 2):(t % 3 + 1) * (D + 2)], F3h[:, ts], F3l[:, ts], W3h[:, :], W3l[:, :], True, True)
                        mm.then_inc(wh_pe.sem, 1)
                    if q < 3 and k:
                        sums(k, NT - 3 + q)
                    if q >= 3 and c:
                        sums(c, q - 3)
                    if f and q == 0:
                        z_ok.reach(pe, f, 1)
                        if later(f, 0):
                            wh_ok.reach(pe, ahead(f, -1), 2)
                        transposes(5, [Z3[:, t * P:(t + 1) * P] for t in range(NT)]).then_inc(zt_ok.sem, 1)
                    if f and q == 4:
                        x3_ok.reach(pe, f, 2)
                        transposes(5, [X3[:, t, :] for t in range(NT)]).then_inc(x3t_ok.sem, 1)
                    if m and q == 5:
                        small.reach(pe, m, 6)
                        nc.tensor.transpose(PS[0:2 * NT, 3, 0:P], RR[:, :], ident[:, :]).then_inc(rr_pe.sem, 1)
                    if f and q == 7:
                        f_lo.reach(pe, f, 1)
                        if m:
                            rrt_ok.reach(pe, m, 1)
                        for h in range(2):
                            hs = slice(h * HALF, (h + 1) * HALF)
                            mm = passes(PS[:, 3 + h, :], A2h[:, 1, :], A2l[:, 1, :], F3h[:, hs], F3l[:, hs], True, True)
                        mm.then_inc(s2_pe.sem, 1)

                pe.sem_inc(att_pe.sem, att_pe.credit)
                turns(pe, step)
        l3.close()
        late.close()


_INS = ["x", "adj", "L0_gnn_Wg0", "L0_gnn_bg0", "L0_gnn_Wg1", "L0_gnn_bg1", "L0_gnn_Wih", "L0_gnn_Whh", "L0_gnn_bih",
        "L0_gnn_bhh", "L1_gnn_w1_loop", "L1_gnn_w1_neigh", "L1_gnn_b1", "L1_gnn_w2_loop", "L1_gnn_w2_neigh",
        "L1_gnn_b2", "L2_gnn_W1", "L2_gnn_b1", "L2_gnn_g1", "L2_gnn_be1", "L2_gnn_W2", "L2_gnn_b2", "L2_gnn_g2",
        "L2_gnn_be2", "L3_gnn_W", "L3_gnn_a"]


def kernel(**inputs):
    import numpy as _np
    import concourse.bacc as _bacc
    from concourse import mybir as _mybir
    from concourse.bass_utils import run_bass_kernel_spmd as _run

    nc = _bacc.Bacc("TRN2", target_bir_lowering=False, num_devices=1)
    arrays, args = {}, []
    for name in _INS:
        a = _np.ascontiguousarray(inputs[name])
        arrays[f"in_{name}_dram"] = a
        args.append(nc.dram_tensor(f"in_{name}_dram", a.shape, _mybir.dt.from_np(a.dtype), kind="ExternalInput").ap())
    args.append(nc.dram_tensor("out_0_dram", (B, T, D), F32, kind="ExternalOutput").ap())
    program(nc, *args)
    r = _run(nc, [arrays], core_ids=[0])
    return r.results[0]["out_0_dram"]
```
